# Optimizing a Trainium2 kernel written in Bass

```python
import numpy as np
import jax
import jax.numpy as jnp

def _softmax(x, axis=-1):
    return jax.nn.softmax(x, axis=axis)

def _gelu(x):
    return jax.nn.gelu(x, approximate=True)

def _silu(x):
    return jax.nn.silu(x)

def _sigmoid(x):
    return jax.nn.sigmoid(x)

def _layernorm(x, axis=-1, eps=1e-05):
    m = jnp.mean(x, axis=axis, keepdims=True)
    v = jnp.var(x, axis=axis, keepdims=True)
    return (x - m) / jnp.sqrt(v + eps)

def _scatter_add(tgt, idx, src, axis=0):
    return tgt.at[idx].add(src)

def _segment_sum(src, seg, n):
    return jax.ops.segment_sum(src, seg, n)
kernel_name = 'mk_adaln_d2_jaxref_r8_c20ac3'

def setup_inputs(seed: int=0):
    np.random.seed(seed)
    _w = jnp.asarray

    def _L0_attn_setup():
        import jax, jax.numpy as jnp
        import numpy as np
        H, DK, DV, M = (8, 64, 64, 8)

        def _l2norm(x, eps=1e-06):
            return x * jax.lax.rsqrt(jnp.sum(x * x, axis=-1, keepdims=True) + eps)

        def _rotary(x, cos, sin):
            d = x.shape[-1] // 2
            x1, x2 = (x[..., :d], x[..., d:])
            c = cos[:, None]
            s = sin[:, None]
            return jnp.concatenate([x1 * c + x2 * s, -x1 * s + x2 * c], axis=-1)
        key = jax.random.key(seed)
        ks = jax.random.split(key, 11)
        B, T, D = (2, 256, 128)
        w = lambda k, shape, s=0.02: jax.random.normal(k, shape, jnp.float32) * s
        return {'hidden_states': jax.random.normal(ks[0], (B, T, D), jnp.float32), 'Wq': w(ks[1], (D, H * DK)), 'Wk': w(ks[2], (D, H * DK)), 'Wv': w(ks[3], (D, H * DV)), 'Wbeta': w(ks[4], (D, H * M)), 'Wtg': w(ks[5], (D, H * M)), 'mode_logits': w(ks[6], (H, M), 0.1), 'log_decay': w(ks[7], (H, M), 0.1), 'omega_log_scale': w(ks[8], (H, M), 0.1), 'Wg': w(ks[9], (D, H * DV)), 'Wo': w(ks[10], (H * DV, D))}
    _L0_attn_in = _L0_attn_setup()

    def _L0_ffn_setup():
        import jax, jax.numpy as jnp
        import numpy as np
        from jax import lax
        HIDDEN = 128
        INTER = 64
        E = 64
        K = 6
        G = 8
        TG = 4
        NSH = 2
        ISH = INTER * NSH

        def _moe_forward(hidden_states, gate_w, gate_bias, eg_w, eu_w, ed_w, sg_w, su_w, sd_w):
            B, S, H = hidden_states.shape
            x = hidden_states.reshape(-1, H)
            T = x.shape[0]
            shared = jax.nn.silu(x @ sg_w.T) * (x @ su_w.T) @ sd_w.T
            logits = x @ gate_w.T
            scores = jax.nn.sigmoid(logits) + gate_bias
            group_scores = scores.reshape(T, G, E // G).max(axis=-1)
            _, sel_groups = lax.top_k(group_scores, TG)
            group_mask = jnp.zeros((T, G), scores.dtype).at[jnp.arange(T)[:, None], sel_groups].set(1.0)
            mask = jnp.repeat(group_mask, E // G, axis=1)
            masked_scores = scores * mask
            topk_w, topk_i = lax.top_k(masked_scores, K)
            topk_w = topk_w / (topk_w.sum(axis=-1, keepdims=True) + 1e-08)
            comb = jnp.zeros((T, E), x.dtype).at[jnp.arange(T)[:, None], topk_i].add(topk_w)
            h = jax.nn.silu(jnp.einsum('th,eih->eti', x, eg_w)) * jnp.einsum('th,eih->eti', x, eu_w)
            routed = jnp.einsum('eti,ehi,te->th', h, ed_w, comb)
            return (shared + routed).reshape(B, S, H)
        key = jax.random.key(seed)
        ks = jax.random.split(key, 9)
        s = 0.02
        return {'hidden_states': jax.random.normal(ks[0], (1, 128, HIDDEN), jnp.float32), 'gate_w': jax.random.normal(ks[1], (E, HIDDEN), jnp.float32) * s, 'gate_bias': jnp.zeros((E,), jnp.float32), 'eg_w': jax.random.normal(ks[2], (E, INTER, HIDDEN), jnp.float32) * s, 'eu_w': jax.random.normal(ks[3], (E, INTER, HIDDEN), jnp.float32) * s, 'ed_w': jax.random.normal(ks[4], (E, HIDDEN, INTER), jnp.float32) * s, 'sg_w': jax.random.normal(ks[5], (ISH, HIDDEN), jnp.float32) * s, 'su_w': jax.random.normal(ks[6], (ISH, HIDDEN), jnp.float32) * s, 'sd_w': jax.random.normal(ks[7], (HIDDEN, ISH), jnp.float32) * s}
    _L0_ffn_in = _L0_ffn_setup()
    _L0_c = _w((lambda *s: np.random.randn(*s).astype(np.float32) * 0.05)(8, 128))
    _L0_wmod = _w((lambda *s: np.random.randn(*s).astype(np.float32) * 0.05)(128, 6 * 128) * 128 ** (-0.5))

    def _L1_attn_setup():
        import jax, jax.numpy as jnp
        import numpy as np
        NUM_HEADS = 16
        D_MODEL = 128
        HEAD_DIM = D_MODEL // NUM_HEADS
        EPS = 1e-06

        def _feature_map(x):
            return jax.nn.elu(x) + 1.0
        key = jax.random.key(seed)
        ks = jax.random.split(key, 9)
        B, S, D = (4, 1024, D_MODEL)
        scale = 1.0 / np.sqrt(D)
        inputs_q = jax.random.normal(ks[0], (B, S, D), dtype=jnp.float32)
        Wq = jax.random.normal(ks[1], (D, D), dtype=jnp.float32) * scale
        Wk = jax.random.normal(ks[2], (D, D), dtype=jnp.float32) * scale
        Wv = jax.random.normal(ks[3], (D, D), dtype=jnp.float32) * scale
        Wo = jax.random.normal(ks[4], (D, D), dtype=jnp.float32) * scale
        bq = jnp.zeros((D,), jnp.float32)
        bk = jnp.zeros((D,), jnp.float32)
        bv = jnp.zeros((D,), jnp.float32)
        bo = jnp.zeros((D,), jnp.float32)
        return {'inputs_q': inputs_q, 'Wq': Wq, 'bq': bq, 'Wk': Wk, 'bk': bk, 'Wv': Wv, 'bv': bv, 'Wo': Wo, 'bo': bo}
    _L1_attn_in = _L1_attn_setup()

    def _L1_ffn_setup():
        import jax, jax.numpy as jnp
        import numpy as np
        import math
        B, L, D = (4, 512, 128)
        F = 512
        E = 16
        CAP_FACTOR = 1.0
        EPS = 1e-05
        key = jax.random.key(seed)
        ks = jax.random.split(key, 8)
        std = 0.02
        return {'x': jax.random.normal(ks[0], (B, L, D), dtype=jnp.float32), 'norm_weight': jnp.ones((D,), dtype=jnp.float32), 'router_weight': jax.random.normal(ks[1], (E, D), dtype=jnp.float32) * std, 'router_bias': jnp.zeros((E,), dtype=jnp.float32), 'fc1_weight': jax.random.normal(ks[2], (E, F, D), dtype=jnp.float32) * std, 'fc1_bias': jnp.zeros((E, F), dtype=jnp.float32), 'fc2_weight': jax.random.normal(ks[3], (E, D, F), dtype=jnp.float32) * std, 'fc2_bias': jnp.zeros((E, D), dtype=jnp.float32)}
    _L1_ffn_in = _L1_ffn_setup()
    _L1_c = _w((lambda *s: np.random.randn(*s).astype(np.float32) * 0.05)(8, 128))
    _L1_wmod = _w((lambda *s: np.random.randn(*s).astype(np.float32) * 0.05)(128, 6 * 128) * 128 ** (-0.5))
    _d = {'L0_attn_hidden_states': _L0_attn_in['hidden_states'], 'L0_attn_Wq': _L0_attn_in['Wq'], 'L0_attn_Wk': _L0_attn_in['Wk'], 'L0_attn_Wv': _L0_attn_in['Wv'], 'L0_attn_Wbeta': _L0_attn_in['Wbeta'], 'L0_attn_Wtg': _L0_attn_in['Wtg'], 'L0_attn_mode_logits': _L0_attn_in['mode_logits'], 'L0_attn_log_decay': _L0_attn_in['log_decay'], 'L0_attn_omega_log_scale': _L0_attn_in['omega_log_scale'], 'L0_attn_Wg': _L0_attn_in['Wg'], 'L0_attn_Wo': _L0_attn_in['Wo'], 'L0_ffn_gate_w': _L0_ffn_in['gate_w'], 'L0_ffn_gate_bias': _L0_ffn_in['gate_bias'], 'L0_ffn_eg_w': _L0_ffn_in['eg_w'], 'L0_ffn_eu_w': _L0_ffn_in['eu_w'], 'L0_ffn_ed_w': _L0_ffn_in['ed_w'], 'L0_ffn_sg_w': _L0_ffn_in['sg_w'], 'L0_ffn_su_w': _L0_ffn_in['su_w'], 'L0_ffn_sd_w': _L0_ffn_in['sd_w'], 'L0_c': _L0_c, 'L0_wmod': _L0_wmod, 'L1_attn_Wq': _L1_attn_in['Wq'], 'L1_attn_bq': _L1_attn_in['bq'], 'L1_attn_Wk': _L1_attn_in['Wk'], 'L1_attn_bk': _L1_attn_in['bk'], 'L1_attn_Wv': _L1_attn_in['Wv'], 'L1_attn_bv': _L1_attn_in['bv'], 'L1_attn_Wo': _L1_attn_in['Wo'], 'L1_attn_bo': _L1_attn_in['bo'], 'L1_ffn_norm_weight': _L1_ffn_in['norm_weight'], 'L1_ffn_router_weight': _L1_ffn_in['router_weight'], 'L1_ffn_router_bias': _L1_ffn_in['router_bias'], 'L1_ffn_fc1_weight': _L1_ffn_in['fc1_weight'], 'L1_ffn_fc1_bias': _L1_ffn_in['fc1_bias'], 'L1_ffn_fc2_weight': _L1_ffn_in['fc2_weight'], 'L1_ffn_fc2_bias': _L1_ffn_in['fc2_bias'], 'L1_c': _L1_c, 'L1_wmod': _L1_wmod}
    _x0 = _d['L0_attn_hidden_states']
    _d['L0_attn_hidden_states'] = jax.random.normal(jax.random.fold_in(jax.random.key(seed), 1), (8, 256, 128), dtype=_x0.dtype)
    del _x0
    return _d

def reference(L0_attn_hidden_states, L0_attn_Wq, L0_attn_Wk, L0_attn_Wv, L0_attn_Wbeta, L0_attn_Wtg, L0_attn_mode_logits, L0_attn_log_decay, L0_attn_omega_log_scale, L0_attn_Wg, L0_attn_Wo, L0_ffn_gate_w, L0_ffn_gate_bias, L0_ffn_eg_w, L0_ffn_eu_w, L0_ffn_ed_w, L0_ffn_sg_w, L0_ffn_su_w, L0_ffn_sd_w, L0_c, L0_wmod, L1_attn_Wq, L1_attn_bq, L1_attn_Wk, L1_attn_bk, L1_attn_Wv, L1_attn_bv, L1_attn_Wo, L1_attn_bo, L1_ffn_norm_weight, L1_ffn_router_weight, L1_ffn_router_bias, L1_ffn_fc1_weight, L1_ffn_fc1_bias, L1_ffn_fc2_weight, L1_ffn_fc2_bias, L1_c, L1_wmod):

    def _L0_attn_ref(hidden_states, Wq, Wk, Wv, Wbeta, Wtg, mode_logits, log_decay, omega_log_scale, Wg, Wo):
        import jax, jax.numpy as jnp
        import numpy as np
        H, DK, DV, M = (8, 64, 64, 8)

        def _l2norm(x, eps=1e-06):
            return x * jax.lax.rsqrt(jnp.sum(x * x, axis=-1, keepdims=True) + eps)

        def _rotary(x, cos, sin):
            d = x.shape[-1] // 2
            x1, x2 = (x[..., :d], x[..., d:])
            c = cos[:, None]
            s = sin[:, None]
            return jnp.concatenate([x1 * c + x2 * s, -x1 * s + x2 * c], axis=-1)
        x = hidden_states
        B, T, D = x.shape
        q = (x @ Wq).reshape(B, T, H, DK)
        k = (x @ Wk).reshape(B, T, H, DK)
        v = (x @ Wv).reshape(B, T, H, DV)
        beta = jax.nn.sigmoid((x @ Wbeta).reshape(B, T, H, M))
        tg = jax.nn.sigmoid((x @ Wtg).reshape(B, T, H, M))
        pair = jnp.arange(0, DK, 2, dtype=jnp.float32)
        inv_freq = 1.0 / 10000.0 ** (pair / DK)
        omega_scale = jnp.exp(omega_log_scale)
        pos = jnp.arange(T, dtype=jnp.float32)
        angles = pos[:, None, None, None] * omega_scale[None, :, :, None] * inv_freq
        cos = jnp.transpose(jnp.cos(angles), (2, 0, 1, 3))
        sin = jnp.transpose(jnp.sin(angles), (2, 0, 1, 3))
        scale = DK ** (-0.5)
        qr = _l2norm(_rotary(q, cos, sin)) * scale
        kr = _l2norm(_rotary(k, cos, sin))
        rho = jnp.exp(-jax.nn.softplus(log_decay))
        g = jnp.log(jnp.clip(tg * rho, 1e-06))
        qt = jnp.transpose(qr, (2, 0, 1, 3, 4))
        kt = jnp.transpose(kr, (2, 0, 1, 3, 4))
        vt = jnp.transpose(v, (1, 0, 2, 3))
        gt = jnp.transpose(g, (1, 3, 0, 2))
        bt = jnp.transpose(beta, (1, 3, 0, 2))

        def step(S, inp):
            q_t, k_t, v_t, b_g, b_beta = inp
            S = S * jnp.exp(b_g)[..., None, None]
            kv = jnp.einsum('mbhk,mbhkv->mbhv', k_t, S)
            dv = (v_t[None] - kv) * b_beta[..., None]
            S = S + k_t[..., :, None] * dv[..., None, :]
            o_t = jnp.einsum('mbhk,mbhkv->mbhv', q_t, S)
            return (S, o_t)
        S0 = jnp.zeros((M, B, H, DK, DV), jnp.float32)
        _, ys = jax.lax.scan(step, S0, (qt, kt, vt, gt, bt))
        mode_w = jax.nn.softmax(mode_logits, axis=-1)
        o = jnp.einsum('tmbhv,hm->bthv', ys, mode_w)
        gate = jax.nn.sigmoid((x @ Wg).reshape(B, T, H, DV))
        o = o * gate
        return o.reshape(B, T, H * DV) @ Wo

    def _L0_ffn_ref(hidden_states, gate_w, gate_bias, eg_w, eu_w, ed_w, sg_w, su_w, sd_w):
        import jax, jax.numpy as jnp
        import numpy as np
        from jax import lax
        HIDDEN = 128
        INTER = 64
        E = 64
        K = 6
        G = 8
        TG = 4
        NSH = 2
        ISH = INTER * NSH

        def _moe_forward(hidden_states, gate_w, gate_bias, eg_w, eu_w, ed_w, sg_w, su_w, sd_w):
            B, S, H = hidden_states.shape
            x = hidden_states.reshape(-1, H)
            T = x.shape[0]
            shared = jax.nn.silu(x @ sg_w.T) * (x @ su_w.T) @ sd_w.T
            logits = x @ gate_w.T
            scores = jax.nn.sigmoid(logits) + gate_bias
            group_scores = scores.reshape(T, G, E // G).max(axis=-1)
            _, sel_groups = lax.top_k(group_scores, TG)
            group_mask = jnp.zeros((T, G), scores.dtype).at[jnp.arange(T)[:, None], sel_groups].set(1.0)
            mask = jnp.repeat(group_mask, E // G, axis=1)
            masked_scores = scores * mask
            topk_w, topk_i = lax.top_k(masked_scores, K)
            topk_w = topk_w / (topk_w.sum(axis=-1, keepdims=True) + 1e-08)
            comb = jnp.zeros((T, E), x.dtype).at[jnp.arange(T)[:, None], topk_i].add(topk_w)
            h = jax.nn.silu(jnp.einsum('th,eih->eti', x, eg_w)) * jnp.einsum('th,eih->eti', x, eu_w)
            routed = jnp.einsum('eti,ehi,te->th', h, ed_w, comb)
            return (shared + routed).reshape(B, S, H)
        return _moe_forward(hidden_states, gate_w, gate_bias, eg_w, eu_w, ed_w, sg_w, su_w, sd_w)

    def _L1_attn_ref(inputs_q, Wq, bq, Wk, bk, Wv, bv, Wo, bo):
        import jax, jax.numpy as jnp
        import numpy as np
        NUM_HEADS = 16
        D_MODEL = 128
        HEAD_DIM = D_MODEL // NUM_HEADS
        EPS = 1e-06

        def _feature_map(x):
            return jax.nn.elu(x) + 1.0
        B, S, D = inputs_q.shape
        H, Dh = (NUM_HEADS, HEAD_DIM)
        q = (inputs_q @ Wq + bq).reshape(B, S, H, Dh)
        k = (inputs_q @ Wk + bk).reshape(B, S, H, Dh)
        v = (inputs_q @ Wv + bv).reshape(B, S, H, Dh)
        q = _feature_map(q)
        k = _feature_map(k)
        kv = jnp.einsum('bkhd,bkhm->bhdm', k, v)
        out = jnp.einsum('bqhd,bhdm->bqhm', q, kv)
        normalizer = jnp.einsum('bqhd,bkhd->bqh', q, k)
        normalizer = jnp.maximum(normalizer, EPS)
        out = out / normalizer[..., None]
        out = out.reshape(B, S, D)
        return out @ Wo + bo

    def _L1_ffn_ref(x, norm_weight, router_weight, router_bias, fc1_weight, fc1_bias, fc2_weight, fc2_bias):
        import jax, jax.numpy as jnp
        import numpy as np
        import math
        B, L, D = (4, 512, 128)
        F = 512
        E = 16
        CAP_FACTOR = 1.0
        EPS = 1e-05
        b, l, d = x.shape
        n_tokens = b * l
        n_experts = router_weight.shape[0]
        capacity = max(1, math.ceil(CAP_FACTOR * n_tokens / n_experts))
        top_k = min(capacity, n_tokens)
        xf = x.reshape(n_tokens, d)
        rms = jnp.sqrt(jnp.mean(xf * xf, axis=-1, keepdims=True) + EPS)
        xn = xf / rms * norm_weight
        logits = xn @ router_weight.T + router_bias
        probs = jax.nn.softmax(logits, axis=-1)
        _, idx = jax.lax.top_k(logits.T, top_k)
        xe = xn[idx]
        h = jnp.einsum('ecd,efd->ecf', xe, fc1_weight) + fc1_bias[:, None, :]
        h = jax.nn.gelu(h, approximate=False)
        y = jnp.einsum('ecf,edf->ecd', h, fc2_weight) + fc2_bias[:, None, :]
        gates = jnp.take_along_axis(probs.T, idx, axis=1)
        flat_idx = idx.reshape(-1)
        contrib = (y * gates[:, :, None]).reshape(-1, d)
        output = jnp.zeros((n_tokens, d), dtype=x.dtype).at[flat_idx].add(contrib)
        gate_sums = jnp.zeros((n_tokens, 1), dtype=x.dtype).at[flat_idx].add(gates.reshape(-1, 1))
        assigned = gate_sums > 0
        output = jnp.where(assigned, output / jnp.where(assigned, gate_sums, 1.0), output)
        return output.reshape(b, l, d)
    x = L0_attn_hidden_states
    mod = (_silu(L0_c) @ L0_wmod).reshape(L0_c.shape[0], 6, 1, -1)
    sa, ca, ga, sb, cb, gb = (mod[:, 0], mod[:, 1], mod[:, 2], mod[:, 3], mod[:, 4], mod[:, 5])
    ga = (2 * (ga >= 0) - 1) * jnp.maximum(jnp.abs(ga), 0.25)
    gb = (2 * (gb >= 0) - 1) * jnp.maximum(jnp.abs(gb), 0.25)
    h = _layernorm(x, axis=-1) * (1 + ca) + sa
    x = x + ga * _L0_attn_ref(h, L0_attn_Wq, L0_attn_Wk, L0_attn_Wv, L0_attn_Wbeta, L0_attn_Wtg, L0_attn_mode_logits, L0_attn_log_decay, L0_attn_omega_log_scale, L0_attn_Wg, L0_attn_Wo)
    h = _layernorm(x, axis=-1) * (1 + cb) + sb
    x = x + gb * _L0_ffn_ref(h, L0_ffn_gate_w, L0_ffn_gate_bias, L0_ffn_eg_w, L0_ffn_eu_w, L0_ffn_ed_w, L0_ffn_sg_w, L0_ffn_su_w, L0_ffn_sd_w)
    mod = (_silu(L1_c) @ L1_wmod).reshape(L1_c.shape[0], 6, 1, -1)
    sa, ca, ga, sb, cb, gb = (mod[:, 0], mod[:, 1], mod[:, 2], mod[:, 3], mod[:, 4], mod[:, 5])
    ga = (2 * (ga >= 0) - 1) * jnp.maximum(jnp.abs(ga), 0.25)
    gb = (2 * (gb >= 0) - 1) * jnp.maximum(jnp.abs(gb), 0.25)
    h = _layernorm(x, axis=-1) * (1 + ca) + sa
    x = x + ga * _L1_attn_ref(h, L1_attn_Wq, L1_attn_bq, L1_attn_Wk, L1_attn_bk, L1_attn_Wv, L1_attn_bv, L1_attn_Wo, L1_attn_bo)
    h = _layernorm(x, axis=-1) * (1 + cb) + sb
    x = x + gb * _L1_ffn_ref(h, L1_ffn_norm_weight, L1_ffn_router_weight, L1_ffn_router_bias, L1_ffn_fc1_weight, L1_ffn_fc1_bias, L1_ffn_fc2_weight, L1_ffn_fc2_bias)
    return x

_drawn_inputs = setup_inputs


def setup_inputs(seed=0):
    import zlib

    import numpy as np

    out = dict(_drawn_inputs(seed))
    spreads = {'L0_ffn_gate_bias': (0.0, 0.8),
     'L1_attn_bq': (0.0, 0.8),
     'L1_attn_bk': (0.0, 2.0),
     'L1_attn_bv': (0.0, 0.292),
     'L1_attn_bo': (0.0, 0.335),
     'L1_ffn_norm_weight': (1.0, 0.6),
     'L1_ffn_router_bias': (0.0, 0.8),
     'L1_ffn_fc1_bias': (0.0, 0.8),
     'L1_ffn_fc2_bias': (0.0, 0.441)}
    factors = {'L0_attn_Wq': 8.0,
     'L0_attn_Wk': 8.0,
     'L0_attn_Wv': 8.0,
     'L0_attn_Wbeta': 8.0,
     'L0_attn_Wtg': 64.0,
     'L0_attn_mode_logits': 23.858,
     'L0_attn_log_decay': 95.367,
     'L0_attn_omega_log_scale': 32.854,
     'L0_attn_Wg': 8.0,
     'L0_attn_Wo': 8.0,
     'L0_ffn_gate_w': 8.0,
     'L0_ffn_eg_w': 8.0,
     'L0_ffn_eu_w': 8.0,
     'L0_ffn_ed_w': 8.0,
     'L0_ffn_sg_w': 8.0,
     'L0_ffn_su_w': 8.0,
     'L0_ffn_sd_w': 8.0,
     'L0_c': 8.0,
     'L0_wmod': 8.0,
     'L1_attn_Wq': 8.0,
     'L1_attn_Wk': 7.023,
     'L1_attn_Wv': 3.257,
     'L1_ffn_router_weight': 2.754,
     'L1_ffn_fc1_weight': 5.485,
     'L1_ffn_fc2_weight': 4.983}
    for name, (base, spread) in spreads.items():
        noise = np.random.default_rng([zlib.crc32(name.encode()), seed]).standard_normal(out[name].shape)
        drawn = base * np.exp(spread * noise) if base else spread * noise
        out[name] = jnp.asarray(drawn.astype(out[name].dtype))
    for name, factor in factors.items():
        out[name] = (out[name] * factor).astype(out[name].dtype)
    return out
```

```python
import numpy as np
from contextlib import ExitStack, contextmanager

import concourse.bass as bass
from concourse import mybir

F32 = mybir.dt.float32
BF16 = mybir.dt.bfloat16
I32 = mybir.dt.int32
ALU = mybir.AluOpType
ACT = mybir.ActivationFunctionType
AX = mybir.AxisListType

P = 128
D = 128
B, T = 8, 256
TILES = B * T // P
TPB = T // P
H, M, DK, DV = 8, 8, 64, 64
HP = H // 2
HD = DK // 2
CB = 32
NB = P // CB
PW = 5
MASKED = -30000.0
ROUND = 12582912.0


def bc(ap, at, n):
    shape = list(ap.shape)
    shape.insert(at, n)
    return ap.unsqueeze(at).broadcast_to(shape)


def stand(engine):
    engine.nop(nofuse=True)


class Chain:

    def __init__(self, engine, sem):
        self.engine, self.sem, self.n = engine, sem, 0

    def __call__(self, ins):
        self.n += 1
        ins.then_inc(self.sem, 1)
        self.engine.wait_ge(self.sem, self.n)


class Kernel:

    def __init__(self, nc, ctx, ins, out):
        self.nc, self.ctx, self.ins, self.out = nc, ctx, ins, out
        self.sems = []
        sb = self.sb
        self.x = sb(ctx, "x_res", [P, TILES, D])
        self.hT = sb(ctx, "hT", [P, TILES * P])
        self.modT = sb(ctx, "modT", [P, 6, B])
        self.gates = sb(ctx, "gates", [P, 2, B, D])
        self.identf = sb(ctx, "identf", [P, P])
        self.identb = sb(ctx, "identb", [P, P], BF16)
        self.after = sb(ctx, "after", [P, P])
        self.upto = sb(ctx, "upto", [P, P])
        self.maskb = sb(ctx, "maskb", [P, P], BF16)
        self.halves = sb(ctx, "halves", [P, P])
        self.ones = sb(ctx, "ones", [P, P])
        self.identc = sb(ctx, "identc", [P, CB])
        self.parity = sb(ctx, "parity", [P, 2])

    def sb(self, ctx, name, shape, dt=F32):
        return ctx.enter_context(self.nc.sbuf_tensor(name, shape, dt))

    def ps(self, ctx, name, shape, dt=F32):
        return ctx.enter_context(self.nc.psum_tensor(name, shape, dt))

    def sem(self, name):
        self.sems.append(self.nc.alloc_semaphore(name=name))
        return self.sems[-1]

    @contextmanager
    def scope(self):
        before = len(self.sems)
        yield
        self.nc.clear_and_free_semaphores(self.sems[before:])
        del self.sems[before:]
        self.nc.all_engine_barrier()


def phase_constants(k):
    nc = k.nc
    loaded, made = k.sem("x_loaded"), k.sem("const_chain")
    with nc.Block() as block:

        @block.sync
        def _(sp):
            sp.dma_start(k.x[:, :, :], k.ins["x"].rearrange("(n p) d -> p n d", p=P)).then_inc(loaded, 16)
            sp.wait_ge(loaded, 16)

        @block.gpsimd
        def _(pool):
            step = Chain(pool, made)
            step(nc.gpsimd.memset(k.ones[:, :], 1.0))
            step(nc.gpsimd.memset(k.halves[:, :], 0.0))
            step(nc.gpsimd.memset(k.maskb[:, :], MASKED))
            step(nc.gpsimd.memset(k.parity[:, :], 0.0))
            for q in range(NB):
                step(nc.gpsimd.memset(k.parity[CB * q:CB * q + CB, q % 2:q % 2 + 1], 1.0))
            for h in (0, 64):
                step(nc.gpsimd.memset(k.halves[h:h + 64, h:h + 64], 1.0))
            sel = nc.gpsimd.affine_select
            step(sel(out=k.identf[:, :], in_=k.ones[:, :], compare_op=ALU.is_equal, fill=0.0, base=0,
                     pattern=[[1, P]], channel_multiplier=-1))
            step(sel(out=k.identb[:, :], in_=k.ones[:, :], compare_op=ALU.is_equal, fill=0.0, base=0,
                     pattern=[[1, P]], channel_multiplier=-1))
            for q in range(NB):
                rs = slice(CB * q, CB * q + CB)
                step(sel(out=k.identc[rs, :], in_=k.ones[rs, 0:CB], compare_op=ALU.is_equal, fill=0.0, base=0,
                         pattern=[[1, CB]], channel_multiplier=-1))
            step(sel(out=k.after[:, :], in_=k.ones[:, :], compare_op=ALU.is_gt, fill=0.0, base=0,
                     pattern=[[-1, P]], channel_multiplier=1))
            step(sel(out=k.upto[:, :], in_=k.ones[:, :], compare_op=ALU.is_ge, fill=0.0, base=0,
                     pattern=[[1, P]], channel_multiplier=-1))
            step(sel(out=k.maskb[:, :], in_=k.maskb[:, :], compare_op=ALU.is_gt, fill=0.0, base=0,
                     pattern=[[-1, P]], channel_multiplier=1))


def phase_modulation(k, layer):
    nc = k.nc
    with ExitStack() as ctx:
        wmod = k.sb(ctx, f"wmod{layer}", [P, 6 * D])
        scT = k.sb(ctx, f"scT{layer}", [P, B])
        scB = k.sb(ctx, f"scB{layer}", [P, B, P])
        sign = k.sb(ctx, f"sign{layer}", [P, 2, B, D])
        pT = k.ps(ctx, f"pmodT{layer}", [P, 6, B])
        pG = k.ps(ctx, f"pgate{layer}", [P, 2, B, D])
        loaded, act_done, rows_done = (k.sem(f"mod{layer}_{n}") for n in ("loaded", "silu", "rows"))
        pe_done, dve_chain = k.sem(f"mod{layer}_pe"), k.sem(f"mod{layer}_chain")
        with nc.Block() as block:

            @block.sync
            def _(sp):
                sp.dma_start(scT[:, :], k.ins[f"cT{layer}"]).then_inc(loaded, 16)
                sp.dma_start(wmod[:, :], k.ins[f"wmod{layer}"]).then_inc(loaded, 16)

            @block.scalar
            def _(act):
                act.wait_ge(loaded, 32)
                nc.scalar.activation(scT[:, :], scT[:, :], ACT.Silu).then_inc(act_done, 1)

            @block.tensor
            def _(pe):
                pe.wait_ge(act_done, 1)
                for j in range(6):
                    nc.tensor.matmul(pT[:, j, :], wmod[:, j * D:(j + 1) * D], scT[:, :], start=True, stop=True)
                pe.wait_ge(rows_done, 1)
                for i, j in enumerate((2, 5)):
                    for b in range(B):
                        last = nc.tensor.matmul(pG[:, i, b, :], scB[:, b, :], wmod[:, j * D:(j + 1) * D],
                                                start=True, stop=True)
                last.then_inc(pe_done, 1)

            @block.vector
            def _(dve):
                step = Chain(dve, dve_chain)
                dve.wait_ge(act_done, 1)
                nc.vector.tensor_copy(scB[:, :, :], bc(scT[:, :], 2, P)).then_inc(rows_done, 1)
                dve.wait_ge(pe_done, 1)
                step(nc.vector.tensor_copy(k.modT[:, :, :], pT[:, :, :]))
                for j in (1, 4):
                    step(nc.vector.tensor_scalar_add(k.modT[:, j, :], k.modT[:, j, :], 1.0))
                step(nc.vector.tensor_scalar(sign[:, :, :, :], pG[:, :, :, :], 0.0, 2.0, ALU.is_ge, ALU.mult))
                step(nc.vector.tensor_copy(k.gates[:, :, :, :], pG[:, :, :, :]))
                step(nc.vector.scalar_tensor_tensor(k.gates[:, :, :, :], k.gates[:, :, :, :], -1.0,
                                                    k.gates[:, :, :, :], ALU.mult, ALU.max))
                step(nc.vector.tensor_scalar_max(k.gates[:, :, :, :], k.gates[:, :, :, :], 0.25))
                step(nc.vector.scalar_tensor_tensor(k.gates[:, :, :, :], sign[:, :, :, :], -1.0,
                                                    k.gates[:, :, :, :], ALU.add, ALU.mult))


def phase_norm(k, name, shift, scale, write_h=False):
    nc = k.nc
    with ExitStack() as ctx:
        xc = k.sb(ctx, f"{name}_xc", [P, TILES, D])
        sq = k.sb(ctx, f"{name}_sq", [P, TILES, D])
        st = k.sb(ctx, f"{name}_st", [P, 5, TILES])
        pt = k.ps(ctx, f"{name}_pt", [P, TILES * P])
        centred, squared, var_done, log_done, normed, turned = (
            k.sem(f"{name}_{n}") for n in ("centred", "squared", "var", "log", "normed", "turned"))
        chain = k.sem(f"{name}_chain")
        with nc.Block() as block:

            @block.vector
            def _(dve):
                step = Chain(dve, chain)
                step(nc.vector.reduce_sum(st[:, 0, :], k.x[:, :, :], AX.X))
                step(nc.vector.tensor_scalar_mul(st[:, 0, :], st[:, 0, :], 1.0 / D))
                nc.vector.tensor_tensor(xc[:, :, :], k.x[:, :, :], bc(st[:, 0, :], 2, D), ALU.subtract)\
                    .then_inc(centred, 1)
                dve.wait_ge(squared, 1)
                step(nc.vector.reduce_sum(st[:, 1, :], sq[:, :, :], AX.X))
                nc.vector.tensor_scalar(st[:, 1, :], st[:, 1, :], 1.0 / D, 1e-5, ALU.mult, ALU.add)\
                    .then_inc(var_done, 1)
                dve.wait_ge(log_done, 2)
                step(nc.vector.tensor_tensor(st[:, 3, :], st[:, 2, :], st[:, 2, :], ALU.mult))
                step(nc.vector.tensor_tensor(st[:, 3, :], st[:, 3, :], st[:, 1, :], ALU.mult))
                step(nc.vector.tensor_scalar(st[:, 3, :], st[:, 3, :], -0.5, 1.5, ALU.mult, ALU.add))
                step(nc.vector.tensor_tensor(st[:, 4, :], st[:, 2, :], st[:, 3, :], ALU.mult))
                nc.vector.tensor_tensor(xc[:, :, :], xc[:, :, :], bc(st[:, 4, :], 2, D), ALU.mult)\
                    .then_inc(normed, 1)

            @block.scalar
            def _(act):
                act.wait_ge(centred, 1)
                nc.scalar.activation(sq[:, :, :], xc[:, :, :], ACT.Square).then_inc(squared, 1)
                act.wait_ge(var_done, 1)
                nc.scalar.activation(st[:, 2, :], st[:, 1, :], ACT.Ln).then_inc(log_done, 1)
                act.wait_ge(log_done, 1)
                nc.scalar.activation(st[:, 2, :], st[:, 2, :], ACT.Exp, scale=-0.5).then_inc(log_done, 1)
                for b in range(B):
                    act.wait_ge(turned, b // 2 + 1)
                    s = slice(b * T, (b + 1) * T)
                    nc.scalar.activation(k.hT[:, s], pt[:, s], ACT.Identity, bias=k.modT[:, shift, b:b + 1],
                                         scale=k.modT[:, scale, b:b + 1])

            @block.tensor
            def _(pe):
                pe.wait_ge(normed, 1)
                for n in range(TILES):
                    last = nc.tensor.transpose(pt[:, n * P:(n + 1) * P], xc[:, n, :], k.identf[:, :])
                    if n % 4 == 3:
                        last.then_inc(turned, 1)


def phase_l0_tokens(k, a):
    nc = k.nc
    HM = H * M
    with ExitStack() as ctx:
        wv = k.sb(ctx, "wv", [P, H * DV])
        wbt = k.sb(ctx, "wbt", [P, 2 * HM])
        ld = k.sb(ctx, "ld", [P, HM])
        ml = k.sb(ctx, "ml", [P, H, M])
        mst = k.sb(ctx, "mst", [P, 3, H])
        bt = k.sb(ctx, "bt", [P, TILES, 2 * HM])
        gg = k.sb(ctx, "gg", [P, TPB, B, HM])
        dec = k.sb(ctx, "dec", [P, B, HM])
        pv = k.ps(ctx, "pv", [P, 4, 512])
        pb = k.ps(ctx, "pb", [P, TILES, 2 * HM])
        loaded = k.sem("tok_loaded")
        v_done, v_out, b_done = k.sem("tok_v"), k.sem("tok_v_out"), k.sem("tok_b")
        chain, act_done, g_done = k.sem("tok_chain"), k.sem("tok_act"), k.sem("tok_g")
        suffix_done, dve_asks = k.sem("tok_suffix"), k.sem("tok_dve")
        with nc.Block() as block:

            @block.sync
            def _(sp):
                sp.dma_start(wbt[:, :], k.ins["wbt"]).then_inc(loaded, 16)
                sp.dma_start(wv[:, :], k.ins["wv"]).then_inc(loaded, 16)
                sp.dma_start(ld[:, :], k.ins["log_decay"].partition_broadcast(P)).then_inc(loaded, 16)
                sp.dma_start(ml[:, :, :], k.ins["mode_logits"].partition_broadcast(P)).then_inc(loaded, 16)

            @block.tensor
            def _(pe):
                pe.wait_ge(loaded, 64)
                for n in range(TILES):
                    last = nc.tensor.matmul(pb[:, n, :], k.hT[:, n * P:(n + 1) * P], wbt[:, :], start=True, stop=True)
                last.then_inc(b_done, 1)
                for n in range(TILES):
                    if n >= 4:
                        pe.wait_ge(v_out, n - 3)
                    nc.tensor.matmul(pv[:, n % 4, :], k.hT[:, n * P:(n + 1) * P], wv[:, :], start=True, stop=True)\
                        .then_inc(v_done, 1)
                pe.wait_ge(g_done, 1)
                pe.wait_ge(v_out, TILES)
                nc.tensor.matmul(pv[:, 0, :], k.after[:, :], gg[:, 0, :, :].rearrange("p b h -> p (b h)"),
                                 start=True, stop=True).then_inc(suffix_done, 1)

            @block.scalar
            def _(act):
                act.wait_ge(dve_asks, 1)
                nc.scalar.activation(bt[:, :, :], bt[:, :, :], ACT.Exp).then_inc(act_done, 1)
                act.wait_ge(dve_asks, 2)
                nc.scalar.activation(ml[:, :, :], ml[:, :, :], ACT.Exp).then_inc(act_done, 1)
                nc.scalar.activation(ld[:, :], ld[:, :], ACT.Exp).then_inc(act_done, 1)
                act.wait_ge(dve_asks, 3)
                nc.scalar.activation(gg[:, :, :, :], gg[:, :, :, :], ACT.Ln).then_inc(g_done, 1)
                for n in range(TILES):
                    act.wait_ge(v_done, n + 1)
                    nc.scalar.activation(a.v[:, n, :], pv[:, n % 4, :], ACT.Copy).then_inc(v_out, 1)
                act.wait_ge(suffix_done, 1)
                nc.scalar.activation(dec[:, :, :].rearrange("p b h -> p (b h)"), pv[:, 0, :], ACT.Exp)\
                    .then_inc(act_done, 1)

            @block.vector
            def _(dve):
                step = Chain(dve, chain)
                dve.wait_ge(b_done, 1)
                nc.vector.tensor_scalar(bt[:, :, :], pb[:, :, :], -1.0, 80.0, ALU.mult, ALU.min)\
                    .then_inc(dve_asks, 1)
                dve.wait_ge(loaded, 64)
                step(nc.vector.tensor_reduce(mst[:, 0, :], ml[:, :, :], AX.X, ALU.max))
                step(nc.vector.tensor_tensor(ml[:, :, :], ml[:, :, :], bc(mst[:, 0, :], 2, M), ALU.subtract))
                nc.vector.tensor_scalar_min(ld[:, :], ld[:, :], 80.0).then_inc(dve_asks, 1)
                dve.wait_ge(act_done, 3)
                step(nc.vector.reduce_sum(mst[:, 1, :], ml[:, :, :], AX.X))
                step(nc.vector.reciprocal(mst[:, 2, :], mst[:, 1, :]))
                step(nc.vector.tensor_scalar_mul(mst[:, 2, :], mst[:, 2, :], float(DK) ** -0.5))
                step(nc.vector.tensor_tensor(a.wmode[:, :, :].rearrange("p a (g m) -> p (a g) m", g=2), ml[:, :, :],
                                             bc(mst[:, 2, :], 2, M), ALU.mult))
                step(nc.vector.tensor_scalar_add(ld[:, :], ld[:, :], 1.0))
                step(nc.vector.reciprocal(ld[:, :], ld[:, :]))
                step(nc.vector.tensor_scalar_add(bt[:, :, :], bt[:, :, :], 1.0))
                step(nc.vector.reciprocal(bt[:, :, :], bt[:, :, :]))
                tg = bt[:, :, HM:2 * HM].rearrange("p (b t) h -> p t b h", t=TPB)
                for t in range(TPB):
                    step(nc.vector.tensor_tensor(gg[:, t, :, :], tg[:, t, :, :], bc(ld[:, :], 1, B), ALU.mult))
                nc.vector.tensor_scalar_max(gg[:, :, :, :], gg[:, :, :, :], 1e-6).then_inc(dve_asks, 1)
                beta = bt[:, :, 0:HM].rearrange("p (b t) (a c) -> p b t a c", t=TPB, a=HP)
                dve.wait_ge(g_done, 1)
                for t in range(TPB):
                    for hp in range(HP):
                        s = slice(16 * hp, 16 * hp + 16)
                        dst = a.scal[:, :, hp, :, t, :]
                        step(nc.vector.tensor_copy(dst[:, :, 0, :], gg[:, t, :, s]))
                        step(nc.vector.tensor_scalar_mul(dst[:, :, 1, :], beta[:, :, t, hp, :], -1.0))
                        step(nc.vector.tensor_copy(dst[:, :, 2, :], beta[:, :, t, hp, :]))
                dve.wait_ge(act_done, 4)
                for hp in range(HP):
                    s = slice(16 * hp, 16 * hp + 16)
                    for t in range(TPB):
                        step(nc.vector.tensor_tensor(a.scal[:, :, hp, 3, t, :], beta[:, :, 0, hp, :],
                                                     dec[:, :, s], ALU.mult))


def phase_l0_angles(k, a, hp):
    nc = k.nc
    C1, C2 = 6.25, 17.0 / 512
    C3 = -37.0 / 2 ** 21
    C4 = float(2 * np.pi - C1 - C2 - C3)
    LN2_HI = 0.693359375
    LN2_LO = float(np.log(2.0) - LN2_HI)
    with ExitStack() as ctx:
        pos = k.sb(ctx, f"pos{hp}", [P, T])
        frq = k.sb(ctx, f"frq{hp}", [P, 2])
        om = k.sb(ctx, f"om{hp}", [P, 6, M])
        two = k.sb(ctx, f"two{hp}", [P, M], I32)
        turns = k.sb(ctx, f"turns{hp}", [P, M, T])
        loaded, posn = k.sem(f"ang{hp}_loaded"), k.sem(f"ang{hp}_pos")
        chain, ready, sines = k.sem(f"ang{hp}_chain"), k.sem(f"ang{hp}_ready"), k.sem(f"ang{hp}_sines")
        with nc.Block() as block:

            @block.sync
            def _(sp):
                sp.dma_start(frq[:, :], k.ins["freq"]).then_inc(loaded, 16)
                for g in range(2):
                    sp.dma_start(om[64 * g:64 * g + 64, 0, :],
                                 k.ins["omega"][2 * hp + g:2 * hp + g + 1, :].broadcast_to([64, M])).then_inc(loaded, 16)

            @block.gpsimd
            def _(pool):
                nc.gpsimd.iota(pos[:, :], pattern=[[1, T]], base=0, channel_multiplier=0,
                               allow_small_or_imprecise_dtypes=True).then_inc(posn, 1)

            @block.vector
            def _(dve):
                v = nc.vector
                step = Chain(dve, chain)
                dve.wait_ge(loaded, 48)
                w, n, r, p = om[:, 0, :], om[:, 1, :], om[:, 2, :], om[:, 3, :]
                step(v.tensor_scalar(n, w, 1.4426950408889634, ROUND, ALU.mult, ALU.add))
                step(v.tensor_scalar_add(n, n, -ROUND))
                step(v.scalar_tensor_tensor(r, n, -LN2_HI, w, ALU.mult, ALU.add))
                step(v.scalar_tensor_tensor(r, n, -LN2_LO, r, ALU.mult, ALU.add))
                step(v.tensor_scalar(p, r, 1.0 / 40320, 1.0 / 5040, ALU.mult, ALU.add))
                for c in (1 / 720, 1 / 120, 1 / 24, 1 / 6, 0.5, 1.0, 1.0):
                    step(v.tensor_tensor(p, p, r, ALU.mult))
                    step(v.tensor_scalar_add(p, p, float(c)))
                step(v.tensor_scalar(two[:, :], n, 127.0, 8388608.0, ALU.add, ALU.mult))
                step(v.tensor_tensor(p, p, two[:, :].bitcast(F32), ALU.mult))
                dve.wait_ge(posn, 1)
                s, c = a.sin[:, :, :], a.cos[:, :, :]
                step(v.tensor_tensor(s, bc(pos[:, :], 1, M), bc(p, 2, T), ALU.mult))
                step(v.tensor_scalar_mul(s, s, frq[:, 0:1]))
                step(v.tensor_scalar(turns[:, :, :], s, float(1 / (2 * np.pi)), ROUND, ALU.mult, ALU.add))
                step(v.tensor_scalar_add(turns[:, :, :], turns[:, :, :], -ROUND))
                for q in (C1, C2, C3, C4):
                    step(v.scalar_tensor_tensor(s, turns[:, :, :], -q, s, ALU.mult, ALU.add))
                step(v.tensor_scalar(s, s, 3.1415925, -3.1415925, ALU.min, ALU.max))
                step(v.scalar_tensor_tensor(c, s, -1.0, s, ALU.mult, ALU.max))
                step(v.tensor_scalar(c, c, -1.0, float(np.pi / 2), ALU.mult, ALU.add))
                v.tensor_scalar_mul(s, s, frq[:, 1:2]).then_inc(ready, 1)

            @block.scalar
            def _(act):
                act.wait_ge(ready, 1)
                nc.scalar.activation(a.sin[:, :, :], a.sin[:, :, :], ACT.Sin)
                nc.scalar.activation(a.cos[:, :, :], a.cos[:, :, :], ACT.Sin)


class L0Attention:

    def __init__(self, k, ctx):
        sb = k.sb
        self.v = sb(ctx, "values", [P, TILES, H * DV])
        self.scal = sb(ctx, "scal", [P, B, HP, 4, TPB, 16])
        self.wmode = sb(ctx, "wmode", [P, HP, 16])
        self.sin = sb(ctx, "sin_t", [P, M, T])
        self.cos = sb(ctx, "cos_t", [P, M, T])
        self.wo = sb(ctx, "wo", [P, HP, D])
        self.w5 = sb(ctx, "w5", [P, PW, P])
        self.sems = {}


def phase_l0_pair(k, a, hp):
    nc = k.nc
    with ExitStack() as ctx:
        def sb(name, shape, dt=F32):
            return k.sb(ctx, f"{name}_{hp}", shape, dt)

        hb = sb("hb", [P, T])
        ld = sb("ld", [P, TPB, 16])
        sc = sb("sc", [P, 3, TPB, 16])
        sq = sb("sq", [P, 2, T])
        rn = sb("rn", [P, 2, T])
        xn = sb("xn", [P, 2, 2, T])
        gx = sb("gx", [P, T])
        gt = sb("gt", [P, T])
        xr = [sb(f"xr{t}", [P, M, 2, P]) for t in range(TPB)]
        tmp = sb("tmp", [P, M, 2, P])
        gl = [sb(f"gl{g}", [P, M, P]) for g in range(2)]
        e = [sb(f"e{g}", [P, M, P]) for g in range(2)]
        nt = [sb(f"nt{n}", [P, M, P]) for n in range(2)]
        pm = [sb(f"pm{n}", [P, M, P]) for n in range(2)]
        ntd = [sb(f"ntd{g}", [P, M, CB]) for g in range(2)]
        ny = [sb(f"ny{g}", [P, M, 3, CB]) for g in range(2)]
        nkt = [sb(f"nkt{g}", [P, M, 2, CB]) for g in range(2)]
        zt = [sb(f"zt{g}", [P, M, CB]) for g in range(2)]
        r = [sb(f"r{g}", [P, M, DV]) for g in range(2)]
        w = [sb(f"w{g}", [P, M, DV]) for g in range(2)]
        ub = [sb(f"ub{g}", [P, M, DV]) for g in range(2)]
        ua = [sb(f"ua{g}", [P, M, DV]) for g in range(2)]
        og = sb("og", [P, T])
        xg = sb("xg", [P, TPB, D])
        kn = sb("kn", [P, M, P])
        st = sb("st", [P, M, DV])
        pe2 = k.ps(ctx, f"pE_{hp}", [P, 2, 512])
        ps2 = k.ps(ctx, f"pS_{hp}", [P, 2, 2, 2, P])
        px = [k.ps(ctx, f"pX{g}_{hp}", [P, 512]) for g in range(2)]
        pk = k.ps(ctx, f"pK_{hp}", [P, 512])
        po = k.ps(ctx, f"pO_{hp}", [P, 512])
        wide = [u[:, :, :].rearrange("p m (s c) -> p m s c", s=2) for u in ua]
        pxl = [x[:, :].rearrange("p (m s c) -> p m s c", m=M, s=2) for x in px]
        pxw = [x[:, :].rearrange("p (m v) -> p m v", m=M) for x in px]

        sems = a.sems

        def S(name):
            if name not in sems:
                sems[name] = k.sem(name)
            return sems[name]

        wl = S("weights_loaded")
        with nc.Block() as block:

            @block.sync
            def _(sp):
                sp.dma_start(a.w5[:, :, :], k.ins["w5"][:, hp, :, :]).then_inc(wl, 16)
                if hp == 0:
                    sp.dma_start(a.wo[:, :, :], k.ins["wo0"]).then_inc(S("wo_loaded"), 16)

            @block.tensor
            def _(pe):
                mm = nc.tensor.matmul
                pe.wait_ge(wl, 16 * (hp + 1))
                pe.wait_ge(S("wo_loaded"), 16)

                def project(nx, it=None):
                    pe.wait_ge(S("staged_h"), nx + 1)
                    if it is not None:
                        pe.wait_ge(S("e_done"), it * 5 + 5)
                        pe.wait_ge(S("state"), it + 1)
                    for j in range(4):
                        last = mm(pe2[:, j // 2, (j % 2) * T:(j % 2 + 1) * T], a.w5[:, j, :], hb[:, :],
                                  start=True, stop=True)
                    last.then_inc(S("proj"), 1)
                    mm(pk[:, 0:T], a.w5[:, 4, :], hb[:, :], start=True, stop=True).then_inc(S("gproj"), 1)

                def norm_sums(nx, it=None):
                    pe.wait_ge(S("squares"), nx + 1)
                    if it is not None:
                        pe.wait_ge(S("pair_out"), it * 16 + 16)
                    mm(ps2[:, 0, :, :, :].rearrange("p a b t -> p (a b t)"), k.halves[:, :],
                       sq[:, :, :].rearrange("p a t -> p (a t)"), start=True, stop=True).then_inc(S("norms"), 1)

                def exponents(it, n):
                    pe.wait_ge(S("gl_done"), it * 4 + n + 1)
                    if n == 0:
                        pe.wait_ge(S("xn_done"), it + 1)
                    else:
                        pe.wait_ge(S("e_done"), it * 5 + n)
                    for i in range(2):
                        mm(pe2[:, i, :], k.after[:, :],
                           gl[n % 2][:, 4 * i:4 * i + 4, :].rearrange("p m t -> p (m t)"), start=True, stop=False)
                        last = mm(pe2[:, i, :], k.identb[:, :], bc(k.maskb[:, :], 1, 4), start=False, stop=True)
                    last.then_inc(S("expo"), 1)

                def products(it, n, j):
                    t, g = n // 2, n % 2
                    hs, kk = slice(64 * g, 64 * g + 64), n * 4 + j
                    if kk % 8 == 0:
                        pe.wait_ge(S("xr_done"), it * 2 + t + 1)
                    if kk >= 2:
                        pe.wait_ge(S("pair_out"), it * 16 + kk - 1)
                    elif not isinstance(it, int):
                        pe.wait_ge(S("pair_out"), it * 16)
                    for m in (2 * j, 2 * j + 1):
                        last = mm(ps2[:, j % 2, m % 2, :, :].rearrange("p a t -> p (a t)"), xr[t][hs, m, 1, :],
                                  xr[t][hs, m, :, :].rearrange("p a t -> p (a t)"), start=True, stop=True)
                    last.then_inc(S("pair"), 1)

                def turn_keys(it, i):
                    if i:
                        pe.wait_ge(S("kn_done"), it * 2 + 1)
                    else:
                        pe.wait_ge(S("gate_read"), it + 1)
                        pe.wait_ge(S("end_dve"), it + 1)
                    for m in range(4 * i, 4 * i + 4):
                        last = nc.tensor.transpose(pk[:, (m % 4) * P:(m % 4 + 1) * P], xr[0][:, m, 1, :],
                                                   k.identf[:, :])
                    last.then_inc(S("kturn"), 1)

                def batch(b, more):
                    it = b + hp * B
                    for t in range(TPB):
                        for g in range(2):
                            n = 2 * t + g
                            hs = slice(64 * g, 64 * g + 64)
                            if n:
                                exponents(it, n)
                            for j in range(0 if n else 2, 4):
                                products(it, n, j)
                        if t == 1:
                            pe.wait_ge(S("e_done"), it * 5 + 4)
                            for g in range(2):
                                for i in range(2):
                                    last = mm(pe2[64 * g:64 * g + 64, i, :], k.ones[:, 0:64],
                                              gl[g][:, 4 * i:4 * i + 4, :].rearrange("p m t -> p (m t)"),
                                              start=True, stop=True)
                            last.then_inc(S("grow"), 1)
                        for lv in range(5):
                            for g in range(2):
                                n = 2 * t + g
                                pe.wait_ge(S(f"level{g}"), it * 12 + t * 6 + lv + 1)
                                if lv:
                                    pe.wait_ge(S(f"kept{g}"), it * 10 + t * 5 + lv)
                                else:
                                    pe.wait_ge(S(f"spread{g}"), it * 2 + t + 1)
                                stand(pe)
                                left = nkt[g] if lv else wide[g]
                                lo, hi = ((0, 1), (0, 2), (0, 2), (0, 2), (1, 2))[lv]
                                for m in range(M):
                                    for hs in (slice(0, 64), slice(64, P)):
                                        last = mm(pxl[g][hs, m, lo:hi, :], left[hs, m, :, :].rearrange("p s c -> p (s c)"),
                                                  ny[g][hs, m, lo:hi, :], start=True, stop=True)
                                last.then_inc(S(f"power{g}"), 1)
                            if t == 1 and more and lv == 0:
                                project(it + 1, it)
                            if t == 1 and more and lv == 1:
                                norm_sums(it + 1, it)
                        if t == 1:
                            pe.wait_ge(S("state"), it + 1)
                            pe.wait_ge(S("xscaled"), it + 1)
                            for g in range(2):
                                hs = slice(64 * g, 64 * g + 64)
                                pe.wait_ge(S(f"level{g}"), it * 12 + 12)
                                for m in range(M):
                                    last = mm(pxw[g][:, m, :], xr[1][hs, m, 1, :], st[hs, m, :], start=True, stop=True)
                                last.then_inc(S("from_state"), 1)
                        for c in range(NB):
                            rs = slice(CB * c, CB * c + CB)
                            if c:
                                for g in range(2):
                                    pe.wait_ge(S(f"w_out{g}"), it * 8 + t * 4 + c)
                                    stand(pe)
                                    for m in range(M):
                                        last = mm(pxw[g][rs, m, :], nt[g][0:CB * c, m, rs], w[g][0:CB * c, m, :],
                                                  start=True, stop=True)
                                    last.then_inc(S(f"carried{g}"), 1)
                            for g in range(2):
                                if c == 0:
                                    pe.wait_ge(S(f"level{g}"), it * 12 + t * 6 + 6)
                                pe.wait_ge(S(f"right{g}"), it * 8 + t * 4 + c + 1)
                                stand(pe)
                                for m in range(M):
                                    last = mm(pxw[g][rs, m, :], zt[g][rs, m, :], r[g][rs, m, :], start=True, stop=True)
                                last.then_inc(S(f"solved{g}"), 1)
                            if t == 0 and c < 2:
                                turn_keys(it, c)
                        for g in range(2):
                            n = 2 * t + g
                            hs = slice(64 * g, 64 * g + 64)
                            pe.wait_ge(S("u_done") if g else S("u_first"), it * 2 + t + 1)
                            for m in range(M):
                                last = mm(po[hs, t * P:(t + 1) * P], ub[g][:, m, :], pm[g][:, m, :],
                                          start=(m == 0), stop=(t == 0 and m == M - 1))
                            if t == 1:
                                for m in range(M):
                                    last = mm(po[hs, P:2 * P], st[hs, m, :], xr[1][hs, m, 0, :],
                                              start=False, stop=(m == M - 1))
                            last.then_inc(S("o_done"), 1)
                        if t == 0:
                            pe.wait_ge(S("kn_done"), it * 2 + 2)
                            for g in range(2):
                                hs = slice(64 * g, 64 * g + 64)
                                pe.wait_ge(S("ua_done"), it * 2 + g + 1)
                                for m in range(M):
                                    last = mm(pk[hs, m * DV:(m + 1) * DV], kn[:, m, hs], ua[g][:, m, :],
                                              start=True, stop=True)
                            last.then_inc(S("s_done"), 1)
                    if more:
                        exponents(it + 1, 0)
                        for j in range(2):
                            products(it + 1, 0, j)
                    pe.wait_ge(S("og_done"), it + 1)
                    for t in range(TPB):
                        last = mm(pk[:, t * D:(t + 1) * D], og[:, t * P:(t + 1) * P], a.wo[:, hp, :],
                                  start=True, stop=True)
                    last.then_inc(S("out_done"), 1)

                project(hp * B)
                norm_sums(hp * B)
                exponents(hp * B, 0)
                for j in range(2):
                    products(hp * B, 0, j)
                with pe.Fori(0, B - 1) as b:
                    batch(b, True)
                batch(B - 1, False)

            @block.scalar
            def _(act):
                cp = nc.scalar.activation

                def stage_h(b, nx):
                    if not isinstance(nx, int) or nx:
                        act.wait_ge(S("gproj"), nx)
                    cp(hb[:, :], k.hT[:, bass.ds(b * T, T)], ACT.Copy).then_inc(S("staged_h"), 1)

                def squares(nx):
                    act.wait_ge(S("proj"), nx + 1)
                    cp(sq[:, :, :], pe2[:, 0, :].rearrange("p (a t) -> p a t", a=2), ACT.Square)\
                        .then_inc(S("squares"), 1)
                    act.wait_ge(S("gproj"), nx + 1)
                    if not isinstance(nx, int) or nx:
                        act.wait_ge(S("gate_one"), nx)
                    cp(gx[:, :], pk[:, 0:T], ACT.Exp, scale=-1.0).then_inc(S("gate_read"), 1)

                def inverse_norms(nx):
                    act.wait_ge(S("norm_eps"), nx + 1)
                    cp(rn[:, :, :], rn[:, :, :], ACT.Ln).then_inc(S("rn_log"), 1)
                    act.wait_ge(S("rn_log"), nx + 1)
                    cp(rn[:, :, :], rn[:, :, :], ACT.Exp, scale=-0.5).then_inc(S("rn_done"), 1)

                def decays(it, n):
                    g = n % 2
                    act.wait_ge(S("expo"), it * 4 + n + 1)
                    if n >= 2:
                        act.wait_ge(S("pair_out"), it * 16 + 4 * (n - 1))
                    elif n == 0 and (not isinstance(it, int) or it):
                        act.wait_ge(S("pair_out"), it * 16)
                    cp(e[g][:, :, :].rearrange("p (a m) t -> p a (m t)", a=2), pe2[:, :, :], ACT.Exp)\
                        .then_inc(S("e_done"), 1)

                def batch(b, more):
                    it = b + hp * B
                    for t in range(TPB):
                        for g in range(2):
                            n = 2 * t + g
                            if n == 2 and more:
                                stage_h(b + 1, it + 1)
                            if n:
                                decays(it, n)
                        if t == 1:
                            act.wait_ge(S("grow"), it + 1)
                            act.wait_ge(S("xr_done"), it * 2 + 2)
                            cp(tmp[:, 0:4, :, :].rearrange("p a b t -> p (a b t)"),
                               pe2[:, :, :].rearrange("p a t -> p (a t)"), ACT.Exp).then_inc(S("e_done"), 1)

                        for g in range(2):
                            act.wait_ge(S("ntd_done"), it * 16 + 4 * (2 * t + g) + 4)
                            for s in range(2):
                                last = cp(wide[g][:, :, s, :], ntd[g][:, :, :], ACT.Identity, scale=k.parity[:, s:s + 1])
                            last.then_inc(S(f"spread{g}"), 1)
                        for lv in range(5):
                            for g in range(2):
                                act.wait_ge(S(f"power{g}"), it * 10 + t * 5 + lv + 1)
                                if lv < 4:
                                    if lv:
                                        act.wait_ge(S(f"level{g}"), it * 12 + t * 6 + lv + 1)
                                    for s in range(2):
                                        last = cp(wide[g][:, :, s, :], pxl[g][:, :, 0, :], ACT.Identity,
                                                  scale=k.parity[:, s:s + 1])
                                    last.then_inc(S(f"wide{g}"), 1)
                                if lv == 0:
                                    cp(ny[g][:, :, 0, :], pxl[g][:, :, 0, :], ACT.Copy).then_inc(S(f"kept{g}"), 1)
                                elif lv < 4:
                                    cp(ny[g][:, :, 0:3:2, :], pxl[g][:, :, :, :], ACT.Copy).then_inc(S(f"kept{g}"), 1)
                                else:
                                    cp(ny[g][:, :, 2, :], pxl[g][:, :, 1, :], ACT.Copy).then_inc(S(f"kept{g}"), 1)
                            if t == 1 and more and lv == 0:
                                squares(it + 1)
                            if t == 1 and more and lv == 2:
                                inverse_norms(it + 1)
                        for c in range(NB):
                            rs = slice(CB * c, CB * c + CB)
                            for g in range(2):
                                act.wait_ge(S(f"solved{g}"), it * 8 + t * 4 + c + 1)
                                cp(w[g][rs, :, :], pxw[g][rs, :, :], ACT.Copy).then_inc(S(f"w_out{g}"), 1)
                            if t == 0 and c < 2:
                                act.wait_ge(S("kturn"), it * 2 + c + 1)
                                cp(kn[:, 4 * c:4 * c + 4, :].rearrange("p m c -> p (m c)"), pk[:, :], ACT.Copy)\
                                    .then_inc(S("kn_done"), 1)
                        if t == 0:
                            act.wait_ge(S("s_done"), it + 1)
                            cp(st[:, :, :].rearrange("p m v -> p (m v)"), pk[:, :], ACT.Copy).then_inc(S("state"), 1)
                    if more:
                        decays(it + 1, 0)

                stage_h(0, hp * B)
                squares(hp * B)
                inverse_norms(hp * B)
                decays(hp * B, 0)
                with act.Fori(0, B - 1) as b:
                    batch(b, True)
                batch(B - 1, False)

            @block.vector
            def _(dve):
                v = nc.vector
                if hp == 0:
                    dve.sem_inc(S("end_dve"), 1)

                def stage_decays(b, nx):
                    if not isinstance(nx, int) or nx:
                        dve.wait_ge(S("gl_done"), nx * 4)
                    v.tensor_copy(ld[:, :, :], a.scal[:, bass.ds(b, 1), hp, 0, :, :].squeeze(1)).then_inc(S("staged_d"), 1)

                def norms(nx):
                    dve.wait_ge(S("norms"), nx + 1)
                    v.tensor_scalar_add(rn[:, :, :].rearrange("p a t -> p (a t)"),
                                        ps2[:, 0, :, :, :].rearrange("p a b t -> p (a b t)"), 1e-6)\
                        .then_inc(S("norm_eps"), 1)

                def normed(nx):
                    dve.wait_ge(S("rn_done"), nx + 1)
                    dve.wait_ge(S("squares"), nx + 1)
                    if not isinstance(nx, int) or nx:
                        dve.wait_ge(S("tmp_done"), nx * 2)
                    v.tensor_tensor(xn[:, :, :, :].rearrange("p s a t -> p s (a t)"), pe2[:, :, :],
                                    bc(rn[:, :, :].rearrange("p a t -> p (a t)"), 1, 2), ALU.mult).then_inc(S("xn_done"), 1)

                def rotate_cos(nx, t, i):
                    ts, ms = slice(t * P, (t + 1) * P), slice(4 * i, 4 * i + 4)
                    if i == 0:
                        dve.wait_ge(S("xn_done"), nx + 1)
                    v.tensor_tensor(xr[t][:, ms, :, :], bc(xn[:, 0, :, ts], 1, 4), bc(a.cos[:, ms, ts], 2, 2), ALU.mult)\
                        .then_inc(S("xr_part"), 1)

                def rotate_sin(nx, t, i):
                    ms = slice(4 * i, 4 * i + 4)
                    dve.wait_ge(S("xr_part"), nx * 4 + 2 * t + i + 1)
                    if i == 0:
                        dve.wait_ge(S("tmp_done"), nx * 2 + t + 1)
                    last = v.tensor_tensor(xr[t][:, ms, :, :], xr[t][:, ms, :, :], tmp[:, ms, :, :], ALU.add)
                    if i:
                        last.then_inc(S("xr_done"), 1)

                def stage_scalars(b, nx):
                    v.tensor_copy(sc[:, :, :, :], a.scal[:, bass.ds(b, 1), hp, 1:4, :, :].squeeze(1)).then_inc(S("staged_s"), 1)
                    dve.wait_ge(S("staged_s"), nx + 1)

                def decayed(it, n, j):
                    t, g = n // 2, n % 2
                    if j == 0:
                        dve.wait_ge(S("e_done"), it * 5 + n + 1)
                        if t == 1:
                            dve.wait_ge(S("o_done"), it * 4 + g + 2)
                    dve.wait_ge(S("pair"), it * 16 + n * 4 + j + 1)
                    for m in (2 * j, 2 * j + 1):
                        v.scalar_tensor_tensor(nt[g][:, m, :], ps2[:, j % 2, m % 2, 1, :],
                                               sc[:, 0, t, g * M + m:g * M + m + 1], e[g][:, m, :],
                                               ALU.mult, ALU.mult)
                    v.tensor_tensor(pm[g][:, 2 * j:2 * j + 2, :], ps2[:, j % 2, :, 0, :],
                                    e[g][:, 2 * j:2 * j + 2, :], ALU.mult).then_inc(S("pair_out"), 1)

                def batch(b, more):
                    it = b + hp * B
                    for t in range(TPB):
                        for g in range(2):
                            n = 2 * t + g
                            for j in range(0 if n else 2, 4):
                                decayed(it, n, j)
                        for g in range(2):
                            n = 2 * t + g
                            dve.wait_ge(S("ntd_done"), it * 16 + 4 * n + 4)
                            v.transpose(ny[g][:, :, 0, :], ntd[g][:, :, :]).then_inc(S(f"turned{g}"), 1)
                            dve.wait_ge(S(f"turned{g}"), it * 2 + t + 1)
                            v.tensor_tensor(ny[g][:, :, 1, :], ny[g][:, :, 0, :], bc(k.identc[:, :], 1, M), ALU.add)\
                                .then_inc(S(f"level{g}"), 1)
                        if t == 1 and more:
                            stage_decays(b + 1, it + 1)
                        for lv in range(5):
                            for g in range(2):
                                if lv < 4:
                                    dve.wait_ge(S(f"wide{g}"), it * 8 + t * 4 + lv + 1)
                                    turn = v.transpose(nkt[g][:, :, :, :].rearrange("p m s c -> p (m s) c"),
                                                       wide[g][:, :, :, :].rearrange("p m s c -> p (m s) c"))
                                    if lv == 0:
                                        turn.then_inc(S(f"level{g}"), 1)
                                if lv:
                                    dve.wait_ge(S(f"kept{g}"), it * 10 + t * 5 + lv + 1)
                                    v.tensor_tensor(ny[g][:, :, 1, :], ny[g][:, :, 1, :], ny[g][:, :, 2, :], ALU.add)\
                                        .then_inc(S(f"level{g}" if lv < 4 else f"summed{g}"), 1)
                                if lv == 4:
                                    dve.wait_ge(S(f"summed{g}"), it * 2 + t + 1)
                                    v.transpose(zt[g][:, :, :], ny[g][:, :, 1, :]).then_inc(S(f"level{g}"), 1)
                                if t == 0 and lv == 0:
                                    rotate_cos(it, 1, g)
                                if t == 0 and lv == 2:
                                    rotate_sin(it, 1, g)
                                if t == 0 and lv == 3 and g == 0:
                                    dve.wait_ge(S("gate_read"), it + 1)
                                    v.tensor_scalar_add(gt[:, :], gx[:, :], 1.0).then_inc(S("gate_one"), 1)
                                    dve.wait_ge(S("gate_one"), it + 1)
                                    v.reciprocal(gt[:, :], gt[:, :]).then_inc(S("gate_done"), 1)
                                if t == 1 and more:
                                    if lv == 1 and g == 1:
                                        norms(it + 1)
                                    if lv == 2 and g == 1:
                                        normed(it + 1)
                                    if lv == 3:
                                        if g == 0:
                                            dve.wait_ge(S("kturn"), it * 2 + 2)
                                        rotate_cos(it + 1, 0, g)
                        if t == 1:
                            if more:
                                for i in range(2):
                                    rotate_sin(it + 1, 0, i)
                            for g in range(2):
                                dve.wait_ge(S("from_state"), it * 2 + g + 1)
                                dve.wait_ge(S("r_done"), it * 4 + 2 + g + 1)
                                v.tensor_tensor(r[g][:, :, :], r[g][:, :, :], pxw[g][:, :, :], ALU.subtract)\
                                    .then_inc(S(f"right{g}"), 1)
                        else:
                            for g in range(2):
                                dve.wait_ge(S("r_done"), it * 4 + g + 1)
                                dve.sem_inc(S(f"right{g}"), 1)
                        for c in range(1, NB):
                            rs = slice(CB * c, CB * c + CB)
                            for g in range(2):
                                dve.wait_ge(S(f"carried{g}"), it * 6 + t * 3 + c)
                                if t == 1:
                                    dve.wait_ge(S(f"right{g}"), it * 8 + 5)
                                v.tensor_tensor(r[g][rs, :, :], r[g][rs, :, :], pxw[g][rs, :, :], ALU.add)\
                                    .then_inc(S(f"right{g}"), 1)
                        dve.wait_ge(S("w_out0"), it * 8 + t * 4 + 4)
                        v.tensor_tensor(ub[0][:, :, :], w[0][:, :, :], bc(sc[:, 1, t, 0:M], 2, DV), ALU.mult)\
                            .then_inc(S("u_first"), 1)
                    dve.wait_ge(S("o_done"), it * 4 + 5)
                    dve.wait_ge(S("gate_done"), it + 1)
                    v.tensor_tensor(og[:, :], po[:, 0:T], gt[:, :], ALU.mult).then_inc(S("og_done"), 1)
                    if more:
                        stage_scalars(b + 1, it + 1)
                        for j in range(2):
                            decayed(it + 1, 0, j)
                    dve.wait_ge(S("out_done"), it + 1)
                    ga = k.gates[:, 0, bass.ds(b, 1), :].broadcast_to([P, TPB, D])
                    v.tensor_tensor(xg[:, :, :], pk[:, 0:T].rearrange("p (t d) -> p t d", t=TPB), ga, ALU.mult)\
                        .then_inc(S("xg_done"), 1)
                    dve.wait_ge(S("xg_done"), it + 1)
                    xb = k.x[:, bass.ds(b * TPB, TPB), :]
                    v.tensor_tensor(xb, xb, xg[:, :, :], ALU.add).then_inc(S("end_dve"), 1)

                stage_decays(0, hp * B)
                norms(hp * B)
                normed(hp * B)
                for i in range(2):
                    rotate_cos(hp * B, 0, i)
                for i in range(2):
                    rotate_sin(hp * B, 0, i)
                stage_scalars(0, hp * B)
                for j in range(2):
                    decayed(hp * B, 0, j)
                with dve.Fori(0, B - 1) as b:
                    batch(b, True)
                batch(B - 1, False)

            @block.gpsimd
            def _(pool):
                p = nc.gpsimd
                if hp == 0:
                    pool.sem_inc(S("o_done"), 1)

                def decays(t, g):
                    p.affine_select(out=gl[g][:, :, :], in_=bc(ld[:, t, g * M:g * M + M], 2, P),
                                    compare_op=ALU.is_ge, fill=0.0, base=0, pattern=[[0, M], [1, P]],
                                    channel_multiplier=-1).then_inc(S("gl_done"), 1)

                def first_decays(nx):
                    if not isinstance(nx, int) or nx:
                        pool.wait_ge(S("grow"), nx)
                    pool.wait_ge(S("staged_d"), nx + 1)
                    stand(pool)
                    decays(0, 0)
                    decays(0, 1)

                def rotate(nx, t):
                    ts = slice(t * P, (t + 1) * P)
                    pool.wait_ge(S("xn_done"), nx + 1)
                    p.tensor_tensor(tmp[:, :, :, :], bc(xn[:, 1, :, ts], 1, M), bc(a.sin[:, :, ts], 2, 2), ALU.mult)\
                        .then_inc(S("tmp_done"), 1)

                def batch(b, more):
                    it = b + hp * B
                    pool.wait_ge(S("staged_s"), it + 1)

                    def right_side(t, g):
                        pool.wait_ge(S("o_done"), it * 4 + 1 + (g + 1 if t else 0))
                        p.tensor_tensor(r[g][:, :, :],
                                        bc(a.v[:, bass.ds(b * TPB + t, 1), (2 * hp + g) * DV:(2 * hp + g + 1) * DV].squeeze(1), 1, M),
                                        bc(a.wmode[:, hp, g * M:g * M + M], 2, DV), ALU.mult).then_inc(S("r_done"), 1)

                    pool.wait_ge(S("xr_done"), it * 2 + 1)
                    rotate(it, 1)
                    for t in range(TPB):
                        if t:
                            for g in range(2):
                                pool.wait_ge(S("expo"), it * 4 + g + 1)
                                stand(pool)
                                decays(1, g)
                        for g in range(2):
                            n = 2 * t + g
                            pool.wait_ge(S("pair_out"), it * 16 + 4 * n + 4)
                            if t:
                                pool.wait_ge(S(f"power{g}"), it * 10 + 1)
                            stand(pool)
                            for q in range(NB):
                                rs = slice(CB * q, CB * q + CB)
                                p.affine_select(out=ntd[g][rs, :, :], in_=nt[g][rs, :, rs], compare_op=ALU.is_gt,
                                                fill=0.0, base=0, pattern=[[0, M], [1, CB]], channel_multiplier=-1)\
                                    .then_inc(S("ntd_done"), 1)
                                pool.wait_ge(S("ntd_done"), it * 16 + 4 * n + q + 1)
                                stand(pool)
                        for g in range(2):
                            right_side(t, g)
                        if t == 1:
                            pool.wait_ge(S("e_done"), it * 5 + 5)
                            pool.wait_ge(S("pair_out"), it * 16 + 16)
                            last = p.tensor_tensor(xr[1][:, :, :, :], xr[1][:, :, :, :],
                                                   bc(tmp[:, 0:4, :, :].rearrange("p a b t -> p (a b) t"), 2, 2), ALU.mult)
                            last.then_inc(S("xscaled"), 1)
                            if more:
                                first_decays(it + 1)
                                pool.wait_ge(S("xscaled"), it + 1)
                                rotate(it + 1, 0)
                        pool.wait_ge(S("w_out1"), it * 8 + t * 4 + 4)
                        p.tensor_tensor(ub[1][:, :, :], w[1][:, :, :], bc(sc[:, 1, t, M:2 * M], 2, DV), ALU.mult)\
                            .then_inc(S("u_done"), 1)
                        if t == 0:
                            pool.wait_ge(S("w_out0"), it * 8 + 4)
                            for g in range(2):
                                p.tensor_tensor(ua[g][:, :, :], w[g][:, :, :], bc(sc[:, 2, t, g * M:g * M + M], 2, DV), ALU.mult)\
                                    .then_inc(S("ua_done"), 1)

                first_decays(hp * B)
                rotate(hp * B, 0)
                with pool.Fori(0, B - 1) as b:
                    batch(b, True)
                batch(B - 1, False)


def program(nc, ins, out, stage=9, first=1):
    with ExitStack() as ctx:
        k = Kernel(nc, ctx, ins, out)

        def run(phase, *args):
            with k.scope():
                phase(k, *args)

        run(phase_constants)
        run(phase_modulation, 0)
        if first <= 1:
            run(phase_norm, "ln0a", 0, 1)
            with ExitStack() as actx, k.scope():
                a = L0Attention(k, actx)
                run(phase_l0_tokens, a)
                for hp in range(HP):
                    run(phase_l0_angles, a, hp)
                    phase_l0_pair(k, a, hp)
        if stage >= 2 and first <= 2:
            run(phase_norm, "ln0f", 3, 4)
            combT = nc.dram_tensor("comb0", (64, TILES * P), F32, kind="Internal").ap()
            with ExitStack() as ectx:
                res = k.sb(ectx, "res0", [P, TILES * P])
                run(phase_route0, combT)
                run(phase_experts0, combT, res)
                run(phase_back, "back0", res, 1)
        if stage >= 3:
            run(phase_modulation, 1)
            run(phase_norm, "ln1a", 0, 1)
            run(phase_l1_attention)
        if stage >= 4:
            run(phase_norm, "ln1f", 3, 4)
            gatesT = nc.dram_tensor("gates1", (16, TILES * P), F32, kind="Internal").ap()
            slotsT = nc.dram_tensor("slotrows1", (16, TILES * P), BF16, kind="Internal").ap()
            with ExitStack() as ectx:
                res = k.sb(ectx, "res1", [P, TILES * P])
                gts = k.sb(ectx, "gts1", [16, TILES * P])
                xt = k.sb(ectx, "xt1", [P, TILES, D])
                slots = k.sb(ectx, "slots1", [P, 16, TILES])
                run(phase_route1, gatesT, slotsT, gts, xt, slots)
                run(phase_experts1, gatesT, slotsT, gts, xt, slots, res)
                run(phase_back, "back1", res, 1)
        run(phase_store)


def phase_route0(k, combT):
    nc = k.nc
    E, G = 64, 8
    TG, K = 4, 6
    with ExitStack() as ctx:
        gw = k.sb(ctx, "r0_gw", [P, E])
        bias = k.sb(ctx, "r0_bias", [P, E])
        sc = k.sb(ctx, "r0_sc", [P, TILES, E])
        gs = k.sb(ctx, "r0_gs", [P, TILES, G])
        cmp = k.sb(ctx, "r0_cmp", [P, TILES, G, G])
        cmq = k.sb(ctx, "r0_cmq", [P, TILES, G, G])
        cnt = k.sb(ctx, "r0_cnt", [P, 2, TILES, G])
        tri = k.sb(ctx, "r0_tri", [P, G, G])
        top = k.sb(ctx, "r0_top", [P, TILES, 8])
        eq = k.sb(ctx, "r0_eq", [P, TILES, E])
        gt = k.sb(ctx, "r0_gt", [P, TILES, E])
        cum = k.sb(ctx, "r0_cum", [P, TILES, E])
        one = k.sb(ctx, "r0_one", [P, E])
        left = k.sb(ctx, "r0_left", [P, 2, TILES])
        ct = k.sb(ctx, "r0_ct", [E, TILES * P])
        pl = k.ps(ctx, "r0_pl", [P, TILES, E])
        pc = k.ps(ctx, "r0_pc", [E, TILES * P])
        loaded, logits, neg, expd, made = (k.sem(f"r0_{n}") for n in ("loaded", "logits", "neg", "exp", "tri"))
        chain, comb, turned, copied, kept = (k.sem(f"r0_{n}") for n in ("chain", "comb", "turned", "copied", "kept"))
        with nc.Block() as block:

            @block.sync
            def _(sp):
                sp.dma_start(gw[:, :], k.ins["gate_w"]).then_inc(loaded, 16)
                sp.dma_start(bias[:, :], k.ins["gate_bias"].partition_broadcast(P)).then_inc(loaded, 16)
                sp.wait_ge(copied, 4)
                sp.dma_start(combT, ct[:, :]).then_inc(kept, 16)
                sp.wait_ge(kept, 16)

            @block.gpsimd
            def _(pool):
                nc.gpsimd.affine_select(out=tri[:, :, :], in_=k.ones[:, 0:G * G].rearrange("p (a b) -> p a b", a=G),
                                        compare_op=ALU.is_gt, fill=0.0, base=0, pattern=[[1, G], [-1, G]],
                                        channel_multiplier=0).then_inc(made, 1)

            @block.tensor
            def _(pe):
                pe.wait_ge(loaded, 32)
                for n in range(TILES):
                    last = nc.tensor.matmul(pl[:, n, :], k.hT[:, n * P:(n + 1) * P], gw[:, :], start=True, stop=True)
                last.then_inc(logits, 1)
                pe.wait_ge(comb, 1)
                for n in range(TILES):
                    last = nc.tensor.transpose(pc[:, n * P:(n + 1) * P], cum[:, n, :], k.identf[:, :])
                    if n % 4 == 3:
                        last.then_inc(turned, 1)

            @block.scalar
            def _(act):
                act.wait_ge(neg, 1)
                nc.scalar.activation(sc[:, :, :], sc[:, :, :], ACT.Exp).then_inc(expd, 1)
                for i in range(4):
                    act.wait_ge(turned, i + 1)
                    nc.scalar.activation(ct[:, i * 512:(i + 1) * 512], pc[:, i * 512:(i + 1) * 512], ACT.Copy)\
                        .then_inc(copied, 1)

            @block.vector
            def _(dve):
                v = nc.vector
                step = Chain(dve, chain)
                step(v.memset(one[:, :], 1.0))
                dve.wait_ge(logits, 1)
                v.tensor_scalar(sc[:, :, :], pl[:, :, :], -1.0, 80.0, ALU.mult, ALU.min).then_inc(neg, 1)
                dve.wait_ge(expd, 1)
                step(v.tensor_scalar_add(sc[:, :, :], sc[:, :, :], 1.0))
                step(v.reciprocal(sc[:, :, :], sc[:, :, :]))
                step(v.tensor_tensor(sc[:, :, :], sc[:, :, :], bc(bias[:, :], 1, TILES), ALU.add))
                step(v.tensor_reduce(gs[:, :, :], sc[:, :, :].rearrange("p n (g e) -> p n g e", g=G), AX.X, ALU.max))
                a, b = bc(gs[:, :, :], 2, G), bc(gs[:, :, :], 3, G)
                step(v.tensor_tensor(cmp[:, :, :, :], a, b, ALU.is_gt))
                step(v.tensor_tensor(cmq[:, :, :, :], a, b, ALU.is_equal))
                dve.wait_ge(made, 1)
                step(v.tensor_tensor(cmq[:, :, :, :], cmq[:, :, :, :], bc(tri[:, :, :], 1, TILES), ALU.mult))
                step(v.tensor_tensor(cmp[:, :, :, :], cmp[:, :, :, :], cmq[:, :, :, :], ALU.add))
                step(v.reduce_sum(cnt[:, 0, :, :], cmp[:, :, :, :], AX.X))
                step(v.tensor_scalar(cnt[:, 1, :, :], cnt[:, 0, :, :], TG - 0.5, None, ALU.is_lt))
                step(v.tensor_tensor(sc[:, :, :].rearrange("p n (g e) -> p n g e", g=G),
                                     sc[:, :, :].rearrange("p n (g e) -> p n g e", g=G),
                                     bc(cnt[:, 1, :, :], 3, E // G), ALU.mult))
                for n in range(TILES):
                    last = v.max(top[:, n, :], sc[:, n, :])
                step(last)
                kth = bc(top[:, :, K - 1], 2, E)
                step(v.tensor_tensor(gt[:, :, :], sc[:, :, :], kth, ALU.is_gt))
                step(v.tensor_tensor(eq[:, :, :], sc[:, :, :], kth, ALU.is_equal))
                step(v.reduce_sum(left[:, 0, :], gt[:, :, :], AX.X))
                step(v.tensor_scalar(left[:, 0, :], left[:, 0, :], -1.0, K + 0.5, ALU.mult, ALU.add))
                for n in range(TILES):
                    last = v.tensor_tensor_scan(cum[:, n, :], one[:, :], eq[:, n, :], 0.0, ALU.mult, ALU.add)
                step(last)
                step(v.tensor_tensor(cum[:, :, :], cum[:, :, :], bc(left[:, 0, :], 2, E), ALU.is_lt))
                step(v.tensor_tensor(eq[:, :, :], eq[:, :, :], cum[:, :, :], ALU.mult))
                step(v.tensor_tensor(gt[:, :, :], gt[:, :, :], eq[:, :, :], ALU.add))
                step(v.tensor_tensor(gt[:, :, :], gt[:, :, :], sc[:, :, :], ALU.mult))
                step(v.reduce_sum(left[:, 1, :], gt[:, :, :], AX.X))
                step(v.tensor_scalar_add(left[:, 1, :], left[:, 1, :], 1e-8))
                step(v.reciprocal(left[:, 1, :], left[:, 1, :]))
                v.tensor_tensor(cum[:, :, :], gt[:, :, :], bc(left[:, 1, :], 2, E), ALU.mult).then_inc(comb, 1)


def phase_experts0(k, combT, res):
    nc = k.nc
    ITEMS, NC = 33, 4
    C = TILES * P // NC
    with ExitStack() as ctx:
        wt = [k.sb(ctx, f"e0_w{s}", [P, 3, P]) for s in range(2)]
        cb = [k.sb(ctx, f"e0_c{s}", [P, TILES * P]) for s in range(2)]
        sg = [k.sb(ctx, f"e0_s{s}", [P, C]) for s in range(2)]
        ht = [k.sb(ctx, f"e0_h{s}", [P, C]) for s in range(2)]
        pg = k.ps(ctx, "e0_pg", [P, C])
        pu = k.ps(ctx, "e0_pu", [P, C])
        acc = k.ps(ctx, "e0_acc", [P, NC, C])
        w_in, c_in = ([k.sem(f"e0_{n}{s}") for s in range(2)] for n in ("w_in", "c_in"))
        g_done, u_done, d_done, silu, h_done, scaled, out = (
            k.sem(f"e0_{n}") for n in ("g", "u", "down", "silu", "h", "scaled", "out"))
        zeroed, zero_read = k.sem("e0_zeroed"), k.sem("e0_zero_read")

        with nc.Block() as block:

            @block.sync
            def _(sp):
                def item(i, s, n):
                    sp.wait_ge(d_done, (i - 1) * NC + 1)
                    sp.dma_start(wt[s][:, :, :], k.ins["moe0"][bass.ds(i, 1)].squeeze(0)).then_inc(w_in[s], 16)
                    for e in range(2):
                        row = combT[bass.ds(i * 2 - 2 + e, 1), :].broadcast_to([64, TILES * P])
                        sp.dma_start(cb[s][64 * e:64 * e + 64, :], row).then_inc(c_in[s], 16)

                sp.dma_start(wt[0][:, :, :], k.ins["moe0"][0]).then_inc(w_in[0], 16)
                with sp.Fori(0, (ITEMS - 3) // 2) as l:
                    item(l * 2 + 1, 1, l + 1)
                    item(l * 2 + 2, 0, l + 2)
                item(ITEMS - 2, 1, ITEMS // 2)
                item(ITEMS - 1, 0, ITEMS // 2 + 1)

            @block.tensor
            def _(pe):
                mm = nc.tensor.matmul
                pe.sem_inc(d_done, 1)

                def down(i, s, j, start, stop):
                    pe.wait_ge(h_done, i * NC + j + 1)
                    mm(acc[:, j, :], wt[s][:, 2, :], ht[j % 2][:, :], start=start, stop=stop,
                       skip_group_check=True).then_inc(d_done, 1)

                def item(i, s, n, first=False, last=False):
                    pe.wait_ge(w_in[s], n * 16)
                    for j in range(NC):
                        cs = slice(j * C, (j + 1) * C)
                        if not (first and j == 0):
                            pe.wait_ge(silu, i * NC + j)
                        mm(pg[:, :], wt[s][:, 0, :], k.hT[:, cs], start=True, stop=True).then_inc(g_done, 1)
                        if not (first and j == 0):
                            pe.wait_ge(h_done, i * NC + j)
                        mm(pu[:, :], wt[s][:, 1, :], k.hT[:, cs], start=True, stop=True).then_inc(u_done, 1)
                        if j:
                            down(i, s, j - 1, first, last)
                        elif not first:
                            down(i - 1, 1 - s, NC - 1, False, False)
                    if last:
                        down(i, s, NC - 1, False, True)

                pe.wait_ge(zeroed, 1)
                for j in range(NC):
                    mm(acc[:, j, :], k.identf[:, :], sg[1][:, :], start=True, stop=False, skip_group_check=True)\
                        .then_inc(zero_read, 1)
                item(0, 0, 1, first=True)
                with pe.Fori(0, (ITEMS - 3) // 2) as l:
                    item(l * 2 + 1, 1, l + 1)
                    item(l * 2 + 2, 0, l + 2)
                item(ITEMS - 2, 1, ITEMS // 2)
                item(ITEMS - 1, 0, ITEMS // 2 + 1, last=True)

            @block.scalar
            def _(act):
                def item(i, s, n, first=False):
                    for j in range(NC):
                        act.wait_ge(g_done, i * NC + j + 1)
                        if not (first and j < 2):
                            act.wait_ge(h_done, i * NC + j - 1)
                        if first and j == 1:
                            act.wait_ge(zero_read, NC)
                        nc.scalar.activation(sg[j % 2][:, :], pg[:, :], ACT.Silu).then_inc(silu, 1)
                item(0, 0, 1, first=True)
                with act.Fori(0, (ITEMS - 3) // 2) as l:
                    item(l * 2 + 1, 1, l + 1)
                    item(l * 2 + 2, 0, l + 2)
                item(ITEMS - 2, 1, ITEMS // 2)
                item(ITEMS - 1, 0, ITEMS // 2 + 1)
                act.wait_ge(d_done, ITEMS * NC + 1)
                nc.scalar.activation(res[:, :], acc[:, :, :].rearrange("p a b -> p (a b)"), ACT.Copy)

            @block.vector
            def _(dve):
                v = nc.vector
                v.memset(sg[1][:, :], 0.0).then_inc(zeroed, 1)

                def item(i, s, n, first=False):
                    for j in range(NC):
                        cs = slice(j * C, (j + 1) * C)
                        dve.wait_ge(silu, i * NC + j + 1)
                        if first:
                            left = sg[j % 2][:, :]
                        else:
                            if j == 0:
                                dve.wait_ge(c_in[s], (n + s - 1) * 32)
                            v.tensor_tensor(cb[s][:, cs], cb[s][:, cs], sg[j % 2][:, :], ALU.mult).then_inc(scaled, 1)
                            dve.wait_ge(scaled, (i - 1) * NC + j + 1)
                            left = cb[s][:, cs]
                        dve.wait_ge(u_done, i * NC + j + 1)
                        if not (first and j < 2):
                            dve.wait_ge(d_done, i * NC + j)
                        v.tensor_tensor(ht[j % 2][:, :], left, pu[:, :], ALU.mult).then_inc(h_done, 1)
                item(0, 0, 1, first=True)
                with dve.Fori(0, (ITEMS - 3) // 2) as l:
                    item(l * 2 + 1, 1, l + 1)
                    item(l * 2 + 2, 0, l + 2)
                item(ITEMS - 2, 1, ITEMS // 2)
                item(ITEMS - 1, 0, ITEMS // 2 + 1)


def phase_back(k, name, res, gate):
    nc = k.nc
    with ExitStack() as ctx:
        xg = k.sb(ctx, f"{name}_xg", [P, TILES, D])
        pt = k.ps(ctx, f"{name}_pb", [P, TILES, D])
        turned, chain = k.sem(f"{name}_turned"), k.sem(f"{name}_chain")
        with nc.Block() as block:

            @block.tensor
            def _(pe):
                for n in range(TILES):
                    last = nc.tensor.transpose(pt[:, n, :], res[:, n * P:(n + 1) * P], k.identf[:, :])
                    if n % 4 == 3:
                        last.then_inc(turned, 1)

            @block.vector
            def _(dve):
                step = Chain(dve, chain)
                for i in range(4):
                    ns = slice(4 * i, 4 * i + 4)
                    dve.wait_ge(turned, i + 1)
                    g = bc(k.gates[:, gate, 2 * i:2 * i + 2, :], 2, TPB)
                    step(nc.vector.tensor_tensor(xg[:, ns, :].rearrange("p (b t) d -> p b t d", t=TPB),
                                                 pt[:, ns, :].rearrange("p (b t) d -> p b t d", t=TPB), g, ALU.mult))
                    step(nc.vector.tensor_tensor(k.x[:, ns, :], k.x[:, ns, :], xg[:, ns, :], ALU.add))


def phase_l1_attention(k):
    nc = k.nc
    DH = 8
    EPS = 1e-6
    with ExitStack() as ctx:
        wqo = k.sb(ctx, "a1_wqo", [P, 2, D])
        wkv = k.sb(ctx, "a1_wkv", [P, 2, D])
        bq = k.sb(ctx, "a1_bq", [P, 1])
        rows = k.sb(ctx, "a1_rows", [P, 3, D])
        mask = k.sb(ctx, "a1_mask", [P, D // DH, DH])
        qT = k.sb(ctx, "a1_qT", [P, TILES * P])
        qe = k.sb(ctx, "a1_qe", [P, TILES * P])
        kv = k.sb(ctx, "a1_kv", [P, TILES, 2, D])
        ke = k.sb(ctx, "a1_ke", [P, TILES, D])
        kvm = k.sb(ctx, "a1_kvm", [P, B, 2, D])
        oT = k.sb(ctx, "a1_oT", [P, TILES * P])
        rc = k.sb(ctx, "a1_rc", [P, TILES * P])
        xg = k.sb(ctx, "a1_xg", [P, TILES, D])
        pa = k.ps(ctx, "a1_pa", [P, 4, 512])
        pb = k.ps(ctx, "a1_pb", [P, 4, 512])
        names = ("loaded", "q_done", "q_clip", "q_exp", "q_read", "kv_done", "kv_read", "k_clip", "k_exp", "kv_ready",
                 "sums", "sums_read", "outs", "outs_read", "proj", "chain", "made", "q_ready")
        sem = {n: k.sem(f"a1_{n}") for n in names}
        with nc.Block() as block:

            @block.sync
            def _(sp):
                sp.dma_start(wqo[:, :, :], k.ins["a1_wqo"]).then_inc(sem["loaded"], 16)
                sp.dma_start(wkv[:, :, :], k.ins["a1_wkv"]).then_inc(sem["loaded"], 16)
                sp.dma_start(bq[:, :], k.ins["a1_bq"]).then_inc(sem["loaded"], 16)
                sp.dma_start(rows[:, :, :], k.ins["a1_rows"].partition_broadcast(P)).then_inc(sem["loaded"], 16)

            @block.gpsimd
            def _(pool):
                nc.gpsimd.affine_select(out=mask[:, :, :], in_=k.ones[:, :].rearrange("p (a b) -> p a b", b=DH),
                                        compare_op=ALU.is_ge, fill=0.0, base=0, pattern=[[-DH, D // DH], [0, DH]],
                                        channel_multiplier=1).then_inc(sem["made"], 1)
                pool.wait_ge(sem["made"], 1)
                nc.gpsimd.affine_select(out=mask[:, :, :], in_=mask[:, :, :],
                                        compare_op=ALU.is_ge, fill=0.0, base=DH - 1,
                                        pattern=[[DH, D // DH], [0, DH]],
                                        channel_multiplier=-1).then_inc(sem["made"], 1)

            @block.tensor
            def _(pe):
                mm = nc.tensor.matmul
                pe.wait_ge(sem["loaded"], 64)
                for j in range(4):
                    mm(pa[:, j, :], wqo[:, 0, :], k.hT[:, j * 512:(j + 1) * 512], start=True, stop=True)\
                        .then_inc(sem["q_done"], 1)
                for j in range(8):
                    if j >= 4:
                        pe.wait_ge(sem["kv_read"], j - 3)
                    for n in (2 * j, 2 * j + 1):
                        last = mm(pb[:, j % 4, (n % 2) * 256:(n % 2 + 1) * 256], k.hT[:, n * P:(n + 1) * P],
                                  wkv[:, :, :].rearrange("p a d -> p (a d)"), start=True, stop=True)
                    last.then_inc(sem["kv_done"], 1)
                pe.wait_ge(sem["kv_ready"], 1)
                pe.wait_ge(sem["q_ready"], 1)
                for b in range(B):
                    for t in range(TPB):
                        n = b * TPB + t
                        mm(pa[:, b // 2, (b % 2) * 256:(b % 2) * 256 + D], kv[:, n, 0, :], kv[:, n, 1, :],
                           start=(t == 0), stop=(t == TPB - 1))
                    for t in range(TPB):
                        n = b * TPB + t
                        last = mm(pa[:, b // 2, (b % 2) * 256 + D:(b % 2) * 256 + 2 * D], kv[:, n, 0, :], k.ones[:, :],
                                  start=(t == 0), stop=(t == TPB - 1))
                    last.then_inc(sem["sums"], 1)
                for j in range(4):
                    pe.wait_ge(sem["sums_read"], 4)
                    if j:
                        pe.wait_ge(sem["outs_read"], j)
                    for b in (2 * j, 2 * j + 1):
                        bs = slice(b * T, (b + 1) * T)
                        for i in range(2):
                            last = mm(pb[:, 2 * (j % 2) + i, (b % 2) * T:(b % 2 + 1) * T], kvm[:, b, i, :], qT[:, bs],
                                      start=True, stop=True)
                    last.then_inc(sem["outs"], 1)
                pe.wait_ge(sem["outs_read"], 4)
                for n in range(TILES):
                    last = mm(pa[:, n // 4, (n % 4) * D:(n % 4 + 1) * D], oT[:, n * P:(n + 1) * P], wqo[:, 1, :],
                              start=True, stop=True)
                    if n % 4 == 3:
                        last.then_inc(sem["proj"], 1)

            @block.scalar
            def _(act):
                act.wait_ge(sem["q_clip"], 1)
                nc.scalar.activation(qe[:, :], qe[:, :], ACT.Exp).then_inc(sem["q_exp"], 1)
                act.wait_ge(sem["k_clip"], 1)
                nc.scalar.activation(ke[:, :, :], ke[:, :, :], ACT.Exp).then_inc(sem["k_exp"], 1)

            @block.vector
            def _(dve):
                v = nc.vector
                step = Chain(dve, sem["chain"])
                dve.wait_ge(sem["loaded"], 64)
                dve.wait_ge(sem["q_done"], 4)
                step(v.tensor_scalar(qT[:, :], pa[:, :, :].rearrange("p a b -> p (a b)"), bq[:, 0:1], None, ALU.add))
                v.tensor_scalar_min(qe[:, :], qT[:, :], 0.0).then_inc(sem["q_clip"], 1)
                for j in range(8):
                    dve.wait_ge(sem["kv_done"], j + 1)
                    v.tensor_tensor(kv[:, 2 * j:2 * j + 2, :, :], pb[:, j % 4, :].rearrange("p (n a d) -> p n a d", n=2, a=2),
                                    bc(rows[:, 0:2, :], 1, 2), ALU.add).then_inc(sem["kv_read"], 1)
                dve.wait_ge(sem["kv_read"], 8)
                v.tensor_scalar_min(ke[:, :, :], kv[:, :, 0, :], 0.0).then_inc(sem["k_clip"], 1)
                dve.wait_ge(sem["q_exp"], 1)
                v.scalar_tensor_tensor(qT[:, :], qT[:, :], 0.0, qe[:, :], ALU.max, ALU.add).then_inc(sem["q_ready"], 1)
                dve.wait_ge(sem["k_exp"], 1)
                v.scalar_tensor_tensor(kv[:, :, 0, :], kv[:, :, 0, :], 0.0, ke[:, :, :], ALU.max, ALU.add)\
                    .then_inc(sem["kv_ready"], 1)
                dve.wait_ge(sem["made"], 2)
                m = mask[:, :, :].rearrange("p a b -> p (a b)")
                for j in range(4):
                    dve.wait_ge(sem["sums"], 2 * j + 2)
                    v.tensor_tensor(kvm[:, 2 * j:2 * j + 2, :, :], pa[:, j, :].rearrange("p (b a d) -> p b a d", b=2, a=2),
                                    bc(bc(m, 1, 2), 1, 2), ALU.mult).then_inc(sem["sums_read"], 1)
                for j in range(4):
                    cs = slice(j * 512, (j + 1) * 512)
                    dve.wait_ge(sem["outs"], j + 1)
                    step(v.tensor_scalar_max(rc[:, cs], pb[:, 2 * (j % 2) + 1, :], EPS))
                    step(v.reciprocal(rc[:, cs], rc[:, cs]))
                    v.tensor_tensor(oT[:, cs], pb[:, 2 * (j % 2), :], rc[:, cs], ALU.mult).then_inc(sem["outs_read"], 1)
                for i in range(4):
                    ns = slice(4 * i, 4 * i + 4)
                    dve.wait_ge(sem["proj"], i + 1)
                    step(v.tensor_tensor(xg[:, ns, :], pa[:, i, :].rearrange("p (n d) -> p n d", d=D),
                                         bc(rows[:, 2, :], 1, 4), ALU.add))
                    g = bc(k.gates[:, 0, 2 * i:2 * i + 2, :], 2, TPB)
                    x4 = xg[:, ns, :].rearrange("p (b t) d -> p b t d", t=TPB)
                    step(v.tensor_tensor(x4, x4, g, ALU.mult))
                    step(v.tensor_tensor(k.x[:, ns, :], k.x[:, ns, :], xg[:, ns, :], ALU.add))


def phase_route1(k, gatesT, slotsT, gts, xt, slots):
    nc = k.nc
    E = 16
    CAP = B * T // E
    GONE = -3.0e38
    with ExitStack() as ctx:
        rw = k.sb(ctx, "r1_rw", [P, E])
        rb = k.sb(ctx, "r1_rb", [P, E])
        nw = k.sb(ctx, "r1_nw", [P, 1])
        sq = k.sb(ctx, "r1_sq", [P, TILES * P])
        ms = k.sb(ctx, "r1_ms", [P, TILES * P])
        lg = k.sb(ctx, "r1_lg", [P, TILES, E])
        pr = k.sb(ctx, "r1_pr", [P, TILES, E])
        gn = k.sb(ctx, "r1_gn", [P, TILES, E])
        st = k.sb(ctx, "r1_st", [P, 4, TILES])
        lt = k.sb(ctx, "r1_lt", [E, TILES * P])
        top = k.sb(ctx, "r1_top", [E, 8])
        ch = k.sb(ctx, "r1_ch", [P, TILES, E])
        off = k.sb(ctx, "r1_off", [P, TILES, E])
        sl = k.sb(ctx, "r1_sl", [P, TILES, E])
        slr = k.sb(ctx, "r1_slr", [E, TILES * P], BF16)
        ps = k.ps(ctx, "r1_ps", [P, TILES * P])
        pl = k.ps(ctx, "r1_pl", [P, TILES, E])
        names = ("loaded", "squared", "means", "var", "log", "normed", "logits", "biased", "turned", "chosen",
                 "back", "gated", "gturned", "copied", "kept", "chain", "shifted", "expd",
                 "ps_free", "xturned", "xcopied", "picked", "counted", "slotted", "sturned", "scopied")
        sem = {n: k.sem(f"r1_{n}") for n in names}
        with nc.Block() as block:

            @block.sync
            def _(sp):
                sp.dma_start(rw[:, :], k.ins["router_w"]).then_inc(sem["loaded"], 16)
                sp.dma_start(rb[:, :], k.ins["router_b"].partition_broadcast(P)).then_inc(sem["loaded"], 16)
                sp.dma_start(nw[:, :], k.ins["norm_w"]).then_inc(sem["loaded"], 16)
                sp.wait_ge(sem["copied"], 1)
                sp.dma_start(gatesT, gts[:, :]).then_inc(sem["kept"], 16)
                sp.wait_ge(sem["scopied"], 1)
                sp.dma_start(slotsT, slr[:, :]).then_inc(sem["kept"], 16)
                sp.wait_ge(sem["kept"], 32)

            @block.scalar
            def _(act):
                nc.scalar.activation(sq[:, :], k.hT[:, :], ACT.Square).then_inc(sem["squared"], 1)
                act.wait_ge(sem["var"], 1)
                nc.scalar.activation(sq[:, :], ms[:, :], ACT.Ln).then_inc(sem["log"], 1)
                act.wait_ge(sem["log"], 1)
                nc.scalar.activation(sq[:, :], sq[:, :], ACT.Exp, scale=-0.5).then_inc(sem["log"], 1)
                act.wait_ge(sem["shifted"], 1)
                nc.scalar.activation(pr[:, :, :], pr[:, :, :], ACT.Exp).then_inc(sem["expd"], 1)
                for j in range(4):
                    act.wait_ge(sem["xturned"], j + 1)
                    nc.scalar.activation(xt[:, 4 * j:4 * j + 4, :].rearrange("p n d -> p (n d)"),
                                         ps[:, j * 512:(j + 1) * 512], ACT.Copy).then_inc(sem["xcopied"], 1)

            @block.tensor
            def _(pe):
                pe.wait_ge(sem["squared"], 1)
                for j in range(4):
                    last = nc.tensor.matmul(ps[:, j * 512:(j + 1) * 512], k.ones[:, :], sq[:, j * 512:(j + 1) * 512],
                                            start=True, stop=True)
                last.then_inc(sem["means"], 1)
                pe.wait_ge(sem["loaded"], 48)
                pe.wait_ge(sem["normed"], 1)
                for n in range(TILES):
                    last = nc.tensor.matmul(pl[:, n, :], k.hT[:, n * P:(n + 1) * P], rw[:, :], start=True, stop=True)
                last.then_inc(sem["logits"], 1)
                pe.wait_ge(sem["biased"], 1)
                for n in range(TILES):
                    last = nc.tensor.transpose(ps[0:E, n * P:(n + 1) * P], lg[:, n, :], k.identf[:, :])
                last.then_inc(sem["turned"], 1)
                pe.wait_ge(sem["ps_free"], 1)
                for n in range(TILES):
                    last = nc.tensor.transpose(ps[:, n * P:(n + 1) * P], k.hT[:, n * P:(n + 1) * P], k.identf[:, :])
                    if n % 4 == 3:
                        last.then_inc(sem["xturned"], 1)
                pe.wait_ge(sem["chosen"], 1)
                for n in range(TILES):
                    last = nc.tensor.transpose(pl[:, n, :], lt[:, n * P:(n + 1) * P], k.identf[0:E, 0:E])
                last.then_inc(sem["back"], 1)
                pe.wait_ge(sem["picked"], 1)
                pe.wait_ge(sem["xcopied"], 4)
                picks = ch[:, :, :].rearrange("p n e -> p (n e)")
                nc.tensor.matmul(ps[:, 0:TILES * E], k.upto[:, :], picks, start=True, stop=True)
                nc.tensor.matmul(ps[:, 512:512 + TILES * E], k.ones[:, :], picks, start=True, stop=True)\
                    .then_inc(sem["counted"], 1)
                pe.wait_ge(sem["slotted"], 1)
                pe.wait_ge(sem["gated"], 1)
                for n in range(TILES):
                    last = nc.tensor.transpose(ps[0:E, n * P:(n + 1) * P], gn[:, n, :], k.identf[:, :])
                last.then_inc(sem["gturned"], 1)
                pe.wait_ge(sem["copied"], 1)
                for n in range(TILES):
                    last = nc.tensor.transpose(ps[0:E, n * P:(n + 1) * P], sl[:, n, :], k.identf[:, :])
                last.then_inc(sem["sturned"], 1)

            @block.vector
            def _(dve):
                v = nc.vector
                step = Chain(dve, sem["chain"])
                dve.wait_ge(sem["means"], 1)
                v.tensor_scalar(ms[:, :], ps[:, :], 1.0 / D, 1e-5, ALU.mult, ALU.add).then_inc(sem["var"], 1)
                dve.wait_ge(sem["log"], 2)
                step(v.tensor_tensor(ms[:, :], ms[:, :], sq[:, :], ALU.mult))
                step(v.tensor_tensor(ms[:, :], ms[:, :], sq[:, :], ALU.mult))
                step(v.tensor_scalar(ms[:, :], ms[:, :], -0.5, 1.5, ALU.mult, ALU.add))
                step(v.tensor_tensor(ms[:, :], ms[:, :], sq[:, :], ALU.mult))
                dve.wait_ge(sem["loaded"], 48)
                v.scalar_tensor_tensor(k.hT[:, :], k.hT[:, :], nw[:, 0:1], ms[:, :], ALU.mult, ALU.mult)\
                    .then_inc(sem["normed"], 1)
                dve.wait_ge(sem["logits"], 1)
                v.tensor_tensor(lg[:, :, :], pl[:, :, :], bc(rb[:, :], 1, TILES), ALU.add).then_inc(sem["biased"], 1)
                dve.wait_ge(sem["biased"], 1)
                step(v.tensor_reduce(st[:, 0, :], lg[:, :, :], AX.X, ALU.max))
                v.tensor_tensor(pr[:, :, :], lg[:, :, :], bc(st[:, 0, :], 2, E), ALU.subtract).then_inc(sem["shifted"], 1)
                dve.wait_ge(sem["turned"], 1)
                v.tensor_copy(lt[:, :], ps[0:E, :]).then_inc(sem["ps_free"], 1)
                dve.wait_ge(sem["ps_free"], 1)
                for _ in range(CAP // 8):
                    step(v.max(top[:, :], lt[:, :]))
                    step(v.match_replace(lt[:, :], top[:, :], lt[:, :], GONE))
                v.tensor_scalar(lt[:, :], lt[:, :], GONE, None, ALU.is_equal).then_inc(sem["chosen"], 1)
                dve.wait_ge(sem["expd"], 1)
                step(v.reduce_sum(st[:, 1, :], pr[:, :, :], AX.X))
                step(v.reciprocal(st[:, 1, :], st[:, 1, :]))
                step(v.tensor_tensor(pr[:, :, :], pr[:, :, :], bc(st[:, 1, :], 2, E), ALU.mult))
                dve.wait_ge(sem["back"], 1)
                v.tensor_copy(ch[:, :, :], pl[:, :, :]).then_inc(sem["picked"], 1)
                step(v.tensor_tensor(gn[:, :, :], pr[:, :, :], pl[:, :, :], ALU.mult))
                step(v.reduce_sum(st[:, 2, :], gn[:, :, :], AX.X))
                step(v.tensor_scalar(st[:, 3, :], st[:, 2, :], 0.0, None, ALU.is_equal))
                step(v.tensor_tensor(st[:, 2, :], st[:, 2, :], st[:, 3, :], ALU.add))
                step(v.reciprocal(st[:, 2, :], st[:, 2, :]))
                v.tensor_tensor(gn[:, :, :], gn[:, :, :], bc(st[:, 2, :], 2, E), ALU.mult).then_inc(sem["gated"], 1)
                dve.wait_ge(sem["counted"], 1)
                tot = ps[:, 512:512 + TILES * E].rearrange("p (n e) -> p n e", e=E)
                step(v.memset(off[:, 0, :], 0.0))
                for n in range(1, TILES):
                    step(v.tensor_tensor(off[:, n, :], off[:, n - 1, :], tot[:, n - 1, :], ALU.add))
                step(v.tensor_tensor(off[:, :, :], off[:, :, :], ps[:, 0:TILES * E].rearrange("p (n e) -> p n e", e=E),
                                     ALU.add))
                step(v.tensor_tensor(off[:, :, :], off[:, :, :], ch[:, :, :], ALU.mult))
                v.tensor_scalar_add(sl[:, :, :], off[:, :, :], -1.0).then_inc(sem["slotted"], 1)
                dve.wait_ge(sem["slotted"], 1)
                step(v.tensor_copy(slots[:, :, :], sl[:, :, :].rearrange("p n e -> p e n")))
                dve.wait_ge(sem["gturned"], 1)
                v.tensor_copy(gts[:, :], ps[0:E, :]).then_inc(sem["copied"], 1)
                dve.wait_ge(sem["sturned"], 1)
                v.tensor_copy(slr[:, :], ps[0:E, :]).then_inc(sem["scopied"], 1)


def phase_experts1(k, gatesT, slotsT, gts, xt, slots, res):
    nc = k.nc
    E, F, NC = 16, 512, 4
    FT = F // P
    C = TILES * P // NC
    with ExitStack() as ctx:
        w1 = [k.sb(ctx, f"e1_w1{s}", [P, FT, P]) for s in range(2)]
        w2 = [k.sb(ctx, f"e1_w2{s}", [P, FT, P]) for s in range(2)]
        gr = [k.sb(ctx, f"e1_gr{s}", [P, TILES * P]) for s in range(2)]
        sr = [k.sb(ctx, f"e1_sr{s}", [P, TILES * P], BF16) for s in range(2)]
        hot = [k.sb(ctx, f"e1_hot{s}", [P, TILES, P]) for s in range(2)]
        back = [k.sb(ctx, f"e1_back{s}", [P, TILES * P]) for s in range(2)]
        b1 = k.sb(ctx, "e1_b1", [P, E, FT])
        b1s = [k.sb(ctx, f"e1_b1s{s}", [P, FT]) for s in range(2)]
        b2 = k.sb(ctx, "e1_b2", [E, D])
        xe = [k.sb(ctx, f"e1_xe{s}", [P, P]) for s in range(2)]
        he = [k.sb(ctx, f"e1_he{s}", [P, FT, P]) for s in range(2)]
        ye = [k.sb(ctx, f"e1_ye{s}", [P, D]) for s in range(2)]
        count = k.sb(ctx, "e1_count", [P, P])
        line = k.sb(ctx, "e1_line", [P, 1])
        px = k.ps(ctx, "e1_px", [P, 512])
        ph = k.ps(ctx, "e1_ph", [P, FT, P])
        py = k.ps(ctx, "e1_py", [P, 512])
        acc = k.ps(ctx, "e1_acc", [P, NC, C])
        w_in = [k.sem(f"e1_w_in{s}") for s in range(2)]
        loaded, counts, staged, hot_done, back_done, gathered, xe_done, up_done, gelu, down_done, y_done, added = (
            k.sem(f"e1_{n}") for n in ("loaded", "counts", "staged", "hot", "back_rows", "gathered", "xe", "up",
                                       "gelu", "down", "y", "added"))
        with nc.Block() as block:

            @block.sync
            def _(sp):
                def expert(e, s):
                    sp.dma_start(w1[s][:, :, :], k.ins["fc1"][bass.ds(e, 1)].squeeze(0)).then_inc(w_in[s], 16)
                    sp.dma_start(w2[s][:, :, :], k.ins["fc2"][bass.ds(e, 1)].squeeze(0)).then_inc(w_in[s], 16)
                    sp.dma_start(gr[s][:, :], gatesT[bass.ds(e, 1), :].broadcast_to([P, TILES * P])).then_inc(w_in[s], 16)
                    sp.dma_start(sr[s][:, :], slotsT[bass.ds(e, 1), :].broadcast_to([P, TILES * P])).then_inc(w_in[s], 16)

                sp.dma_start(b1[:, :, :], k.ins["b1"]).then_inc(loaded, 16)
                sp.dma_start(b2[:, :], k.ins["b2"]).then_inc(loaded, 16)
                for e in range(2):
                    expert(e, e)
                with sp.Fori(0, E // 2 - 1) as l:
                    for s in range(2):
                        sp.wait_ge(down_done, l * 2 + (s + 2))
                        sp.wait_ge(back_done, l * 2 + (s + 2))
                        expert(l * 2 + (s + 2), s)

            @block.gpsimd
            def _(pool):
                nc.gpsimd.iota(count[:, :], pattern=[[1, P]], base=0, channel_multiplier=0,
                               allow_small_or_imprecise_dtypes=True).then_inc(counts, 1)
                nc.gpsimd.iota(line[:, :], pattern=[[0, 1]], base=0, channel_multiplier=1,
                               allow_small_or_imprecise_dtypes=True).then_inc(counts, 1)

            @block.tensor
            def _(pe):
                mm = nc.tensor.matmul
                for sm in (gathered, up_done, down_done, added):
                    pe.sem_inc(sm, 1)
                pe.wait_ge(loaded, 32)
                for j in range(NC):
                    mm(acc[:, j, :], b2[:, :], gts[:, j * C:(j + 1) * C], start=True, stop=False,
                       skip_group_check=True)

                def gather(e, s):
                    pe.wait_ge(hot_done, e + 1)
                    if not isinstance(e, int) or e:
                        pe.wait_ge(xe_done, e)
                    for n in range(TILES):
                        last = mm(px[:, 0:P], xt[:, n, :], hot[s][:, n, :], start=(n == 0), stop=(n == TILES - 1))
                    last.then_inc(gathered, 1)

                def add(e, s, stop=False):
                    pe.wait_ge(y_done, e + 1)
                    pe.wait_ge(back_done, e + 2)
                    for j in range(NC):
                        last = mm(acc[:, j, :], ye[s][:, :], back[s][:, j * C:(j + 1) * C], start=False, stop=stop,
                                  skip_group_check=True)
                    last.then_inc(added, 1)

                def expert(e, s, n, first=False, last=False):
                    pe.wait_ge(w_in[s], n * 64)
                    pe.wait_ge(xe_done, e + 1)
                    if not first:
                        pe.wait_ge(gelu, e)
                    for f in range(FT):
                        up = mm(ph[:, f, :], w1[s][:, f, :], xe[s][:, :], start=True, stop=True)
                    up.then_inc(up_done, 1)
                    if not last:
                        gather(e + 1, 1 - s)
                    pe.wait_ge(gelu, e + 1)
                    if not first:
                        pe.wait_ge(y_done, e)
                    for f in range(FT):
                        down = mm(py[:, 0:D], he[s][:, f, :], w2[s][:, f, :], start=(f == 0), stop=(f == FT - 1))
                    down.then_inc(down_done, 1)
                    if not first:
                        add(e - 1, 1 - s)

                gather(0, 0)
                expert(0, 0, 1, first=True)
                with pe.Fori(0, E // 2 - 1) as l:
                    expert(l * 2 + 1, 1, l + 1)
                    expert(l * 2 + 2, 0, l + 2)
                expert(E - 1, 1, E // 2, last=True)
                add(E - 1, 1, stop=True)

            @block.scalar
            def _(act):
                act.wait_ge(loaded, 32)

                def take(e, s):
                    act.wait_ge(gathered, e + 2)
                    if not isinstance(e, int) or e:
                        act.wait_ge(up_done, e)
                    nc.scalar.activation(xe[s][:, :], px[:, 0:P], ACT.Copy).then_inc(xe_done, 1)

                def expert(e, s, last=False):
                    nc.scalar.activation(b1s[s][:, :], b1[:, bass.ds(e, 1), :].squeeze(1), ACT.Copy).then_inc(staged, 1)
                    act.wait_ge(staged, e + 1)
                    act.wait_ge(up_done, e + 2)
                    if not isinstance(e, int) or e:
                        act.wait_ge(down_done, e)
                    for f in range(FT):
                        g = nc.scalar.activation(he[s][:, f, :], ph[:, f, :], ACT.Gelu, bias=b1s[s][:, f:f + 1])
                    g.then_inc(gelu, 1)
                    if not last:
                        take(e + 1, 1 - s)

                take(0, 0)
                expert(0, 0)
                with act.Fori(0, E // 2 - 1) as l:
                    expert(l * 2 + 1, 1)
                    expert(l * 2 + 2, 0)
                expert(E - 1, 1, last=True)
                act.wait_ge(added, E + 1)
                nc.scalar.activation(res[:, :], acc[:, :, :].rearrange("p a b -> p (a b)"), ACT.Copy)

            @block.vector
            def _(dve):
                v = nc.vector
                dve.wait_ge(counts, 2)
                dve.sem_inc(back_done, 1)

                def one_hot(e, s):
                    if not isinstance(e, int) or e:
                        dve.wait_ge(gathered, e)
                    v.tensor_tensor(hot[s][:, :, :], bc(slots[:, bass.ds(e, 1), :].squeeze(1), 2, P),
                                    bc(count[:, :], 1, TILES), ALU.is_equal).then_inc(hot_done, 1)

                def expert(e, s, n, last=False):
                    if not last:
                        one_hot(e + 1, 1 - s)
                    dve.wait_ge(w_in[s], n * 64)
                    if not isinstance(e, int) or e:
                        dve.wait_ge(added, e)
                    v.scalar_tensor_tensor(back[s][:, :], sr[s][:, :], line[:, 0:1], gr[s][:, :],
                                           ALU.is_equal, ALU.mult).then_inc(back_done, 1)
                    dve.wait_ge(down_done, e + 2)
                    v.tensor_copy(ye[s][:, :], py[:, 0:D]).then_inc(y_done, 1)

                one_hot(0, 0)
                expert(0, 0, 1)
                with dve.Fori(0, E // 2 - 1) as l:
                    expert(l * 2 + 1, 1, l + 1)
                    expert(l * 2 + 2, 0, l + 2)
                expert(E - 1, 1, E // 2, last=True)


def phase_store(k):
    nc = k.nc
    stored = k.sem("stored")
    with nc.Block() as block:

        @block.sync
        def _(sp):
            sp.dma_start(k.out.rearrange("(n p) d -> p n d", p=P), k.x[:, :, :]).then_inc(stored, 16)
            sp.wait_ge(stored, 16)


def layouts(i):
    c = np.ascontiguousarray
    o = {}
    o["x"] = c(i["L0_attn_hidden_states"].reshape(B * T, D))
    for n in (0, 1):
        o[f"cT{n}"] = c(i[f"L{n}_c"].T)
        o[f"wmod{n}"] = c(i[f"L{n}_wmod"])
    heads = lambda w: w.reshape(D, HP, 2 * DK)
    swap = lambda w: c(w.reshape(D, H, 2, HD)[:, :, ::-1, :]).reshape(D, HP, 2 * DK)
    wq, wk = i["L0_attn_Wq"], i["L0_attn_Wk"]
    o["w5"] = c(np.stack([heads(wq), heads(wk), swap(wq), swap(wk), heads(i["L0_attn_Wg"])], 2))
    o["wv"] = c(i["L0_attn_Wv"])
    o["wbt"] = c(np.concatenate([i["L0_attn_Wbeta"], i["L0_attn_Wtg"]], 1))
    o["log_decay"] = c(i["L0_attn_log_decay"].reshape(-1))
    o["mode_logits"] = c(i["L0_attn_mode_logits"])
    o["omega"] = c(i["L0_attn_omega_log_scale"])
    pair = np.arange(0, DK, 2, dtype=np.float32)
    inv = (np.float32(1.0) / np.float32(10000.0) ** (pair / np.float32(DK))).astype(np.float32)
    f = np.arange(P)
    o["freq"] = c(np.stack([inv[f % HD], np.where(f % DK < HD, 1.0, -1.0)], 1).astype(np.float32))
    o["wo0"] = c(i["L0_attn_Wo"].reshape(HP, P, D).transpose(1, 0, 2))
    eg, eu, ed = i["L0_ffn_eg_w"], i["L0_ffn_eu_w"], i["L0_ffn_ed_w"]
    up = lambda w: w.reshape(32, P, D).transpose(0, 2, 1)
    down = ed.transpose(0, 2, 1).reshape(32, P, D)
    moe = np.stack([up(eg), up(eu), down], 2)
    shared = np.stack([i["L0_ffn_sg_w"].T, i["L0_ffn_su_w"].T, i["L0_ffn_sd_w"].T], 1)
    o["moe0"] = c(np.concatenate([shared[None], moe], 0))
    o["gate_w"] = c(i["L0_ffn_gate_w"].T)
    o["gate_bias"] = c(i["L0_ffn_gate_bias"])
    o["a1_wqo"] = c(np.stack([i["L1_attn_Wq"], i["L1_attn_Wo"]], 1))
    o["a1_wkv"] = c(np.stack([i["L1_attn_Wk"], i["L1_attn_Wv"]], 1))
    o["a1_bq"] = c(i["L1_attn_bq"].reshape(P, 1))
    o["a1_rows"] = c(np.stack([i["L1_attn_bk"], i["L1_attn_bv"], i["L1_attn_bo"]], 0))
    o["router_w"] = c(i["L1_ffn_router_weight"].T)
    o["router_b"] = c(i["L1_ffn_router_bias"])
    o["norm_w"] = c(i["L1_ffn_norm_weight"].reshape(P, 1))
    o["fc1"] = c(i["L1_ffn_fc1_weight"].reshape(16, 4, P, D).transpose(0, 3, 1, 2))
    o["fc2"] = c(i["L1_ffn_fc2_weight"].reshape(16, D, 4, P).transpose(0, 3, 2, 1))
    o["b1"] = c(i["L1_ffn_fc1_bias"].reshape(16, 4, P).transpose(2, 0, 1))
    o["b2"] = c(i["L1_ffn_fc2_bias"])
    return o


def kernel(**inputs):
    from concourse import bacc
    from concourse.bass_utils import run_bass_kernel_spmd

    nc = bacc.Bacc("TRN2", target_bir_lowering=False, num_devices=1)
    arrays = layouts({n: np.asarray(a) for n, a in inputs.items()})
    ins = {n: nc.dram_tensor(f"in_{n}", a.shape, F32, kind="ExternalInput").ap() for n, a in arrays.items()}
    out = nc.dram_tensor("out", (B * T, D), F32, kind="ExternalOutput").ap()
    program(nc, ins, out)
    r = run_bass_kernel_spmd(nc, [{f"in_{n}": a for n, a in arrays.items()}], core_ids=[0])
    return r.results[0]["out"].reshape(B, T, D)
```

```python
import numpy as np
from contextlib import ExitStack, contextmanager

import concourse.bass as bass
from concourse import mybir

F32 = mybir.dt.float32
BF16 = mybir.dt.bfloat16
I32 = mybir.dt.int32
ALU = mybir.AluOpType
ACT = mybir.ActivationFunctionType
AX = mybir.AxisListType

P = 128
D = 128
B, T = 8, 256
TILES = B * T // P
TPB = T // P
H, M, DK, DV = 8, 8, 64, 64
HP = H // 2
HD = DK // 2
CB = 32
NB = P // CB
PW = 6
MASKED = -30000.0
ROUND = 12582912.0


def bc(ap, at, n):
    shape = list(ap.shape)
    shape.insert(at, n)
    return ap.unsqueeze(at).broadcast_to(shape)


def stand(engine):
    engine.nop(nofuse=True)


class Chain:

    def __init__(self, engine, sem):
        self.engine, self.sem, self.n = engine, sem, 0

    def __call__(self, ins):
        self.n += 1
        ins.then_inc(self.sem, 1)
        self.engine.wait_ge(self.sem, self.n)


class Kernel:

    def __init__(self, nc, ctx, ins, out):
        self.nc, self.ctx, self.ins, self.out = nc, ctx, ins, out
        self.sems = []
        sb = self.sb
        self.x = sb(ctx, "x_res", [P, TILES, D])
        self.hT = sb(ctx, "hT", [P, TILES * P])
        self.modT = sb(ctx, "modT", [P, 6, B])
        self.gates = sb(ctx, "gates", [P, 2, B, D])
        self.identf = sb(ctx, "identf", [P, P])
        self.identb = sb(ctx, "identb", [P, P], BF16)
        self.after = sb(ctx, "after", [P, P])
        self.upto = sb(ctx, "upto", [P, P])
        self.maskb = sb(ctx, "maskb", [P, P], BF16)
        self.halves = sb(ctx, "halves", [P, P])
        self.ones = sb(ctx, "ones", [P, P])
        self.identc = sb(ctx, "identc", [P, CB])
        self.parity = sb(ctx, "parity", [P, 2])

    def sb(self, ctx, name, shape, dt=F32):
        return ctx.enter_context(self.nc.sbuf_tensor(name, shape, dt))

    def ps(self, ctx, name, shape, dt=F32):
        return ctx.enter_context(self.nc.psum_tensor(name, shape, dt))

    def sem(self, name):
        self.sems.append(self.nc.alloc_semaphore(name=name))
        return self.sems[-1]

    @contextmanager
    def scope(self):
        before = len(self.sems)
        yield
        self.nc.clear_and_free_semaphores(self.sems[before:])
        del self.sems[before:]
        self.nc.all_engine_barrier()


def phase_constants(k):
    nc = k.nc
    loaded, made = k.sem("x_loaded"), k.sem("const_chain")
    with nc.Block() as block:

        @block.sync
        def _(sp):
            sp.dma_start(k.x[:, :, :], k.ins["x"].rearrange("(n p) d -> p n d", p=P)).then_inc(loaded, 16)
            sp.wait_ge(loaded, 16)

        @block.gpsimd
        def _(pool):
            step = Chain(pool, made)
            step(nc.gpsimd.memset(k.ones[:, :], 1.0))
            step(nc.gpsimd.memset(k.halves[:, :], 0.0))
            step(nc.gpsimd.memset(k.maskb[:, :], MASKED))
            step(nc.gpsimd.memset(k.parity[:, :], 0.0))
            for q in range(NB):
                step(nc.gpsimd.memset(k.parity[CB * q:CB * q + CB, q % 2:q % 2 + 1], 1.0))
            for h in (0, 64):
                step(nc.gpsimd.memset(k.halves[h:h + 64, h:h + 64], 1.0))
            sel = nc.gpsimd.affine_select
            step(sel(out=k.identf[:, :], in_=k.ones[:, :], compare_op=ALU.is_equal, fill=0.0, base=0,
                     pattern=[[1, P]], channel_multiplier=-1))
            step(sel(out=k.identb[:, :], in_=k.ones[:, :], compare_op=ALU.is_equal, fill=0.0, base=0,
                     pattern=[[1, P]], channel_multiplier=-1))
            for q in range(NB):
                rs = slice(CB * q, CB * q + CB)
                step(sel(out=k.identc[rs, :], in_=k.ones[rs, 0:CB], compare_op=ALU.is_equal, fill=0.0, base=0,
                         pattern=[[1, CB]], channel_multiplier=-1))
            step(sel(out=k.after[:, :], in_=k.ones[:, :], compare_op=ALU.is_gt, fill=0.0, base=0,
                     pattern=[[-1, P]], channel_multiplier=1))
            step(sel(out=k.upto[:, :], in_=k.ones[:, :], compare_op=ALU.is_ge, fill=0.0, base=0,
                     pattern=[[1, P]], channel_multiplier=-1))
            step(sel(out=k.maskb[:, :], in_=k.maskb[:, :], compare_op=ALU.is_gt, fill=0.0, base=0,
                     pattern=[[-1, P]], channel_multiplier=1))


def phase_modulation(k, layer):
    nc = k.nc
    with ExitStack() as ctx:
        wmod = k.sb(ctx, f"wmod{layer}", [P, 6 * D])
        scT = k.sb(ctx, f"scT{layer}", [P, B])
        scB = k.sb(ctx, f"scB{layer}", [P, B, P])
        sign = k.sb(ctx, f"sign{layer}", [P, 2, B, D])
        pT = k.ps(ctx, f"pmodT{layer}", [P, 6, B])
        pG = k.ps(ctx, f"pgate{layer}", [P, 2, B, D])
        loaded, act_done, rows_done = (k.sem(f"mod{layer}_{n}") for n in ("loaded", "silu", "rows"))
        pe_done, dve_chain = k.sem(f"mod{layer}_pe"), k.sem(f"mod{layer}_chain")
        with nc.Block() as block:

            @block.sync
            def _(sp):
                sp.dma_start(scT[:, :], k.ins[f"cT{layer}"]).then_inc(loaded, 16)
                sp.dma_start(wmod[:, :], k.ins[f"wmod{layer}"]).then_inc(loaded, 16)

            @block.scalar
            def _(act):
                act.wait_ge(loaded, 32)
                nc.scalar.activation(scT[:, :], scT[:, :], ACT.Silu).then_inc(act_done, 1)

            @block.tensor
            def _(pe):
                pe.wait_ge(act_done, 1)
                for j in range(6):
                    nc.tensor.matmul(pT[:, j, :], wmod[:, j * D:(j + 1) * D], scT[:, :], start=True, stop=True)
                pe.wait_ge(rows_done, 1)
                for i, j in enumerate((2, 5)):
                    for b in range(B):
                        last = nc.tensor.matmul(pG[:, i, b, :], scB[:, b, :], wmod[:, j * D:(j + 1) * D],
                                                start=True, stop=True)
                last.then_inc(pe_done, 1)

            @block.vector
            def _(dve):
                step = Chain(dve, dve_chain)
                dve.wait_ge(act_done, 1)
                nc.vector.tensor_copy(scB[:, :, :], bc(scT[:, :], 2, P)).then_inc(rows_done, 1)
                dve.wait_ge(pe_done, 1)
                step(nc.vector.tensor_copy(k.modT[:, :, :], pT[:, :, :]))
                for j in (1, 4):
                    step(nc.vector.tensor_scalar_add(k.modT[:, j, :], k.modT[:, j, :], 1.0))
                step(nc.vector.tensor_scalar(sign[:, :, :, :], pG[:, :, :, :], 0.0, 2.0, ALU.is_ge, ALU.mult))
                step(nc.vector.tensor_copy(k.gates[:, :, :, :], pG[:, :, :, :]))
                step(nc.vector.scalar_tensor_tensor(k.gates[:, :, :, :], k.gates[:, :, :, :], -1.0,
                                                    k.gates[:, :, :, :], ALU.mult, ALU.max))
                step(nc.vector.tensor_scalar_max(k.gates[:, :, :, :], k.gates[:, :, :, :], 0.25))
                step(nc.vector.scalar_tensor_tensor(k.gates[:, :, :, :], sign[:, :, :, :], -1.0,
                                                    k.gates[:, :, :, :], ALU.add, ALU.mult))


def phase_norm(k, name, shift, scale):
    nc = k.nc
    with ExitStack() as ctx:
        xc = k.sb(ctx, f"{name}_xc", [P, TILES, D])
        sq = k.sb(ctx, f"{name}_sq", [P, TILES, D])
        st = k.sb(ctx, f"{name}_st", [P, 5, TILES])
        pt = k.ps(ctx, f"{name}_pt", [P, TILES * P])
        centred, squared, var_done, log_done, normed, turned = (
            k.sem(f"{name}_{n}") for n in ("centred", "squared", "var", "log", "normed", "turned"))
        chain = k.sem(f"{name}_chain")
        with nc.Block() as block:

            @block.vector
            def _(dve):
                step = Chain(dve, chain)
                step(nc.vector.reduce_sum(st[:, 0, :], k.x[:, :, :], AX.X))
                step(nc.vector.tensor_scalar_mul(st[:, 0, :], st[:, 0, :], 1.0 / D))
                nc.vector.tensor_tensor(xc[:, :, :], k.x[:, :, :], bc(st[:, 0, :], 2, D), ALU.subtract)\
                    .then_inc(centred, 1)
                dve.wait_ge(squared, 1)
                step(nc.vector.reduce_sum(st[:, 1, :], sq[:, :, :], AX.X))
                nc.vector.tensor_scalar(st[:, 1, :], st[:, 1, :], 1.0 / D, 1e-5, ALU.mult, ALU.add)\
                    .then_inc(var_done, 1)
                dve.wait_ge(log_done, 2)
                step(nc.vector.tensor_tensor(st[:, 3, :], st[:, 2, :], st[:, 2, :], ALU.mult))
                step(nc.vector.tensor_tensor(st[:, 3, :], st[:, 3, :], st[:, 1, :], ALU.mult))
                step(nc.vector.tensor_scalar(st[:, 3, :], st[:, 3, :], -0.5, 1.5, ALU.mult, ALU.add))
                step(nc.vector.tensor_tensor(st[:, 4, :], st[:, 2, :], st[:, 3, :], ALU.mult))
                nc.vector.tensor_tensor(xc[:, :, :], xc[:, :, :], bc(st[:, 4, :], 2, D), ALU.mult)\
                    .then_inc(normed, 1)

            @block.scalar
            def _(act):
                act.wait_ge(centred, 1)
                nc.scalar.activation(sq[:, :, :], xc[:, :, :], ACT.Square).then_inc(squared, 1)
                act.wait_ge(var_done, 1)
                nc.scalar.activation(st[:, 2, :], st[:, 1, :], ACT.Ln).then_inc(log_done, 1)
                act.wait_ge(log_done, 1)
                nc.scalar.activation(st[:, 2, :], st[:, 2, :], ACT.Exp, scale=-0.5).then_inc(log_done, 1)
                for b in range(B):
                    act.wait_ge(turned, b // 2 + 1)
                    s = slice(b * T, (b + 1) * T)
                    nc.scalar.activation(k.hT[:, s], pt[:, s], ACT.Identity, bias=k.modT[:, shift, b:b + 1],
                                         scale=k.modT[:, scale, b:b + 1])

            @block.tensor
            def _(pe):
                pe.wait_ge(normed, 1)
                for n in range(TILES):
                    last = nc.tensor.transpose(pt[:, n * P:(n + 1) * P], xc[:, n, :], k.identf[:, :])
                    if n % 4 == 3:
                        last.then_inc(turned, 1)


def phase_l0_tokens(k, a):
    nc = k.nc
    HM = H * M
    with ExitStack() as ctx:
        wbt = k.sb(ctx, "wbt", [P, 2 * HM])
        ld = k.sb(ctx, "ld", [P, HM])
        ml = k.sb(ctx, "ml", [P, H, M])
        mst = k.sb(ctx, "mst", [P, 3, H])
        bt = k.sb(ctx, "bt", [P, TILES, 2 * HM])
        gg = k.sb(ctx, "gg", [P, TPB, B, HM])
        dec = k.sb(ctx, "dec", [P, B, HM])
        pv = k.ps(ctx, "pv", [P, 512])
        pb = k.ps(ctx, "pb", [P, TILES, 2 * HM])
        loaded = k.sem("tok_loaded")
        b_done = k.sem("tok_b")
        chain, act_done, g_done = k.sem("tok_chain"), k.sem("tok_act"), k.sem("tok_g")
        suffix_done, dve_asks = k.sem("tok_suffix"), k.sem("tok_dve")
        with nc.Block() as block:

            @block.sync
            def _(sp):
                sp.dma_start(wbt[:, :], k.ins["wbt"]).then_inc(loaded, 16)
                sp.dma_start(ld[:, :], k.ins["log_decay"].partition_broadcast(P)).then_inc(loaded, 16)
                sp.dma_start(ml[:, :, :], k.ins["mode_logits"].partition_broadcast(P)).then_inc(loaded, 16)

            @block.tensor
            def _(pe):
                pe.wait_ge(loaded, 48)
                for n in range(TILES):
                    last = nc.tensor.matmul(pb[:, n, :], k.hT[:, n * P:(n + 1) * P], wbt[:, :], start=True, stop=True)
                last.then_inc(b_done, 1)
                pe.wait_ge(g_done, 1)
                nc.tensor.matmul(pv[:, :], k.after[:, :], gg[:, 0, :, :].rearrange("p b h -> p (b h)"),
                                 start=True, stop=True).then_inc(suffix_done, 1)

            @block.scalar
            def _(act):
                act.wait_ge(dve_asks, 1)
                nc.scalar.activation(bt[:, :, :], bt[:, :, :], ACT.Exp).then_inc(act_done, 1)
                act.wait_ge(dve_asks, 2)
                nc.scalar.activation(ml[:, :, :], ml[:, :, :], ACT.Exp).then_inc(act_done, 1)
                nc.scalar.activation(ld[:, :], ld[:, :], ACT.Exp).then_inc(act_done, 1)
                act.wait_ge(dve_asks, 3)
                nc.scalar.activation(gg[:, :, :, :], gg[:, :, :, :], ACT.Ln).then_inc(g_done, 1)
                act.wait_ge(suffix_done, 1)
                nc.scalar.activation(dec[:, :, :].rearrange("p b h -> p (b h)"), pv[:, :], ACT.Exp)\
                    .then_inc(act_done, 1)

            @block.vector
            def _(dve):
                step = Chain(dve, chain)
                dve.wait_ge(b_done, 1)
                nc.vector.tensor_scalar(bt[:, :, :], pb[:, :, :], -1.0, 80.0, ALU.mult, ALU.min)\
                    .then_inc(dve_asks, 1)
                dve.wait_ge(loaded, 48)
                step(nc.vector.tensor_reduce(mst[:, 0, :], ml[:, :, :], AX.X, ALU.max))
                step(nc.vector.tensor_tensor(ml[:, :, :], ml[:, :, :], bc(mst[:, 0, :], 2, M), ALU.subtract))
                nc.vector.tensor_scalar_min(ld[:, :], ld[:, :], 80.0).then_inc(dve_asks, 1)
                dve.wait_ge(act_done, 3)
                step(nc.vector.reduce_sum(mst[:, 1, :], ml[:, :, :], AX.X))
                step(nc.vector.reciprocal(mst[:, 2, :], mst[:, 1, :]))
                step(nc.vector.tensor_scalar_mul(mst[:, 2, :], mst[:, 2, :], float(DK) ** -0.5))
                step(nc.vector.tensor_tensor(a.wmode[:, :, :].rearrange("p a (g m) -> p (a g) m", g=2), ml[:, :, :],
                                             bc(mst[:, 2, :], 2, M), ALU.mult))
                step(nc.vector.tensor_scalar_add(ld[:, :], ld[:, :], 1.0))
                step(nc.vector.reciprocal(ld[:, :], ld[:, :]))
                step(nc.vector.tensor_scalar_add(bt[:, :, :], bt[:, :, :], 1.0))
                step(nc.vector.reciprocal(bt[:, :, :], bt[:, :, :]))
                tg = bt[:, :, HM:2 * HM].rearrange("p (b t) h -> p t b h", t=TPB)
                for t in range(TPB):
                    step(nc.vector.tensor_tensor(gg[:, t, :, :], tg[:, t, :, :], bc(ld[:, :], 1, B), ALU.mult))
                nc.vector.tensor_scalar_max(gg[:, :, :, :], gg[:, :, :, :], 1e-6).then_inc(dve_asks, 1)
                beta = bt[:, :, 0:HM].rearrange("p (b t) (a c) -> p b t a c", t=TPB, a=HP)
                dve.wait_ge(g_done, 1)
                for t in range(TPB):
                    for hp in range(HP):
                        s = slice(16 * hp, 16 * hp + 16)
                        dst = a.scal[:, :, hp, :, t, :]
                        step(nc.vector.tensor_copy(dst[:, :, 0, :], gg[:, t, :, s]))
                        step(nc.vector.tensor_scalar_mul(dst[:, :, 1, :], beta[:, :, t, hp, :], -1.0))
                        step(nc.vector.tensor_copy(dst[:, :, 2, :], beta[:, :, t, hp, :]))
                dve.wait_ge(act_done, 4)
                for hp in range(HP):
                    s = slice(16 * hp, 16 * hp + 16)
                    for t in range(TPB):
                        step(nc.vector.tensor_tensor(a.scal[:, :, hp, 3, t, :], beta[:, :, 0, hp, :],
                                                     dec[:, :, s], ALU.mult))


PI_PARTS = (6.25, 17.0 / 512, -37.0 / 2 ** 21)
PI_PARTS += (float(2 * np.pi - sum(PI_PARTS)),)
TURN_STEPS = 13


def reduce_angles(v, step, angle, cosine, turns, freq):
    step(v.tensor_scalar_mul(angle, angle, freq[:, 0:1]))
    step(v.tensor_scalar(turns, angle, float(1 / (2 * np.pi)), ROUND, ALU.mult, ALU.add))
    step(v.tensor_scalar_add(turns, turns, -ROUND))
    for q in PI_PARTS:
        step(v.scalar_tensor_tensor(angle, turns, -q, angle, ALU.mult, ALU.add))
    step(v.tensor_scalar(angle, angle, 3.1415925, -3.1415925, ALU.min, ALU.max))
    step(v.scalar_tensor_tensor(cosine, angle, -1.0, angle, ALU.mult, ALU.max))
    step(v.tensor_scalar(cosine, cosine, -1.0, float(np.pi / 2), ALU.mult, ALU.add))
    step(v.tensor_scalar_mul(angle, angle, freq[:, 1:2]))


def phase_l0_angles(k, a):
    nc = k.nc
    LN2_HI = 0.693359375
    LN2_LO = float(np.log(2.0) - LN2_HI)
    with ExitStack() as ctx:
        om = k.sb(ctx, "om", [P, 3, HP, M])
        two = k.sb(ctx, "two", [P, HP, M], I32)
        turns = k.sb(ctx, "turns", [P, M, T])
        loaded, posn = k.sem("ang_loaded"), k.sem("ang_pos")
        chain, ready = k.sem("ang_chain"), k.sem("ang_ready")
        with nc.Block() as block:

            @block.sync
            def _(sp):
                sp.dma_start(a.freq[:, :], k.ins["freq"]).then_inc(loaded, 16)
                for g in range(2):
                    sp.dma_start(om[64 * g:64 * g + 64, 0, :, :],
                                 k.ins["omega"][g:g + 1, :, :].broadcast_to([64, HP, M])).then_inc(loaded, 16)

            @block.gpsimd
            def _(pool):
                nc.gpsimd.iota(a.pos[:, :], pattern=[[1, T]], base=0, channel_multiplier=0,
                               allow_small_or_imprecise_dtypes=True).then_inc(posn, 1)

            @block.vector
            def _(dve):
                v = nc.vector
                step = Chain(dve, chain)
                dve.wait_ge(loaded, 48)
                w, n, r, p = om[:, 0, :, :], om[:, 1, :, :], om[:, 2, :, :], a.omega[:, :, :]
                step(v.tensor_scalar(n, w, 1.4426950408889634, ROUND, ALU.mult, ALU.add))
                step(v.tensor_scalar_add(n, n, -ROUND))
                step(v.scalar_tensor_tensor(r, n, -LN2_HI, w, ALU.mult, ALU.add))
                step(v.scalar_tensor_tensor(r, n, -LN2_LO, r, ALU.mult, ALU.add))
                step(v.tensor_scalar(p, r, 1.0 / 40320, 1.0 / 5040, ALU.mult, ALU.add))
                for c in (1 / 720, 1 / 120, 1 / 24, 1 / 6, 0.5, 1.0, 1.0):
                    step(v.tensor_tensor(p, p, r, ALU.mult))
                    step(v.tensor_scalar_add(p, p, float(c)))
                step(v.tensor_scalar(two[:, :, :], n, 127.0, 8388608.0, ALU.add, ALU.mult))
                step(v.tensor_tensor(p, p, two[:, :, :].bitcast(F32), ALU.mult))
                dve.wait_ge(posn, 1)
                s, c = a.sin[0][:, :, :], a.cos[0][:, :, :]
                step(v.tensor_tensor(s, bc(a.pos[:, :], 1, M), bc(a.omega[:, 0, :], 2, T), ALU.mult))
                reduce_angles(v, step, s, c, turns[:, :, :], a.freq)
                dve.sem_inc(ready, 1)

            @block.scalar
            def _(act):
                act.wait_ge(ready, 1)
                nc.scalar.activation(a.sin[0][:, :, :], a.sin[0][:, :, :], ACT.Sin)
                nc.scalar.activation(a.cos[0][:, :, :], a.cos[0][:, :, :], ACT.Sin)


class L0Attention:

    def __init__(self, k, ctx):
        sb = k.sb
        self.scal = sb(ctx, "scal", [P, B, HP, 4, TPB, 16])
        self.wmode = sb(ctx, "wmode", [P, HP, 16])
        self.sin = [sb(ctx, f"sin{i}", [P, M, T]) for i in range(2)]
        self.cos = [sb(ctx, f"cos{i}", [P, M, T]) for i in range(2)]
        self.omega = sb(ctx, "omega", [P, HP, M])
        self.freq = sb(ctx, "freq", [P, 2])
        self.pos = sb(ctx, "pos", [P, T])


def phase_l0_pairs(k, a):
    nc = k.nc
    with ExitStack() as ctx:
        def sb(name, shape, dt=F32):
            return k.sb(ctx, f"pair_{name}", shape, dt)

        hb = sb("hb", [P, T])
        ld = sb("ld", [P, TPB, 16])
        sc = sb("sc", [P, 3, TPB, 16])
        sq = sb("sq", [P, 2, T])
        rn = sb("rn", [P, 2, T])
        xn = sb("xn", [P, 2, 2, T])
        vv = sb("vv", [P, TPB, P])
        gx = sb("gx", [P, T])
        gt = sb("gt", [P, T])
        xr = [sb(f"xr{t}", [P, M, 2, P]) for t in range(TPB)]
        tmp = sb("tmp", [P, M, 2, P])
        gl = [sb(f"gl{g}", [P, M, P]) for g in range(2)]
        e = [sb(f"e{g}", [P, M, P]) for g in range(2)]
        nt = [sb(f"nt{n}", [P, M, P]) for n in range(2)]
        pm = [sb(f"pm{n}", [P, M, P]) for n in range(2)]
        ntd = [sb(f"ntd{g}", [P, M, CB]) for g in range(2)]
        ny = [sb(f"ny{g}", [P, M, 3, CB]) for g in range(2)]
        nkt = [sb(f"nkt{g}", [P, M, 2, CB]) for g in range(2)]
        zt = [sb(f"zt{g}", [P, M, CB]) for g in range(2)]
        r = [sb(f"r{g}", [P, M, DV]) for g in range(2)]
        w = [sb(f"w{g}", [P, M, DV]) for g in range(2)]
        ub = [sb(f"ub{g}", [P, M, DV]) for g in range(2)]
        ua = [sb(f"ua{g}", [P, M, DV]) for g in range(2)]
        og = sb("og", [P, T])
        xg = sb("xg", [P, TPB, D])
        w5 = [sb(f"w5_{i}", [P, PW, P]) for i in range(2)]
        wo = sb("wo", [P, HP, D])
        angle = sb("angle", [P, T])
        cosine = sb("cosine", [P, T])
        turns = sb("turns1", [P, T])
        om = sb("om1", [P, 1])
        kn = sb("kn", [P, M, P])
        st = sb("st", [P, M, DV])
        pe2 = k.ps(ctx, "pE", [P, 2, 512])
        ps2 = k.ps(ctx, "pS", [P, 2, 2, 2, P])
        px = [k.ps(ctx, f"pX{g}", [P, 512]) for g in range(2)]
        pk = k.ps(ctx, "pK", [P, 512])
        po = k.ps(ctx, "pO", [P, 512])
        wide = [u[:, :, :].rearrange("p m (s c) -> p m s c", s=2) for u in ua]
        pxl = [x[:, :].rearrange("p (m s c) -> p m s c", m=M, s=2) for x in px]
        pxw = [x[:, :].rearrange("p (m v) -> p m v", m=M) for x in px]

        sems = {}

        def S(name):
            if name not in sems:
                sems[name] = k.sem(name)
            return sems[name]

        with nc.Block() as block:

            @block.sync
            def _(sp):
                for hp in range(HP):
                    if hp >= 2:
                        sp.wait_ge(S("gproj"), (hp - 1) * B)
                    sp.dma_start(w5[hp % 2][:, :, :], k.ins["w5"][:, hp, :, :]).then_inc(S(f"weights{hp % 2}"), 16)
                    if hp == 0:
                        sp.dma_start(wo[:, :, :], k.ins["wo0"]).then_inc(S("wo_loaded"), 16)

            @block.tensor
            def _(pe):
                mm = nc.tensor.matmul

                def project(nx, hp, it=None):
                    if isinstance(nx, int):
                        pe.wait_ge(S(f"weights{hp % 2}"), 16 * (hp // 2 + 1))
                    pe.wait_ge(S("staged_h"), nx + 1)
                    if it is not None:
                        pe.wait_ge(S("e_done"), it * 5 + 5)
                        pe.wait_ge(S("state"), it + 1)
                    for j in range(4):
                        last = mm(pe2[:, j // 2, (j % 2) * T:(j % 2 + 1) * T], w5[hp % 2][:, j, :], hb[:, :],
                                  start=True, stop=True)
                    last.then_inc(S("proj"), 1)
                    mm(pk[:, 0:T], w5[hp % 2][:, 4, :], hb[:, :], start=True, stop=True)
                    for t in range(TPB):
                        last = mm(pk[:, T + t * P:T + (t + 1) * P], hb[:, t * P:(t + 1) * P], w5[hp % 2][:, 5, :],
                                  start=True, stop=True)
                    last.then_inc(S("gproj"), 1)

                def norm_sums(nx, it=None):
                    pe.wait_ge(S("squares"), nx + 1)
                    if it is not None:
                        pe.wait_ge(S("pair_out"), it * 16 + 16)
                    mm(ps2[:, 0, :, :, :].rearrange("p a b t -> p (a b t)"), k.halves[:, :],
                       sq[:, :, :].rearrange("p a t -> p (a t)"), start=True, stop=True).then_inc(S("norms"), 1)

                def exponents(it, n):
                    pe.wait_ge(S("gl_done"), it * 4 + n + 1)
                    if n == 0:
                        pe.wait_ge(S("xn_done"), it + 1)
                    else:
                        pe.wait_ge(S("e_done"), it * 5 + n)
                    for i in range(2):
                        mm(pe2[:, i, :], k.after[:, :],
                           gl[n % 2][:, 4 * i:4 * i + 4, :].rearrange("p m t -> p (m t)"), start=True, stop=False)
                        last = mm(pe2[:, i, :], k.identb[:, :], bc(k.maskb[:, :], 1, 4), start=False, stop=True)
                    last.then_inc(S("expo"), 1)

                def products(it, n, j):
                    t, g = n // 2, n % 2
                    hs, kk = slice(64 * g, 64 * g + 64), n * 4 + j
                    if kk % 8 == 0:
                        pe.wait_ge(S("xr_done"), it * 2 + t + 1)
                    if kk >= 2:
                        pe.wait_ge(S("pair_out"), it * 16 + kk - 1)
                    elif not isinstance(it, int) or it:
                        pe.wait_ge(S("pair_out"), it * 16)
                    for m in (2 * j, 2 * j + 1):
                        last = mm(ps2[:, j % 2, m % 2, :, :].rearrange("p a t -> p (a t)"), xr[t][hs, m, 1, :],
                                  xr[t][hs, m, :, :].rearrange("p a t -> p (a t)"), start=True, stop=True)
                    last.then_inc(S("pair"), 1)

                def turn_keys(it, i):
                    if i:
                        pe.wait_ge(S("kn_done"), it * 2 + 1)
                    else:
                        pe.wait_ge(S("gate_read"), it + 1)
                        pe.wait_ge(S("v_read"), it + 1)
                        pe.wait_ge(S("end_dve"), it + 1)
                    for m in range(4 * i, 4 * i + 4):
                        last = nc.tensor.transpose(pk[:, (m % 4) * P:(m % 4 + 1) * P], xr[0][:, m, 1, :],
                                                   k.identf[:, :])
                    last.then_inc(S("kturn"), 1)

                def batch(b, hp, nhp):
                    it = b + hp * B
                    for t in range(TPB):
                        for g in range(2):
                            n = 2 * t + g
                            hs = slice(64 * g, 64 * g + 64)
                            if n:
                                exponents(it, n)
                            for j in range(0 if n else 2, 4):
                                products(it, n, j)
                        if t == 1:
                            pe.wait_ge(S("e_done"), it * 5 + 4)
                            for g in range(2):
                                for i in range(2):
                                    last = mm(pe2[64 * g:64 * g + 64, i, :], k.ones[:, 0:64],
                                              gl[g][:, 4 * i:4 * i + 4, :].rearrange("p m t -> p (m t)"),
                                              start=True, stop=True)
                            last.then_inc(S("grow"), 1)
                        for lv in range(5):
                            for g in range(2):
                                n = 2 * t + g
                                pe.wait_ge(S(f"level{g}"), it * 12 + t * 6 + lv + 1)
                                if lv:
                                    pe.wait_ge(S(f"kept{g}"), it * 10 + t * 5 + lv)
                                else:
                                    pe.wait_ge(S(f"spread{g}"), it * 2 + t + 1)
                                stand(pe)
                                left = nkt[g] if lv else wide[g]
                                lo, hi = ((0, 1), (0, 2), (0, 2), (0, 2), (1, 2))[lv]
                                for m in range(M):
                                    for hs in (slice(0, 64), slice(64, P)):
                                        last = mm(pxl[g][hs, m, lo:hi, :], left[hs, m, :, :].rearrange("p s c -> p (s c)"),
                                                  ny[g][hs, m, lo:hi, :], start=True, stop=True)
                                last.then_inc(S(f"power{g}"), 1)
                            if t == 1 and nhp is not None and lv == 0:
                                project(it + 1, nhp, it)
                            if t == 1 and nhp is not None and lv == 1:
                                norm_sums(it + 1, it)
                        if t == 1:
                            pe.wait_ge(S("state"), it + 1)
                            pe.wait_ge(S("xscaled"), it + 1)
                            for g in range(2):
                                hs = slice(64 * g, 64 * g + 64)
                                pe.wait_ge(S(f"level{g}"), it * 12 + 12)
                                for m in range(M):
                                    last = mm(pxw[g][:, m, :], xr[1][hs, m, 1, :], st[hs, m, :], start=True, stop=True)
                                last.then_inc(S("from_state"), 1)
                        for c in range(NB):
                            rs = slice(CB * c, CB * c + CB)
                            if c:
                                for g in range(2):
                                    pe.wait_ge(S(f"w_out{g}"), it * 8 + t * 4 + c)
                                    stand(pe)
                                    for m in range(M):
                                        last = mm(pxw[g][rs, m, :], nt[g][0:CB * c, m, rs], w[g][0:CB * c, m, :],
                                                  start=True, stop=True)
                                    last.then_inc(S(f"carried{g}"), 1)
                            for g in range(2):
                                if c == 0:
                                    pe.wait_ge(S(f"level{g}"), it * 12 + t * 6 + 6)
                                pe.wait_ge(S(f"right{g}"), it * 8 + t * 4 + c + 1)
                                stand(pe)
                                for m in range(M):
                                    last = mm(pxw[g][rs, m, :], zt[g][rs, m, :], r[g][rs, m, :], start=True, stop=True)
                                last.then_inc(S(f"solved{g}"), 1)
                            if t == 0 and c < 2:
                                turn_keys(it, c)
                        for g in range(2):
                            n = 2 * t + g
                            hs = slice(64 * g, 64 * g + 64)
                            pe.wait_ge(S("u_done") if g else S("u_first"), it * 2 + t + 1)
                            for m in range(M):
                                last = mm(po[hs, t * P:(t + 1) * P], ub[g][:, m, :], pm[g][:, m, :],
                                          start=(m == 0), stop=(t == 0 and m == M - 1))
                            if t == 1:
                                for m in range(M):
                                    last = mm(po[hs, P:2 * P], st[hs, m, :], xr[1][hs, m, 0, :],
                                              start=False, stop=(m == M - 1))
                            last.then_inc(S("o_done"), 1)
                        if t == 0:
                            pe.wait_ge(S("kn_done"), it * 2 + 2)
                            for g in range(2):
                                hs = slice(64 * g, 64 * g + 64)
                                pe.wait_ge(S("ua_done"), it * 2 + g + 1)
                                for m in range(M):
                                    last = mm(pk[hs, m * DV:(m + 1) * DV], kn[:, m, hs], ua[g][:, m, :],
                                              start=True, stop=True)
                            last.then_inc(S("s_done"), 1)
                    if nhp is not None:
                        exponents(it + 1, 0)
                        for j in range(2):
                            products(it + 1, 0, j)
                    pe.wait_ge(S("og_done"), it + 1)
                    for t in range(TPB):
                        last = mm(pk[:, t * D:(t + 1) * D], og[:, t * P:(t + 1) * P], wo[:, hp, :],
                                  start=True, stop=True)
                    last.then_inc(S("out_done"), 1)

                project(0, 0)
                norm_sums(0)
                exponents(0, 0)
                for j in range(2):
                    products(0, 0, j)
                pe.wait_ge(S("wo_loaded"), 16)
                for hp in range(HP):
                    with pe.Fori(0, B - 1) as b:
                        batch(b, hp, hp)
                    batch(B - 1, hp, hp + 1 if hp + 1 < HP else None)

            @block.scalar
            def _(act):
                cp = nc.scalar.activation

                def stage_h(b, nx):
                    if not isinstance(nx, int) or nx:
                        act.wait_ge(S("gproj"), nx)
                    cp(hb[:, :], k.hT[:, bass.ds(b * T, T)], ACT.Copy).then_inc(S("staged_h"), 1)

                def squares(nx):
                    act.wait_ge(S("proj"), nx + 1)
                    cp(sq[:, :, :], pe2[:, 0, :].rearrange("p (a t) -> p a t", a=2), ACT.Square)\
                        .then_inc(S("squares"), 1)
                    act.wait_ge(S("gproj"), nx + 1)
                    if not isinstance(nx, int) or nx:
                        act.wait_ge(S("gate_one"), nx)
                    cp(gx[:, :], pk[:, 0:T], ACT.Exp, scale=-1.0).then_inc(S("gate_read"), 1)

                def stage_values(nx):
                    if not isinstance(nx, int) or nx:
                        act.wait_ge(S("r_done"), nx * 4)
                    cp(vv[:, :, :].rearrange("p t v -> p (t v)"), pk[:, T:2 * T], ACT.Copy).then_inc(S("v_read"), 1)

                def inverse_norms(nx):
                    act.wait_ge(S("norm_eps"), nx + 1)
                    cp(rn[:, :, :], rn[:, :, :], ACT.Ln).then_inc(S("rn_log"), 1)
                    act.wait_ge(S("rn_log"), nx + 1)
                    cp(rn[:, :, :], rn[:, :, :], ACT.Exp, scale=-0.5).then_inc(S("rn_done"), 1)

                def decays(it, n):
                    g = n % 2
                    act.wait_ge(S("expo"), it * 4 + n + 1)
                    if n >= 2:
                        act.wait_ge(S("pair_out"), it * 16 + 4 * (n - 1))
                    elif n == 0 and (not isinstance(it, int) or it):
                        act.wait_ge(S("pair_out"), it * 16)
                    cp(e[g][:, :, :].rearrange("p (a m) t -> p a (m t)", a=2), pe2[:, :, :], ACT.Exp)\
                        .then_inc(S("e_done"), 1)

                def spread(it, t, g):
                    act.wait_ge(S("ntd_done"), it * 16 + 4 * (2 * t + g) + 4)
                    for s in range(2):
                        last = cp(wide[g][:, :, s, :], ntd[g][:, :, :], ACT.Identity, scale=k.parity[:, s:s + 1])
                    last.then_inc(S(f"spread{g}"), 1)

                def batch(b, hp, nhp):
                    it = b + hp * B
                    for t in range(TPB):
                        for g in range(2):
                            n = 2 * t + g
                            if n == 2 and nhp is not None:
                                stage_h(b + 1 if nhp == hp else 0, it + 1)
                            if n:
                                decays(it, n)
                        if t == 1:
                            spread(it, t, 0)
                            act.wait_ge(S("grow"), it + 1)
                            act.wait_ge(S("xr_done"), it * 2 + 2)
                            cp(tmp[:, 0:4, :, :].rearrange("p a b t -> p (a b t)"),
                               pe2[:, :, :].rearrange("p a t -> p (a t)"), ACT.Exp).then_inc(S("e_done"), 1)

                        if t == 0:
                            spread(it, t, 0)
                        spread(it, t, 1)
                        for lv in range(5):
                            for g in range(2):
                                act.wait_ge(S(f"power{g}"), it * 10 + t * 5 + lv + 1)
                                if lv < 4:
                                    if lv:
                                        act.wait_ge(S(f"level{g}"), it * 12 + t * 6 + lv + 1)
                                    for s in range(2):
                                        last = cp(wide[g][:, :, s, :], pxl[g][:, :, 0, :], ACT.Identity,
                                                  scale=k.parity[:, s:s + 1])
                                    last.then_inc(S(f"wide{g}"), 1)
                                if lv == 0:
                                    cp(ny[g][:, :, 0, :], pxl[g][:, :, 0, :], ACT.Copy).then_inc(S(f"kept{g}"), 1)
                                elif lv < 4:
                                    cp(ny[g][:, :, 0:3:2, :], pxl[g][:, :, :, :], ACT.Copy).then_inc(S(f"kept{g}"), 1)
                                else:
                                    cp(ny[g][:, :, 2, :], pxl[g][:, :, 1, :], ACT.Copy).then_inc(S(f"kept{g}"), 1)
                            if t == 1 and nhp is not None and lv == 0:
                                squares(it + 1)
                            if t == 1 and lv == 4 and hp + 1 < HP:
                                act.wait_ge(S("angles"), it + 1)
                                cp(a.sin[(hp + 1) % 2][:, bass.ds(b, 1), :].squeeze(1), angle[:, :], ACT.Sin)
                                cp(a.cos[(hp + 1) % 2][:, bass.ds(b, 1), :].squeeze(1), cosine[:, :], ACT.Sin)\
                                    .then_inc(S("sines"), 1)
                            if t == 1 and nhp is not None and lv == 4:
                                inverse_norms(it + 1)
                            if t == 1 and nhp is not None and lv == 1:
                                stage_values(it + 1)
                        for c in range(NB):
                            rs = slice(CB * c, CB * c + CB)
                            for g in range(2):
                                act.wait_ge(S(f"solved{g}"), it * 8 + t * 4 + c + 1)
                                cp(w[g][rs, :, :], pxw[g][rs, :, :], ACT.Copy).then_inc(S(f"w_out{g}"), 1)
                            if t == 0 and c < 2:
                                act.wait_ge(S("kturn"), it * 2 + c + 1)
                                cp(kn[:, 4 * c:4 * c + 4, :].rearrange("p m c -> p (m c)"), pk[:, :], ACT.Copy)\
                                    .then_inc(S("kn_done"), 1)
                        if t == 0:
                            act.wait_ge(S("s_done"), it + 1)
                            cp(st[:, :, :].rearrange("p m v -> p (m v)"), pk[:, :], ACT.Copy).then_inc(S("state"), 1)
                    if nhp is not None:
                        decays(it + 1, 0)

                act.sem_inc(S("sines"), 1)
                stage_h(0, 0)
                squares(0)
                stage_values(0)
                inverse_norms(0)
                decays(0, 0)
                for hp in range(HP):
                    with act.Fori(0, B - 1) as b:
                        batch(b, hp, hp)
                    batch(B - 1, hp, hp + 1 if hp + 1 < HP else None)

            @block.vector
            def _(dve):
                v = nc.vector
                dve.sem_inc(S("end_dve"), 1)

                def stage_decays(b, nx, hp):
                    if not isinstance(nx, int) or nx:
                        dve.wait_ge(S("gl_done"), nx * 4)
                    v.tensor_copy(ld[:, :, :], a.scal[:, bass.ds(b, 1), hp, 0, :, :].squeeze(1)).then_inc(S("staged_d"), 1)

                def norms(nx):
                    dve.wait_ge(S("norms"), nx + 1)
                    v.tensor_scalar_add(rn[:, :, :].rearrange("p a t -> p (a t)"),
                                        ps2[:, 0, :, :, :].rearrange("p a b t -> p (a b t)"), 1e-6)\
                        .then_inc(S("norm_eps"), 1)

                def normed(nx):
                    dve.wait_ge(S("rn_done"), nx + 1)
                    dve.wait_ge(S("squares"), nx + 1)
                    if not isinstance(nx, int) or nx:
                        dve.wait_ge(S("tmp_done"), nx * 2)
                    v.tensor_tensor(xn[:, :, :, :].rearrange("p s a t -> p s (a t)"), pe2[:, :, :],
                                    bc(rn[:, :, :].rearrange("p a t -> p (a t)"), 1, 2), ALU.mult).then_inc(S("xn_done"), 1)

                def rotate_cos(nx, t, i, hp):
                    ts, ms = slice(t * P, (t + 1) * P), slice(4 * i, 4 * i + 4)
                    if i == 0:
                        dve.wait_ge(S("xn_done"), nx + 1)
                    v.tensor_tensor(xr[t][:, ms, :, :], bc(xn[:, 0, :, ts], 1, 4), bc(a.cos[hp % 2][:, ms, ts], 2, 2), ALU.mult)\
                        .then_inc(S("xr_part"), 1)

                def rotate_sin(nx, t, i):
                    ms = slice(4 * i, 4 * i + 4)
                    dve.wait_ge(S("xr_part"), nx * 4 + 2 * t + i + 1)
                    if i == 0:
                        dve.wait_ge(S("tmp_done"), nx * 2 + t + 1)
                    last = v.tensor_tensor(xr[t][:, ms, :, :], xr[t][:, ms, :, :], tmp[:, ms, :, :], ALU.add)
                    if i:
                        last.then_inc(S("xr_done"), 1)

                def stage_scalars(b, nx, hp):
                    v.tensor_copy(sc[:, :, :, :], a.scal[:, bass.ds(b, 1), hp, 1:4, :, :].squeeze(1)).then_inc(S("staged_s"), 1)
                    dve.wait_ge(S("staged_s"), nx + 1)

                def next_angles(b, it, hp):
                    done = [0]

                    def step(ins):
                        done[0] += 1
                        ins.then_inc(S("angle_step"), 1)
                        dve.wait_ge(S("angle_step"), it * TURN_STEPS + done[0])

                    dve.wait_ge(S("sines"), it + 1)
                    step(v.tensor_copy(om[:, :], a.omega[:, hp, bass.ds(b, 1)]))
                    step(v.tensor_scalar_mul(angle[:, :], a.pos[:, :], om[:, 0:1]))
                    reduce_angles(v, step, angle[:, :], cosine[:, :], turns[:, :], a.freq)
                    dve.sem_inc(S("angles"), 1)

                def decayed(it, n, j):
                    t, g = n // 2, n % 2
                    if j == 0:
                        dve.wait_ge(S("e_done"), it * 5 + n + 1)
                        if t == 1:
                            dve.wait_ge(S("o_done"), it * 4 + g + 2)
                    dve.wait_ge(S("pair"), it * 16 + n * 4 + j + 1)
                    for m in (2 * j, 2 * j + 1):
                        v.scalar_tensor_tensor(nt[g][:, m, :], ps2[:, j % 2, m % 2, 1, :],
                                               sc[:, 0, t, g * M + m:g * M + m + 1], e[g][:, m, :],
                                               ALU.mult, ALU.mult)
                    v.tensor_tensor(pm[g][:, 2 * j:2 * j + 2, :], ps2[:, j % 2, :, 0, :],
                                    e[g][:, 2 * j:2 * j + 2, :], ALU.mult).then_inc(S("pair_out"), 1)

                def start_inverse(it, t, g):
                    dve.wait_ge(S("ntd_done"), it * 16 + 4 * (2 * t + g) + 4)
                    v.transpose(ny[g][:, :, 0, :], ntd[g][:, :, :]).then_inc(S(f"turned{g}"), 1)
                    dve.wait_ge(S(f"turned{g}"), it * 2 + t + 1)
                    v.tensor_tensor(ny[g][:, :, 1, :], ny[g][:, :, 0, :], bc(k.identc[:, :], 1, M), ALU.add)\
                        .then_inc(S(f"level{g}"), 1)

                def batch(b, hp, nhp):
                    it = b + hp * B
                    for t in range(TPB):
                        for g in range(2):
                            n = 2 * t + g
                            for j in range(0 if n else 2, 4):
                                if g == 1 and j == 2:
                                    start_inverse(it, t, 0)
                                decayed(it, n, j)
                        start_inverse(it, t, 1)
                        if t == 1 and nhp is not None:
                            stage_decays(b + 1 if nhp == hp else 0, it + 1, nhp)
                        for lv in range(5):
                            for g in range(2):
                                if lv < 4:
                                    dve.wait_ge(S(f"wide{g}"), it * 8 + t * 4 + lv + 1)
                                    turn = v.transpose(nkt[g][:, :, :, :].rearrange("p m s c -> p (m s) c"),
                                                       wide[g][:, :, :, :].rearrange("p m s c -> p (m s) c"))
                                    if lv == 0:
                                        turn.then_inc(S(f"level{g}"), 1)
                                if lv:
                                    dve.wait_ge(S(f"kept{g}"), it * 10 + t * 5 + lv + 1)
                                    v.tensor_tensor(ny[g][:, :, 1, :], ny[g][:, :, 1, :], ny[g][:, :, 2, :], ALU.add)\
                                        .then_inc(S(f"level{g}" if lv < 4 else f"summed{g}"), 1)
                                if lv == 4:
                                    dve.wait_ge(S(f"summed{g}"), it * 2 + t + 1)
                                    v.transpose(zt[g][:, :, :], ny[g][:, :, 1, :]).then_inc(S(f"level{g}"), 1)
                                if t == 0 and lv == 0:
                                    rotate_cos(it, 1, g, hp)
                                if t == 0 and lv == 2:
                                    rotate_sin(it, 1, g)
                                if t == 0 and lv == 3 and g == 0:
                                    dve.wait_ge(S("gate_read"), it + 1)
                                    v.tensor_scalar_add(gt[:, :], gx[:, :], 1.0).then_inc(S("gate_one"), 1)
                                    dve.wait_ge(S("gate_one"), it + 1)
                                    v.reciprocal(gt[:, :], gt[:, :]).then_inc(S("gate_done"), 1)
                                if t == 1 and nhp is not None:
                                    if lv == 1 and g == 1:
                                        norms(it + 1)
                        if t == 1:
                            for g in range(2):
                                dve.wait_ge(S("from_state"), it * 2 + g + 1)
                                dve.wait_ge(S("r_done"), it * 4 + 2 + g + 1)
                                v.tensor_tensor(r[g][:, :, :], r[g][:, :, :], pxw[g][:, :, :], ALU.subtract)\
                                    .then_inc(S(f"right{g}"), 1)
                            if nhp is not None:
                                normed(it + 1)
                                dve.wait_ge(S("kturn"), it * 2 + 2)
                                if nhp > hp:
                                    dve.wait_ge(S("sines"), nhp * B + 1)
                                for i in range(2):
                                    rotate_cos(it + 1, 0, i, nhp)
                        else:
                            for g in range(2):
                                dve.wait_ge(S("r_done"), it * 4 + g + 1)
                                dve.sem_inc(S(f"right{g}"), 1)
                        for c in range(1, NB):
                            rs = slice(CB * c, CB * c + CB)
                            for g in range(2):
                                dve.wait_ge(S(f"carried{g}"), it * 6 + t * 3 + c)
                                if t == 1:
                                    dve.wait_ge(S(f"right{g}"), it * 8 + 5)
                                v.tensor_tensor(r[g][rs, :, :], r[g][rs, :, :], pxw[g][rs, :, :], ALU.add)\
                                    .then_inc(S(f"right{g}"), 1)
                        dve.wait_ge(S("w_out0"), it * 8 + t * 4 + 4)
                        v.tensor_tensor(ub[0][:, :, :], w[0][:, :, :], bc(sc[:, 1, t, 0:M], 2, DV), ALU.mult)\
                            .then_inc(S("u_first"), 1)
                        if t == 0 and hp + 1 < HP:
                            next_angles(b, it, hp + 1)
                    if nhp is not None:
                        for i in range(2):
                            rotate_sin(it + 1, 0, i)
                    dve.wait_ge(S("o_done"), it * 4 + 5)
                    dve.wait_ge(S("gate_done"), it + 1)
                    v.tensor_tensor(og[:, :], po[:, 0:T], gt[:, :], ALU.mult).then_inc(S("og_done"), 1)
                    if nhp is not None:
                        stage_scalars(b + 1 if nhp == hp else 0, it + 1, nhp)
                        for j in range(2):
                            decayed(it + 1, 0, j)
                    dve.wait_ge(S("out_done"), it + 1)
                    ga = k.gates[:, 0, bass.ds(b, 1), :].broadcast_to([P, TPB, D])
                    v.tensor_tensor(xg[:, :, :], pk[:, 0:T].rearrange("p (t d) -> p t d", t=TPB), ga, ALU.mult)\
                        .then_inc(S("xg_done"), 1)
                    dve.wait_ge(S("xg_done"), it + 1)
                    xb = k.x[:, bass.ds(b * TPB, TPB), :]
                    v.tensor_tensor(xb, xb, xg[:, :, :], ALU.add).then_inc(S("end_dve"), 1)

                stage_decays(0, 0, 0)
                norms(0)
                normed(0)
                for i in range(2):
                    rotate_cos(0, 0, i, 0)
                for i in range(2):
                    rotate_sin(0, 0, i)
                stage_scalars(0, 0, 0)
                for j in range(2):
                    decayed(0, 0, j)
                for hp in range(HP):
                    with dve.Fori(0, B - 1) as b:
                        batch(b, hp, hp)
                    batch(B - 1, hp, hp + 1 if hp + 1 < HP else None)

            @block.gpsimd
            def _(pool):
                p = nc.gpsimd
                pool.sem_inc(S("o_done"), 1)

                def decays(t, g):
                    p.affine_select(out=gl[g][:, :, :], in_=bc(ld[:, t, g * M:g * M + M], 2, P),
                                    compare_op=ALU.is_ge, fill=0.0, base=0, pattern=[[0, M], [1, P]],
                                    channel_multiplier=-1).then_inc(S("gl_done"), 1)

                def first_decays(nx):
                    if not isinstance(nx, int) or nx:
                        pool.wait_ge(S("grow"), nx)
                    pool.wait_ge(S("staged_d"), nx + 1)
                    stand(pool)
                    decays(0, 0)
                    decays(0, 1)

                def rotate(nx, t, hp):
                    ts = slice(t * P, (t + 1) * P)
                    pool.wait_ge(S("xn_done"), nx + 1)
                    p.tensor_tensor(tmp[:, :, :, :], bc(xn[:, 1, :, ts], 1, M), bc(a.sin[hp % 2][:, :, ts], 2, 2), ALU.mult)\
                        .then_inc(S("tmp_done"), 1)

                def batch(b, hp, nhp):
                    it = b + hp * B
                    pool.wait_ge(S("staged_s"), it + 1)

                    def right_side(t, g):
                        pool.wait_ge(S("o_done"), it * 4 + 1 + (g + 1 if t else 0))
                        if t == 0:
                            pool.wait_ge(S("v_read"), it + 1)
                        p.tensor_tensor(r[g][:, :, :],
                                        bc(vv[:, t, g * DV:(g + 1) * DV], 1, M),
                                        bc(a.wmode[:, hp, g * M:g * M + M], 2, DV), ALU.mult).then_inc(S("r_done"), 1)

                    for t in range(TPB):
                        if t:
                            for g in range(2):
                                pool.wait_ge(S("expo"), it * 4 + g + 1)
                                stand(pool)
                                decays(1, g)
                        for g in range(2):
                            n = 2 * t + g
                            pool.wait_ge(S("pair_out"), it * 16 + 4 * n + 4)
                            if t:
                                pool.wait_ge(S(f"power{g}"), it * 10 + 1)
                            stand(pool)
                            for q in range(NB):
                                rs = slice(CB * q, CB * q + CB)
                                p.affine_select(out=ntd[g][rs, :, :], in_=nt[g][rs, :, rs], compare_op=ALU.is_gt,
                                                fill=0.0, base=0, pattern=[[0, M], [1, CB]], channel_multiplier=-1)\
                                    .then_inc(S("ntd_done"), 1)
                                pool.wait_ge(S("ntd_done"), it * 16 + 4 * n + q + 1)
                                stand(pool)
                        if t == 0:
                            pool.wait_ge(S("xr_done"), it * 2 + 1)
                            rotate(it, 1, hp)
                        for g in range(2):
                            right_side(t, g)
                        if t == 1:
                            pool.wait_ge(S("e_done"), it * 5 + 5)
                            pool.wait_ge(S("pair_out"), it * 16 + 16)
                            last = p.tensor_tensor(xr[1][:, :, :, :], xr[1][:, :, :, :],
                                                   bc(tmp[:, 0:4, :, :].rearrange("p a b t -> p (a b) t"), 2, 2), ALU.mult)
                            last.then_inc(S("xscaled"), 1)
                            if nhp is not None:
                                first_decays(it + 1)
                                pool.wait_ge(S("xscaled"), it + 1)
                                if nhp > hp:
                                    pool.wait_ge(S("sines"), nhp * B + 1)
                                rotate(it + 1, 0, nhp)
                        pool.wait_ge(S("w_out1"), it * 8 + t * 4 + 4)
                        p.tensor_tensor(ub[1][:, :, :], w[1][:, :, :], bc(sc[:, 1, t, M:2 * M], 2, DV), ALU.mult)\
                            .then_inc(S("u_done"), 1)
                        if t == 0:
                            pool.wait_ge(S("w_out0"), it * 8 + 4)
                            for g in range(2):
                                p.tensor_tensor(ua[g][:, :, :], w[g][:, :, :], bc(sc[:, 2, t, g * M:g * M + M], 2, DV), ALU.mult)\
                                    .then_inc(S("ua_done"), 1)

                first_decays(0)
                rotate(0, 0, 0)
                for hp in range(HP):
                    with pool.Fori(0, B - 1) as b:
                        batch(b, hp, hp)
                    batch(B - 1, hp, hp + 1 if hp + 1 < HP else None)


def program(nc, ins, out):
    with ExitStack() as ctx:
        k = Kernel(nc, ctx, ins, out)

        def run(phase, *args):
            with k.scope():
                phase(k, *args)

        run(phase_constants)
        run(phase_modulation, 0)
        run(phase_norm, "ln0a", 0, 1)
        with ExitStack() as actx:
            a = L0Attention(k, actx)
            run(phase_l0_tokens, a)
            run(phase_l0_angles, a)
            run(phase_l0_pairs, a)
        run(phase_norm, "ln0f", 3, 4)
        combT = nc.dram_tensor("comb0", (64, TILES * P), F32, kind="Internal").ap()
        with ExitStack() as ectx:
            res = k.sb(ectx, "res0", [P, TILES * P])
            run(phase_route0, combT)
            run(phase_experts0, combT, res)
            run(phase_back, "back0", res, 1)
        run(phase_modulation, 1)
        run(phase_norm, "ln1a", 0, 1)
        run(phase_l1_attention)
        run(phase_norm, "ln1f", 3, 4)
        gatesT = nc.dram_tensor("gates1", (16, TILES * P), F32, kind="Internal").ap()
        slotsT = nc.dram_tensor("slotrows1", (16, TILES * P), BF16, kind="Internal").ap()
        with ExitStack() as ectx:
            res = k.sb(ectx, "res1", [P, TILES * P])
            gts = k.sb(ectx, "gts1", [16, TILES * P])
            xt = k.sb(ectx, "xt1", [P, TILES, D])
            slots = k.sb(ectx, "slots1", [P, 16, TILES])
            run(phase_route1, gatesT, slotsT, gts, xt, slots)
            run(phase_experts1, gatesT, slotsT, gts, xt, slots, res)
            run(phase_back, "back1", res, 1)
        run(phase_store)


def phase_route0(k, combT):
    nc = k.nc
    E, G = 64, 8
    TG, K = 4, 6
    with ExitStack() as ctx:
        gw = k.sb(ctx, "r0_gw", [P, E])
        bias = k.sb(ctx, "r0_bias", [P, E])
        sc = k.sb(ctx, "r0_sc", [P, TILES, E])
        gs = k.sb(ctx, "r0_gs", [P, TILES, G])
        cmp = k.sb(ctx, "r0_cmp", [P, TILES, G, G])
        cmq = k.sb(ctx, "r0_cmq", [P, TILES, G, G])
        cnt = k.sb(ctx, "r0_cnt", [P, 2, TILES, G])
        tri = k.sb(ctx, "r0_tri", [P, G, G])
        top = k.sb(ctx, "r0_top", [P, TILES, 8])
        eq = k.sb(ctx, "r0_eq", [P, TILES, E])
        gt = k.sb(ctx, "r0_gt", [P, TILES, E])
        cum = k.sb(ctx, "r0_cum", [P, TILES, E])
        one = k.sb(ctx, "r0_one", [P, E])
        left = k.sb(ctx, "r0_left", [P, 2, TILES])
        ct = k.sb(ctx, "r0_ct", [E, TILES * P])
        pl = k.ps(ctx, "r0_pl", [P, TILES, E])
        pc = k.ps(ctx, "r0_pc", [E, TILES * P])
        loaded, logits, neg, expd, made = (k.sem(f"r0_{n}") for n in ("loaded", "logits", "neg", "exp", "tri"))
        chain, comb, turned, copied, kept = (k.sem(f"r0_{n}") for n in ("chain", "comb", "turned", "copied", "kept"))
        with nc.Block() as block:

            @block.sync
            def _(sp):
                sp.dma_start(gw[:, :], k.ins["gate_w"]).then_inc(loaded, 16)
                sp.dma_start(bias[:, :], k.ins["gate_bias"].partition_broadcast(P)).then_inc(loaded, 16)
                sp.wait_ge(copied, 4)
                sp.dma_start(combT, ct[:, :]).then_inc(kept, 16)
                sp.wait_ge(kept, 16)

            @block.gpsimd
            def _(pool):
                nc.gpsimd.affine_select(out=tri[:, :, :], in_=k.ones[:, 0:G * G].rearrange("p (a b) -> p a b", a=G),
                                        compare_op=ALU.is_gt, fill=0.0, base=0, pattern=[[1, G], [-1, G]],
                                        channel_multiplier=0).then_inc(made, 1)

            @block.tensor
            def _(pe):
                pe.wait_ge(loaded, 32)
                for n in range(TILES):
                    last = nc.tensor.matmul(pl[:, n, :], k.hT[:, n * P:(n + 1) * P], gw[:, :], start=True, stop=True)
                last.then_inc(logits, 1)
                pe.wait_ge(comb, 1)
                for n in range(TILES):
                    last = nc.tensor.transpose(pc[:, n * P:(n + 1) * P], cum[:, n, :], k.identf[:, :])
                    if n % 4 == 3:
                        last.then_inc(turned, 1)

            @block.scalar
            def _(act):
                act.wait_ge(neg, 1)
                nc.scalar.activation(sc[:, :, :], sc[:, :, :], ACT.Exp).then_inc(expd, 1)
                for i in range(4):
                    act.wait_ge(turned, i + 1)
                    nc.scalar.activation(ct[:, i * 512:(i + 1) * 512], pc[:, i * 512:(i + 1) * 512], ACT.Copy)\
                        .then_inc(copied, 1)

            @block.vector
            def _(dve):
                v = nc.vector
                step = Chain(dve, chain)
                step(v.memset(one[:, :], 1.0))
                dve.wait_ge(logits, 1)
                v.tensor_scalar(sc[:, :, :], pl[:, :, :], -1.0, 80.0, ALU.mult, ALU.min).then_inc(neg, 1)
                dve.wait_ge(expd, 1)
                step(v.tensor_scalar_add(sc[:, :, :], sc[:, :, :], 1.0))
                step(v.reciprocal(sc[:, :, :], sc[:, :, :]))
                step(v.tensor_tensor(sc[:, :, :], sc[:, :, :], bc(bias[:, :], 1, TILES), ALU.add))
                step(v.tensor_reduce(gs[:, :, :], sc[:, :, :].rearrange("p n (g e) -> p n g e", g=G), AX.X, ALU.max))
                a, b = bc(gs[:, :, :], 2, G), bc(gs[:, :, :], 3, G)
                step(v.tensor_tensor(cmp[:, :, :, :], a, b, ALU.is_gt))
                step(v.tensor_tensor(cmq[:, :, :, :], a, b, ALU.is_equal))
                dve.wait_ge(made, 1)
                step(v.tensor_tensor(cmq[:, :, :, :], cmq[:, :, :, :], bc(tri[:, :, :], 1, TILES), ALU.mult))
                step(v.tensor_tensor(cmp[:, :, :, :], cmp[:, :, :, :], cmq[:, :, :, :], ALU.add))
                step(v.reduce_sum(cnt[:, 0, :, :], cmp[:, :, :, :], AX.X))
                step(v.tensor_scalar(cnt[:, 1, :, :], cnt[:, 0, :, :], TG - 0.5, None, ALU.is_lt))
                step(v.tensor_tensor(sc[:, :, :].rearrange("p n (g e) -> p n g e", g=G),
                                     sc[:, :, :].rearrange("p n (g e) -> p n g e", g=G),
                                     bc(cnt[:, 1, :, :], 3, E // G), ALU.mult))
                for n in range(TILES):
                    last = v.max(top[:, n, :], sc[:, n, :])
                step(last)
                kth = bc(top[:, :, K - 1], 2, E)
                step(v.tensor_tensor(gt[:, :, :], sc[:, :, :], kth, ALU.is_gt))
                step(v.tensor_tensor(eq[:, :, :], sc[:, :, :], kth, ALU.is_equal))
                step(v.reduce_sum(left[:, 0, :], gt[:, :, :], AX.X))
                step(v.tensor_scalar(left[:, 0, :], left[:, 0, :], -1.0, K + 0.5, ALU.mult, ALU.add))
                for n in range(TILES):
                    last = v.tensor_tensor_scan(cum[:, n, :], one[:, :], eq[:, n, :], 0.0, ALU.mult, ALU.add)
                step(last)
                step(v.tensor_tensor(cum[:, :, :], cum[:, :, :], bc(left[:, 0, :], 2, E), ALU.is_lt))
                step(v.tensor_tensor(eq[:, :, :], eq[:, :, :], cum[:, :, :], ALU.mult))
                step(v.tensor_tensor(gt[:, :, :], gt[:, :, :], eq[:, :, :], ALU.add))
                step(v.tensor_tensor(gt[:, :, :], gt[:, :, :], sc[:, :, :], ALU.mult))
                step(v.reduce_sum(left[:, 1, :], gt[:, :, :], AX.X))
                step(v.tensor_scalar_add(left[:, 1, :], left[:, 1, :], 1e-8))
                step(v.reciprocal(left[:, 1, :], left[:, 1, :]))
                v.tensor_tensor(cum[:, :, :], gt[:, :, :], bc(left[:, 1, :], 2, E), ALU.mult).then_inc(comb, 1)


def phase_experts0(k, combT, res):
    nc = k.nc
    ITEMS, NC = 33, 4
    C = TILES * P // NC
    with ExitStack() as ctx:
        wt = [k.sb(ctx, f"e0_w{s}", [P, 3, P]) for s in range(2)]
        cb = [k.sb(ctx, f"e0_c{s}", [P, TILES * P]) for s in range(2)]
        sg = [k.sb(ctx, f"e0_s{s}", [P, C]) for s in range(2)]
        ht = [k.sb(ctx, f"e0_h{s}", [P, C]) for s in range(2)]
        pg = k.ps(ctx, "e0_pg", [P, C])
        pu = k.ps(ctx, "e0_pu", [P, C])
        acc = k.ps(ctx, "e0_acc", [P, NC, C])
        w_in, c_in = ([k.sem(f"e0_{n}{s}") for s in range(2)] for n in ("w_in", "c_in"))
        g_done, u_done, d_done, silu, h_done, scaled, out = (
            k.sem(f"e0_{n}") for n in ("g", "u", "down", "silu", "h", "scaled", "out"))
        zeroed, zero_read = k.sem("e0_zeroed"), k.sem("e0_zero_read")

        with nc.Block() as block:

            @block.sync
            def _(sp):
                def item(i, s, n):
                    sp.wait_ge(d_done, (i - 1) * NC + 1)
                    sp.dma_start(wt[s][:, :, :], k.ins["moe0"][bass.ds(i, 1)].squeeze(0)).then_inc(w_in[s], 16)
                    for e in range(2):
                        row = combT[bass.ds(i * 2 - 2 + e, 1), :].broadcast_to([64, TILES * P])
                        sp.dma_start(cb[s][64 * e:64 * e + 64, :], row).then_inc(c_in[s], 16)

                sp.dma_start(wt[0][:, :, :], k.ins["moe0"][0]).then_inc(w_in[0], 16)
                with sp.Fori(0, (ITEMS - 3) // 2) as l:
                    item(l * 2 + 1, 1, l + 1)
                    item(l * 2 + 2, 0, l + 2)
                item(ITEMS - 2, 1, ITEMS // 2)
                item(ITEMS - 1, 0, ITEMS // 2 + 1)

            @block.tensor
            def _(pe):
                mm = nc.tensor.matmul
                pe.sem_inc(d_done, 1)

                def down(i, s, j, start, stop):
                    pe.wait_ge(h_done, i * NC + j + 1)
                    mm(acc[:, j, :], wt[s][:, 2, :], ht[j % 2][:, :], start=start, stop=stop,
                       skip_group_check=True).then_inc(d_done, 1)

                def item(i, s, n, first=False, last=False):
                    pe.wait_ge(w_in[s], n * 16)
                    for j in range(NC):
                        cs = slice(j * C, (j + 1) * C)
                        if not (first and j == 0):
                            pe.wait_ge(silu, i * NC + j)
                        mm(pg[:, :], wt[s][:, 0, :], k.hT[:, cs], start=True, stop=True).then_inc(g_done, 1)
                        if not (first and j == 0):
                            pe.wait_ge(h_done, i * NC + j)
                        mm(pu[:, :], wt[s][:, 1, :], k.hT[:, cs], start=True, stop=True).then_inc(u_done, 1)
                        if j:
                            down(i, s, j - 1, first, last)
                        elif not first:
                            down(i - 1, 1 - s, NC - 1, False, False)
                    if last:
                        down(i, s, NC - 1, False, True)

                pe.wait_ge(zeroed, 1)
                for j in range(NC):
                    mm(acc[:, j, :], k.identf[:, :], sg[1][:, :], start=True, stop=False, skip_group_check=True)\
                        .then_inc(zero_read, 1)
                item(0, 0, 1, first=True)
                with pe.Fori(0, (ITEMS - 3) // 2) as l:
                    item(l * 2 + 1, 1, l + 1)
                    item(l * 2 + 2, 0, l + 2)
                item(ITEMS - 2, 1, ITEMS // 2)
                item(ITEMS - 1, 0, ITEMS // 2 + 1, last=True)

            @block.scalar
            def _(act):
                def item(i, s, n, first=False):
                    for j in range(NC):
                        act.wait_ge(g_done, i * NC + j + 1)
                        if not (first and j < 2):
                            act.wait_ge(h_done, i * NC + j - 1)
                        if first and j == 1:
                            act.wait_ge(zero_read, NC)
                        nc.scalar.activation(sg[j % 2][:, :], pg[:, :], ACT.Silu).then_inc(silu, 1)
                item(0, 0, 1, first=True)
                with act.Fori(0, (ITEMS - 3) // 2) as l:
                    item(l * 2 + 1, 1, l + 1)
                    item(l * 2 + 2, 0, l + 2)
                item(ITEMS - 2, 1, ITEMS // 2)
                item(ITEMS - 1, 0, ITEMS // 2 + 1)
                act.wait_ge(d_done, ITEMS * NC + 1)
                nc.scalar.activation(res[:, :], acc[:, :, :].rearrange("p a b -> p (a b)"), ACT.Copy)

            @block.vector
            def _(dve):
                v = nc.vector
                v.memset(sg[1][:, :], 0.0).then_inc(zeroed, 1)

                def item(i, s, n, first=False):
                    for j in range(NC):
                        cs = slice(j * C, (j + 1) * C)
                        dve.wait_ge(silu, i * NC + j + 1)
                        if first:
                            left = sg[j % 2][:, :]
                        else:
                            if j == 0:
                                dve.wait_ge(c_in[s], (n + s - 1) * 32)
                            v.tensor_tensor(cb[s][:, cs], cb[s][:, cs], sg[j % 2][:, :], ALU.mult).then_inc(scaled, 1)
                            dve.wait_ge(scaled, (i - 1) * NC + j + 1)
                            left = cb[s][:, cs]
                        dve.wait_ge(u_done, i * NC + j + 1)
                        if not (first and j < 2):
                            dve.wait_ge(d_done, i * NC + j)
                        v.tensor_tensor(ht[j % 2][:, :], left, pu[:, :], ALU.mult).then_inc(h_done, 1)
                item(0, 0, 1, first=True)
                with dve.Fori(0, (ITEMS - 3) // 2) as l:
                    item(l * 2 + 1, 1, l + 1)
                    item(l * 2 + 2, 0, l + 2)
                item(ITEMS - 2, 1, ITEMS // 2)
                item(ITEMS - 1, 0, ITEMS // 2 + 1)


def phase_back(k, name, res, gate):
    nc = k.nc
    with ExitStack() as ctx:
        xg = k.sb(ctx, f"{name}_xg", [P, TILES, D])
        pt = k.ps(ctx, f"{name}_pb", [P, TILES, D])
        turned, chain = k.sem(f"{name}_turned"), k.sem(f"{name}_chain")
        with nc.Block() as block:

            @block.tensor
            def _(pe):
                for n in range(TILES):
                    last = nc.tensor.transpose(pt[:, n, :], res[:, n * P:(n + 1) * P], k.identf[:, :])
                    if n % 4 == 3:
                        last.then_inc(turned, 1)

            @block.vector
            def _(dve):
                step = Chain(dve, chain)
                for i in range(4):
                    ns = slice(4 * i, 4 * i + 4)
                    dve.wait_ge(turned, i + 1)
                    g = bc(k.gates[:, gate, 2 * i:2 * i + 2, :], 2, TPB)
                    step(nc.vector.tensor_tensor(xg[:, ns, :].rearrange("p (b t) d -> p b t d", t=TPB),
                                                 pt[:, ns, :].rearrange("p (b t) d -> p b t d", t=TPB), g, ALU.mult))
                    step(nc.vector.tensor_tensor(k.x[:, ns, :], k.x[:, ns, :], xg[:, ns, :], ALU.add))


def phase_l1_attention(k):
    nc = k.nc
    DH = 8
    EPS = 1e-6
    with ExitStack() as ctx:
        wqo = k.sb(ctx, "a1_wqo", [P, 2, D])
        wkv = k.sb(ctx, "a1_wkv", [P, 2, D])
        bq = k.sb(ctx, "a1_bq", [P, 1])
        rows = k.sb(ctx, "a1_rows", [P, 3, D])
        mask = k.sb(ctx, "a1_mask", [P, D // DH, DH])
        qT = k.sb(ctx, "a1_qT", [P, TILES * P])
        qe = k.sb(ctx, "a1_qe", [P, TILES * P])
        kv = k.sb(ctx, "a1_kv", [P, TILES, 2, D])
        ke = k.sb(ctx, "a1_ke", [P, TILES, D])
        kvm = k.sb(ctx, "a1_kvm", [P, B, 2, D])
        oT = k.sb(ctx, "a1_oT", [P, TILES * P])
        rc = k.sb(ctx, "a1_rc", [P, TILES * P])
        xg = k.sb(ctx, "a1_xg", [P, TILES, D])
        pa = k.ps(ctx, "a1_pa", [P, 4, 512])
        pb = k.ps(ctx, "a1_pb", [P, 4, 512])
        names = ("loaded", "q_done", "q_clip", "q_exp", "q_read", "kv_done", "kv_read", "k_clip", "k_exp", "kv_ready",
                 "sums", "sums_read", "outs", "outs_read", "proj", "chain", "made", "q_ready")
        sem = {n: k.sem(f"a1_{n}") for n in names}
        with nc.Block() as block:

            @block.sync
            def _(sp):
                sp.dma_start(wqo[:, :, :], k.ins["a1_wqo"]).then_inc(sem["loaded"], 16)
                sp.dma_start(wkv[:, :, :], k.ins["a1_wkv"]).then_inc(sem["loaded"], 16)
                sp.dma_start(bq[:, :], k.ins["a1_bq"]).then_inc(sem["loaded"], 16)
                sp.dma_start(rows[:, :, :], k.ins["a1_rows"].partition_broadcast(P)).then_inc(sem["loaded"], 16)

            @block.gpsimd
            def _(pool):
                nc.gpsimd.affine_select(out=mask[:, :, :], in_=k.ones[:, :].rearrange("p (a b) -> p a b", b=DH),
                                        compare_op=ALU.is_ge, fill=0.0, base=0, pattern=[[-DH, D // DH], [0, DH]],
                                        channel_multiplier=1).then_inc(sem["made"], 1)
                pool.wait_ge(sem["made"], 1)
                nc.gpsimd.affine_select(out=mask[:, :, :], in_=mask[:, :, :],
                                        compare_op=ALU.is_ge, fill=0.0, base=DH - 1,
                                        pattern=[[DH, D // DH], [0, DH]],
                                        channel_multiplier=-1).then_inc(sem["made"], 1)

            @block.tensor
            def _(pe):
                mm = nc.tensor.matmul
                pe.wait_ge(sem["loaded"], 64)
                for j in range(4):
                    mm(pa[:, j, :], wqo[:, 0, :], k.hT[:, j * 512:(j + 1) * 512], start=True, stop=True)\
                        .then_inc(sem["q_done"], 1)
                for j in range(8):
                    if j >= 4:
                        pe.wait_ge(sem["kv_read"], j - 3)
                    for n in (2 * j, 2 * j + 1):
                        last = mm(pb[:, j % 4, (n % 2) * 256:(n % 2 + 1) * 256], k.hT[:, n * P:(n + 1) * P],
                                  wkv[:, :, :].rearrange("p a d -> p (a d)"), start=True, stop=True)
                    last.then_inc(sem["kv_done"], 1)
                pe.wait_ge(sem["kv_ready"], 1)
                pe.wait_ge(sem["q_ready"], 1)
                for b in range(B):
                    for t in range(TPB):
                        n = b * TPB + t
                        mm(pa[:, b // 2, (b % 2) * 256:(b % 2) * 256 + D], kv[:, n, 0, :], kv[:, n, 1, :],
                           start=(t == 0), stop=(t == TPB - 1))
                    for t in range(TPB):
                        n = b * TPB + t
                        last = mm(pa[:, b // 2, (b % 2) * 256 + D:(b % 2) * 256 + 2 * D], kv[:, n, 0, :], k.ones[:, :],
                                  start=(t == 0), stop=(t == TPB - 1))
                    last.then_inc(sem["sums"], 1)
                for j in range(4):
                    pe.wait_ge(sem["sums_read"], 4)
                    if j:
                        pe.wait_ge(sem["outs_read"], j)
                    for b in (2 * j, 2 * j + 1):
                        bs = slice(b * T, (b + 1) * T)
                        for i in range(2):
                            last = mm(pb[:, 2 * (j % 2) + i, (b % 2) * T:(b % 2 + 1) * T], kvm[:, b, i, :], qT[:, bs],
                                      start=True, stop=True)
                    last.then_inc(sem["outs"], 1)
                pe.wait_ge(sem["outs_read"], 4)
                for n in range(TILES):
                    last = mm(pa[:, n // 4, (n % 4) * D:(n % 4 + 1) * D], oT[:, n * P:(n + 1) * P], wqo[:, 1, :],
                              start=True, stop=True)
                    if n % 4 == 3:
                        last.then_inc(sem["proj"], 1)

            @block.scalar
            def _(act):
                act.wait_ge(sem["q_clip"], 1)
                nc.scalar.activation(qe[:, :], qe[:, :], ACT.Exp).then_inc(sem["q_exp"], 1)
                act.wait_ge(sem["k_clip"], 1)
                nc.scalar.activation(ke[:, :, :], ke[:, :, :], ACT.Exp).then_inc(sem["k_exp"], 1)

            @block.vector
            def _(dve):
                v = nc.vector
                step = Chain(dve, sem["chain"])
                dve.wait_ge(sem["loaded"], 64)
                dve.wait_ge(sem["q_done"], 4)
                step(v.tensor_scalar(qT[:, :], pa[:, :, :].rearrange("p a b -> p (a b)"), bq[:, 0:1], None, ALU.add))
                v.tensor_scalar_min(qe[:, :], qT[:, :], 0.0).then_inc(sem["q_clip"], 1)
                for j in range(8):
                    dve.wait_ge(sem["kv_done"], j + 1)
                    v.tensor_tensor(kv[:, 2 * j:2 * j + 2, :, :], pb[:, j % 4, :].rearrange("p (n a d) -> p n a d", n=2, a=2),
                                    bc(rows[:, 0:2, :], 1, 2), ALU.add).then_inc(sem["kv_read"], 1)
                dve.wait_ge(sem["kv_read"], 8)
                v.tensor_scalar_min(ke[:, :, :], kv[:, :, 0, :], 0.0).then_inc(sem["k_clip"], 1)
                dve.wait_ge(sem["q_exp"], 1)
                v.scalar_tensor_tensor(qT[:, :], qT[:, :], 0.0, qe[:, :], ALU.max, ALU.add).then_inc(sem["q_ready"], 1)
                dve.wait_ge(sem["k_exp"], 1)
                v.scalar_tensor_tensor(kv[:, :, 0, :], kv[:, :, 0, :], 0.0, ke[:, :, :], ALU.max, ALU.add)\
                    .then_inc(sem["kv_ready"], 1)
                dve.wait_ge(sem["made"], 2)
                m = mask[:, :, :].rearrange("p a b -> p (a b)")
                for j in range(4):
                    dve.wait_ge(sem["sums"], 2 * j + 2)
                    v.tensor_tensor(kvm[:, 2 * j:2 * j + 2, :, :], pa[:, j, :].rearrange("p (b a d) -> p b a d", b=2, a=2),
                                    bc(bc(m, 1, 2), 1, 2), ALU.mult).then_inc(sem["sums_read"], 1)
                for j in range(4):
                    cs = slice(j * 512, (j + 1) * 512)
                    dve.wait_ge(sem["outs"], j + 1)
                    step(v.tensor_scalar_max(rc[:, cs], pb[:, 2 * (j % 2) + 1, :], EPS))
                    step(v.reciprocal(rc[:, cs], rc[:, cs]))
                    v.tensor_tensor(oT[:, cs], pb[:, 2 * (j % 2), :], rc[:, cs], ALU.mult).then_inc(sem["outs_read"], 1)
                for i in range(4):
                    ns = slice(4 * i, 4 * i + 4)
                    dve.wait_ge(sem["proj"], i + 1)
                    step(v.tensor_tensor(xg[:, ns, :], pa[:, i, :].rearrange("p (n d) -> p n d", d=D),
                                         bc(rows[:, 2, :], 1, 4), ALU.add))
                    g = bc(k.gates[:, 0, 2 * i:2 * i + 2, :], 2, TPB)
                    x4 = xg[:, ns, :].rearrange("p (b t) d -> p b t d", t=TPB)
                    step(v.tensor_tensor(x4, x4, g, ALU.mult))
                    step(v.tensor_tensor(k.x[:, ns, :], k.x[:, ns, :], xg[:, ns, :], ALU.add))


def phase_route1(k, gatesT, slotsT, gts, xt, slots):
    nc = k.nc
    E = 16
    CAP = B * T // E
    GONE = -3.0e38
    with ExitStack() as ctx:
        rw = k.sb(ctx, "r1_rw", [P, E])
        rb = k.sb(ctx, "r1_rb", [P, E])
        nw = k.sb(ctx, "r1_nw", [P, 1])
        sq = k.sb(ctx, "r1_sq", [P, TILES * P])
        ms = k.sb(ctx, "r1_ms", [P, TILES * P])
        lg = k.sb(ctx, "r1_lg", [P, TILES, E])
        pr = k.sb(ctx, "r1_pr", [P, TILES, E])
        gn = k.sb(ctx, "r1_gn", [P, TILES, E])
        st = k.sb(ctx, "r1_st", [P, 4, TILES])
        lt = k.sb(ctx, "r1_lt", [E, TILES * P])
        top = k.sb(ctx, "r1_top", [E, 8])
        ch = k.sb(ctx, "r1_ch", [P, TILES, E])
        off = k.sb(ctx, "r1_off", [P, TILES, E])
        sl = k.sb(ctx, "r1_sl", [P, TILES, E])
        slr = k.sb(ctx, "r1_slr", [E, TILES * P], BF16)
        ps = k.ps(ctx, "r1_ps", [P, TILES * P])
        pl = k.ps(ctx, "r1_pl", [P, TILES, E])
        names = ("loaded", "squared", "means", "var", "log", "normed", "logits", "biased", "turned", "chosen",
                 "back", "gated", "gturned", "copied", "kept", "chain", "shifted", "expd",
                 "ps_free", "xturned", "xcopied", "picked", "counted", "slotted", "sturned", "scopied")
        sem = {n: k.sem(f"r1_{n}") for n in names}
        with nc.Block() as block:

            @block.sync
            def _(sp):
                sp.dma_start(rw[:, :], k.ins["router_w"]).then_inc(sem["loaded"], 16)
                sp.dma_start(rb[:, :], k.ins["router_b"].partition_broadcast(P)).then_inc(sem["loaded"], 16)
                sp.dma_start(nw[:, :], k.ins["norm_w"]).then_inc(sem["loaded"], 16)
                sp.wait_ge(sem["copied"], 1)
                sp.dma_start(gatesT, gts[:, :]).then_inc(sem["kept"], 16)
                sp.wait_ge(sem["scopied"], 1)
                sp.dma_start(slotsT, slr[:, :]).then_inc(sem["kept"], 16)
                sp.wait_ge(sem["kept"], 32)

            @block.scalar
            def _(act):
                nc.scalar.activation(sq[:, :], k.hT[:, :], ACT.Square).then_inc(sem["squared"], 1)
                act.wait_ge(sem["var"], 1)
                nc.scalar.activation(sq[:, :], ms[:, :], ACT.Ln).then_inc(sem["log"], 1)
                act.wait_ge(sem["log"], 1)
                nc.scalar.activation(sq[:, :], sq[:, :], ACT.Exp, scale=-0.5).then_inc(sem["log"], 1)
                act.wait_ge(sem["shifted"], 1)
                nc.scalar.activation(pr[:, :, :], pr[:, :, :], ACT.Exp).then_inc(sem["expd"], 1)
                for j in range(4):
                    act.wait_ge(sem["xturned"], j + 1)
                    nc.scalar.activation(xt[:, 4 * j:4 * j + 4, :].rearrange("p n d -> p (n d)"),
                                         ps[:, j * 512:(j + 1) * 512], ACT.Copy).then_inc(sem["xcopied"], 1)

            @block.tensor
            def _(pe):
                pe.wait_ge(sem["squared"], 1)
                for j in range(4):
                    last = nc.tensor.matmul(ps[:, j * 512:(j + 1) * 512], k.ones[:, :], sq[:, j * 512:(j + 1) * 512],
                                            start=True, stop=True)
                last.then_inc(sem["means"], 1)
                pe.wait_ge(sem["loaded"], 48)
                pe.wait_ge(sem["normed"], 1)
                for n in range(TILES):
                    last = nc.tensor.matmul(pl[:, n, :], k.hT[:, n * P:(n + 1) * P], rw[:, :], start=True, stop=True)
                last.then_inc(sem["logits"], 1)
                pe.wait_ge(sem["biased"], 1)
                for n in range(TILES):
                    last = nc.tensor.transpose(ps[0:E, n * P:(n + 1) * P], lg[:, n, :], k.identf[:, :])
                last.then_inc(sem["turned"], 1)
                pe.wait_ge(sem["ps_free"], 1)
                for n in range(TILES):
                    last = nc.tensor.transpose(ps[:, n * P:(n + 1) * P], k.hT[:, n * P:(n + 1) * P], k.identf[:, :])
                    if n % 4 == 3:
                        last.then_inc(sem["xturned"], 1)
                pe.wait_ge(sem["chosen"], 1)
                for n in range(TILES):
                    last = nc.tensor.transpose(pl[:, n, :], lt[:, n * P:(n + 1) * P], k.identf[0:E, 0:E])
                last.then_inc(sem["back"], 1)
                pe.wait_ge(sem["picked"], 1)
                pe.wait_ge(sem["xcopied"], 4)
                picks = ch[:, :, :].rearrange("p n e -> p (n e)")
                nc.tensor.matmul(ps[:, 0:TILES * E], k.upto[:, :], picks, start=True, stop=True)
                nc.tensor.matmul(ps[:, 512:512 + TILES * E], k.ones[:, :], picks, start=True, stop=True)\
                    .then_inc(sem["counted"], 1)
                pe.wait_ge(sem["slotted"], 1)
                pe.wait_ge(sem["gated"], 1)
                for n in range(TILES):
                    last = nc.tensor.transpose(ps[0:E, n * P:(n + 1) * P], gn[:, n, :], k.identf[:, :])
                last.then_inc(sem["gturned"], 1)
                pe.wait_ge(sem["copied"], 1)
                for n in range(TILES):
                    last = nc.tensor.transpose(ps[0:E, n * P:(n + 1) * P], sl[:, n, :], k.identf[:, :])
                last.then_inc(sem["sturned"], 1)

            @block.vector
            def _(dve):
                v = nc.vector
                step = Chain(dve, sem["chain"])
                dve.wait_ge(sem["means"], 1)
                v.tensor_scalar(ms[:, :], ps[:, :], 1.0 / D, 1e-5, ALU.mult, ALU.add).then_inc(sem["var"], 1)
                dve.wait_ge(sem["log"], 2)
                step(v.tensor_tensor(ms[:, :], ms[:, :], sq[:, :], ALU.mult))
                step(v.tensor_tensor(ms[:, :], ms[:, :], sq[:, :], ALU.mult))
                step(v.tensor_scalar(ms[:, :], ms[:, :], -0.5, 1.5, ALU.mult, ALU.add))
                step(v.tensor_tensor(ms[:, :], ms[:, :], sq[:, :], ALU.mult))
                dve.wait_ge(sem["loaded"], 48)
                v.scalar_tensor_tensor(k.hT[:, :], k.hT[:, :], nw[:, 0:1], ms[:, :], ALU.mult, ALU.mult)\
                    .then_inc(sem["normed"], 1)
                dve.wait_ge(sem["logits"], 1)
                v.tensor_tensor(lg[:, :, :], pl[:, :, :], bc(rb[:, :], 1, TILES), ALU.add).then_inc(sem["biased"], 1)
                dve.wait_ge(sem["biased"], 1)
                step(v.tensor_reduce(st[:, 0, :], lg[:, :, :], AX.X, ALU.max))
                v.tensor_tensor(pr[:, :, :], lg[:, :, :], bc(st[:, 0, :], 2, E), ALU.subtract).then_inc(sem["shifted"], 1)
                dve.wait_ge(sem["turned"], 1)
                v.tensor_copy(lt[:, :], ps[0:E, :]).then_inc(sem["ps_free"], 1)
                dve.wait_ge(sem["ps_free"], 1)
                for _ in range(CAP // 8):
                    step(v.max(top[:, :], lt[:, :]))
                    step(v.match_replace(lt[:, :], top[:, :], lt[:, :], GONE))
                v.tensor_scalar(lt[:, :], lt[:, :], GONE, None, ALU.is_equal).then_inc(sem["chosen"], 1)
                dve.wait_ge(sem["expd"], 1)
                step(v.reduce_sum(st[:, 1, :], pr[:, :, :], AX.X))
                step(v.reciprocal(st[:, 1, :], st[:, 1, :]))
                step(v.tensor_tensor(pr[:, :, :], pr[:, :, :], bc(st[:, 1, :], 2, E), ALU.mult))
                dve.wait_ge(sem["back"], 1)
                v.tensor_copy(ch[:, :, :], pl[:, :, :]).then_inc(sem["picked"], 1)
                step(v.tensor_tensor(gn[:, :, :], pr[:, :, :], pl[:, :, :], ALU.mult))
                step(v.reduce_sum(st[:, 2, :], gn[:, :, :], AX.X))
                step(v.tensor_scalar(st[:, 3, :], st[:, 2, :], 0.0, None, ALU.is_equal))
                step(v.tensor_tensor(st[:, 2, :], st[:, 2, :], st[:, 3, :], ALU.add))
                step(v.reciprocal(st[:, 2, :], st[:, 2, :]))
                v.tensor_tensor(gn[:, :, :], gn[:, :, :], bc(st[:, 2, :], 2, E), ALU.mult).then_inc(sem["gated"], 1)
                dve.wait_ge(sem["counted"], 1)
                tot = ps[:, 512:512 + TILES * E].rearrange("p (n e) -> p n e", e=E)
                step(v.memset(off[:, 0, :], 0.0))
                for n in range(1, TILES):
                    step(v.tensor_tensor(off[:, n, :], off[:, n - 1, :], tot[:, n - 1, :], ALU.add))
                step(v.tensor_tensor(off[:, :, :], off[:, :, :], ps[:, 0:TILES * E].rearrange("p (n e) -> p n e", e=E),
                                     ALU.add))
                step(v.tensor_tensor(off[:, :, :], off[:, :, :], ch[:, :, :], ALU.mult))
                v.tensor_scalar_add(sl[:, :, :], off[:, :, :], -1.0).then_inc(sem["slotted"], 1)
                dve.wait_ge(sem["slotted"], 1)
                step(v.tensor_copy(slots[:, :, :], sl[:, :, :].rearrange("p n e -> p e n")))
                dve.wait_ge(sem["gturned"], 1)
                v.tensor_copy(gts[:, :], ps[0:E, :]).then_inc(sem["copied"], 1)
                dve.wait_ge(sem["sturned"], 1)
                v.tensor_copy(slr[:, :], ps[0:E, :]).then_inc(sem["scopied"], 1)


def phase_experts1(k, gatesT, slotsT, gts, xt, slots, res):
    nc = k.nc
    E, F, NC = 16, 512, 4
    FT = F // P
    C = TILES * P // NC
    with ExitStack() as ctx:
        w1 = [k.sb(ctx, f"e1_w1{s}", [P, FT, P]) for s in range(2)]
        w2 = [k.sb(ctx, f"e1_w2{s}", [P, FT, P]) for s in range(2)]
        gr = [k.sb(ctx, f"e1_gr{s}", [P, TILES * P]) for s in range(2)]
        sr = [k.sb(ctx, f"e1_sr{s}", [P, TILES * P], BF16) for s in range(2)]
        hot = [k.sb(ctx, f"e1_hot{s}", [P, TILES, P]) for s in range(2)]
        back = [k.sb(ctx, f"e1_back{s}", [P, TILES * P]) for s in range(2)]
        b1 = k.sb(ctx, "e1_b1", [P, E, FT])
        b1s = [k.sb(ctx, f"e1_b1s{s}", [P, FT]) for s in range(2)]
        b2 = k.sb(ctx, "e1_b2", [E, D])
        xe = [k.sb(ctx, f"e1_xe{s}", [P, P]) for s in range(2)]
        he = [k.sb(ctx, f"e1_he{s}", [P, FT, P]) for s in range(2)]
        ye = [k.sb(ctx, f"e1_ye{s}", [P, D]) for s in range(2)]
        count = k.sb(ctx, "e1_count", [P, P])
        line = k.sb(ctx, "e1_line", [P, 1])
        px = k.ps(ctx, "e1_px", [P, 512])
        ph = k.ps(ctx, "e1_ph", [P, FT, P])
        py = k.ps(ctx, "e1_py", [P, 512])
        acc = k.ps(ctx, "e1_acc", [P, NC, C])
        w_in = [k.sem(f"e1_w_in{s}") for s in range(2)]
        loaded, counts, staged, hot_done, back_done, gathered, xe_done, up_done, gelu, down_done, y_done, added = (
            k.sem(f"e1_{n}") for n in ("loaded", "counts", "staged", "hot", "back_rows", "gathered", "xe", "up",
                                       "gelu", "down", "y", "added"))
        with nc.Block() as block:

            @block.sync
            def _(sp):
                def expert(e, s):
                    sp.dma_start(w1[s][:, :, :], k.ins["fc1"][bass.ds(e, 1)].squeeze(0)).then_inc(w_in[s], 16)
                    sp.dma_start(w2[s][:, :, :], k.ins["fc2"][bass.ds(e, 1)].squeeze(0)).then_inc(w_in[s], 16)
                    sp.dma_start(gr[s][:, :], gatesT[bass.ds(e, 1), :].broadcast_to([P, TILES * P])).then_inc(w_in[s], 16)
                    sp.dma_start(sr[s][:, :], slotsT[bass.ds(e, 1), :].broadcast_to([P, TILES * P])).then_inc(w_in[s], 16)

                sp.dma_start(b1[:, :, :], k.ins["b1"]).then_inc(loaded, 16)
                sp.dma_start(b2[:, :], k.ins["b2"]).then_inc(loaded, 16)
                for e in range(2):
                    expert(e, e)
                with sp.Fori(0, E // 2 - 1) as l:
                    for s in range(2):
                        sp.wait_ge(down_done, l * 2 + (s + 2))
                        sp.wait_ge(back_done, l * 2 + (s + 2))
                        expert(l * 2 + (s + 2), s)

            @block.gpsimd
            def _(pool):
                nc.gpsimd.iota(count[:, :], pattern=[[1, P]], base=0, channel_multiplier=0,
                               allow_small_or_imprecise_dtypes=True).then_inc(counts, 1)
                nc.gpsimd.iota(line[:, :], pattern=[[0, 1]], base=0, channel_multiplier=1,
                               allow_small_or_imprecise_dtypes=True).then_inc(counts, 1)

            @block.tensor
            def _(pe):
                mm = nc.tensor.matmul
                for sm in (gathered, up_done, down_done, added):
                    pe.sem_inc(sm, 1)
                pe.wait_ge(loaded, 32)
                for j in range(NC):
                    mm(acc[:, j, :], b2[:, :], gts[:, j * C:(j + 1) * C], start=True, stop=False,
                       skip_group_check=True)

                def gather(e, s):
                    pe.wait_ge(hot_done, e + 1)
                    if not isinstance(e, int) or e:
                        pe.wait_ge(xe_done, e)
                    for n in range(TILES):
                        last = mm(px[:, 0:P], xt[:, n, :], hot[s][:, n, :], start=(n == 0), stop=(n == TILES - 1))
                    last.then_inc(gathered, 1)

                def add(e, s, stop=False):
                    pe.wait_ge(y_done, e + 1)
                    pe.wait_ge(back_done, e + 2)
                    for j in range(NC):
                        last = mm(acc[:, j, :], ye[s][:, :], back[s][:, j * C:(j + 1) * C], start=False, stop=stop,
                                  skip_group_check=True)
                    last.then_inc(added, 1)

                def expert(e, s, n, first=False, last=False):
                    pe.wait_ge(w_in[s], n * 64)
                    pe.wait_ge(xe_done, e + 1)
                    if not first:
                        pe.wait_ge(gelu, e)
                    for f in range(FT):
                        up = mm(ph[:, f, :], w1[s][:, f, :], xe[s][:, :], start=True, stop=True)
                    up.then_inc(up_done, 1)
                    if not last:
                        gather(e + 1, 1 - s)
                    pe.wait_ge(gelu, e + 1)
                    if not first:
                        pe.wait_ge(y_done, e)
                    for f in range(FT):
                        down = mm(py[:, 0:D], he[s][:, f, :], w2[s][:, f, :], start=(f == 0), stop=(f == FT - 1))
                    down.then_inc(down_done, 1)
                    if not first:
                        add(e - 1, 1 - s)

                gather(0, 0)
                expert(0, 0, 1, first=True)
                with pe.Fori(0, E // 2 - 1) as l:
                    expert(l * 2 + 1, 1, l + 1)
                    expert(l * 2 + 2, 0, l + 2)
                expert(E - 1, 1, E // 2, last=True)
                add(E - 1, 1, stop=True)

            @block.scalar
            def _(act):
                act.wait_ge(loaded, 32)

                def take(e, s):
                    act.wait_ge(gathered, e + 2)
                    if not isinstance(e, int) or e:
                        act.wait_ge(up_done, e)
                    nc.scalar.activation(xe[s][:, :], px[:, 0:P], ACT.Copy).then_inc(xe_done, 1)

                def expert(e, s, last=False):
                    nc.scalar.activation(b1s[s][:, :], b1[:, bass.ds(e, 1), :].squeeze(1), ACT.Copy).then_inc(staged, 1)
                    act.wait_ge(staged, e + 1)
                    act.wait_ge(up_done, e + 2)
                    if not isinstance(e, int) or e:
                        act.wait_ge(down_done, e)
                    for f in range(FT):
                        g = nc.scalar.activation(he[s][:, f, :], ph[:, f, :], ACT.Gelu, bias=b1s[s][:, f:f + 1])
                    g.then_inc(gelu, 1)
                    if not last:
                        take(e + 1, 1 - s)

                take(0, 0)
                expert(0, 0)
                with act.Fori(0, E // 2 - 1) as l:
                    expert(l * 2 + 1, 1)
                    expert(l * 2 + 2, 0)
                expert(E - 1, 1, last=True)
                act.wait_ge(added, E + 1)
                nc.scalar.activation(res[:, :], acc[:, :, :].rearrange("p a b -> p (a b)"), ACT.Copy)

            @block.vector
            def _(dve):
                v = nc.vector
                dve.wait_ge(counts, 2)
                dve.sem_inc(back_done, 1)

                def one_hot(e, s):
                    if not isinstance(e, int) or e:
                        dve.wait_ge(gathered, e)
                    v.tensor_tensor(hot[s][:, :, :], bc(slots[:, bass.ds(e, 1), :].squeeze(1), 2, P),
                                    bc(count[:, :], 1, TILES), ALU.is_equal).then_inc(hot_done, 1)

                def expert(e, s, n, last=False):
                    if not last:
                        one_hot(e + 1, 1 - s)
                    dve.wait_ge(w_in[s], n * 64)
                    if not isinstance(e, int) or e:
                        dve.wait_ge(added, e)
                    v.scalar_tensor_tensor(back[s][:, :], sr[s][:, :], line[:, 0:1], gr[s][:, :],
                                           ALU.is_equal, ALU.mult).then_inc(back_done, 1)
                    dve.wait_ge(down_done, e + 2)
                    v.tensor_copy(ye[s][:, :], py[:, 0:D]).then_inc(y_done, 1)

                one_hot(0, 0)
                expert(0, 0, 1)
                with dve.Fori(0, E // 2 - 1) as l:
                    expert(l * 2 + 1, 1, l + 1)
                    expert(l * 2 + 2, 0, l + 2)
                expert(E - 1, 1, E // 2, last=True)


def phase_store(k):
    nc = k.nc
    stored = k.sem("stored")
    with nc.Block() as block:

        @block.sync
        def _(sp):
            sp.dma_start(k.out.rearrange("(n p) d -> p n d", p=P), k.x[:, :, :]).then_inc(stored, 16)
            sp.wait_ge(stored, 16)


def layouts(i):
    c = np.ascontiguousarray
    o = {}
    o["x"] = c(i["L0_attn_hidden_states"].reshape(B * T, D))
    for n in (0, 1):
        o[f"cT{n}"] = c(i[f"L{n}_c"].T)
        o[f"wmod{n}"] = c(i[f"L{n}_wmod"])
    heads = lambda w: w.reshape(D, HP, 2 * DK)
    swap = lambda w: c(w.reshape(D, H, 2, HD)[:, :, ::-1, :]).reshape(D, HP, 2 * DK)
    wq, wk = i["L0_attn_Wq"], i["L0_attn_Wk"]
    o["w5"] = c(np.stack([heads(wq), heads(wk), swap(wq), swap(wk), heads(i["L0_attn_Wg"]),
                         heads(i["L0_attn_Wv"])], 2))
    o["wbt"] = c(np.concatenate([i["L0_attn_Wbeta"], i["L0_attn_Wtg"]], 1))
    o["log_decay"] = c(i["L0_attn_log_decay"].reshape(-1))
    o["mode_logits"] = c(i["L0_attn_mode_logits"])
    o["omega"] = c(i["L0_attn_omega_log_scale"].reshape(HP, 2, M).transpose(1, 0, 2))
    pair = np.arange(0, DK, 2, dtype=np.float32)
    inv = (np.float32(1.0) / np.float32(10000.0) ** (pair / np.float32(DK))).astype(np.float32)
    f = np.arange(P)
    o["freq"] = c(np.stack([inv[f % HD], np.where(f % DK < HD, 1.0, -1.0)], 1).astype(np.float32))
    o["wo0"] = c(i["L0_attn_Wo"].reshape(HP, P, D).transpose(1, 0, 2))
    eg, eu, ed = i["L0_ffn_eg_w"], i["L0_ffn_eu_w"], i["L0_ffn_ed_w"]
    up = lambda w: w.reshape(32, P, D).transpose(0, 2, 1)
    down = ed.transpose(0, 2, 1).reshape(32, P, D)
    moe = np.stack([up(eg), up(eu), down], 2)
    shared = np.stack([i["L0_ffn_sg_w"].T, i["L0_ffn_su_w"].T, i["L0_ffn_sd_w"].T], 1)
    o["moe0"] = c(np.concatenate([shared[None], moe], 0))
    o["gate_w"] = c(i["L0_ffn_gate_w"].T)
    o["gate_bias"] = c(i["L0_ffn_gate_bias"])
    o["a1_wqo"] = c(np.stack([i["L1_attn_Wq"], i["L1_attn_Wo"]], 1))
    o["a1_wkv"] = c(np.stack([i["L1_attn_Wk"], i["L1_attn_Wv"]], 1))
    o["a1_bq"] = c(i["L1_attn_bq"].reshape(P, 1))
    o["a1_rows"] = c(np.stack([i["L1_attn_bk"], i["L1_attn_bv"], i["L1_attn_bo"]], 0))
    o["router_w"] = c(i["L1_ffn_router_weight"].T)
    o["router_b"] = c(i["L1_ffn_router_bias"])
    o["norm_w"] = c(i["L1_ffn_norm_weight"].reshape(P, 1))
    o["fc1"] = c(i["L1_ffn_fc1_weight"].reshape(16, 4, P, D).transpose(0, 3, 1, 2))
    o["fc2"] = c(i["L1_ffn_fc2_weight"].reshape(16, D, 4, P).transpose(0, 3, 2, 1))
    o["b1"] = c(i["L1_ffn_fc1_bias"].reshape(16, 4, P).transpose(2, 0, 1))
    o["b2"] = c(i["L1_ffn_fc2_bias"])
    return o


def kernel(**inputs):
    from concourse import bacc
    from concourse.bass_utils import run_bass_kernel_spmd

    nc = bacc.Bacc("TRN2", target_bir_lowering=False, num_devices=1)
    arrays = layouts({n: np.asarray(a) for n, a in inputs.items()})
    ins = {n: nc.dram_tensor(f"in_{n}", a.shape, F32, kind="ExternalInput").ap() for n, a in arrays.items()}
    out = nc.dram_tensor("out", (B * T, D), F32, kind="ExternalOutput").ap()
    program(nc, ins, out)
    r = run_bass_kernel_spmd(nc, [{f"in_{n}": a for n, a in arrays.items()}], core_ids=[0])
    return r.results[0]["out"].reshape(B, T, D)
```
